# Optimizing a Trainium2 kernel written in Bass

```python
import numpy as np
import jax
import jax.numpy as jnp

def _softmax(x, axis=-1):
    return jax.nn.softmax(x, axis=axis)

def _gelu(x):
    return jax.nn.gelu(x, approximate=True)

def _silu(x):
    return jax.nn.silu(x)

def _sigmoid(x):
    return jax.nn.sigmoid(x)

def _layernorm(x, axis=-1, eps=1e-05):
    m = jnp.mean(x, axis=axis, keepdims=True)
    v = jnp.var(x, axis=axis, keepdims=True)
    return (x - m) / jnp.sqrt(v + eps)

def _scatter_add(tgt, idx, src, axis=0):
    return tgt.at[idx].add(src)

def _segment_sum(src, seg, n):
    return jax.ops.segment_sum(src, seg, n)
kernel_name = 'mk_gps_d2_gnn_r8_f01994'

def setup_inputs(seed: int=0):
    np.random.seed(seed)
    _w = jnp.asarray

    def _rec_inputs():
        import jax
        import jax.numpy as jnp
        _gk = jax.random.key(seed)
        x = -8.776e-05 + 1 * jax.random.normal(jax.random.fold_in(_gk, 1), (1250, 512), jnp.float32)
        src = jax.random.randint(jax.random.fold_in(_gk, 2), (20000,), 0, 1250, jnp.int32)
        dst = jax.random.randint(jax.random.fold_in(_gk, 3), (20000,), 0, 1250, jnp.int32)
        _o = jnp.argsort(dst, stable=True)
        src = src[_o]
        dst = dst[_o]
        return (x, src, dst)
    x, src, dst = _rec_inputs()

    def _L0_gnn_setup():
        import jax, jax.numpy as jnp
        import numpy as np
        N_NODES = 1250
        key = jax.random.key(seed)
        k1, k2, k3, k4, k5 = jax.random.split(key, 5)
        x = jax.random.normal(k1, (N_NODES, 512), dtype=jnp.float32)
        edge_index = jax.random.randint(k2, (2, 20000), 0, N_NODES, dtype=jnp.int64)
        W_l = jax.random.normal(k3, (512, 512), dtype=jnp.float32) * 0.04
        b_l = jax.random.normal(k4, (512,), dtype=jnp.float32) * 0.04
        W_r = jax.random.normal(k5, (512, 512), dtype=jnp.float32) * 0.04
        return {'x': x, 'edge_index': edge_index, 'W_l': W_l, 'b_l': b_l, 'W_r': W_r}
    _L0_gnn_all = _L0_gnn_setup()
    _L0_gnn_in = {k: v for k, v in _L0_gnn_all.items() if k in ('W_l', 'b_l', 'W_r')}
    del _L0_gnn_all

    def _L0_mix_setup():
        import jax, jax.numpy as jnp
        import numpy as np
        B, N, C = (8, 1024, 512)
        H = 8
        D = C // H
        EPS = 1e-06

        def _linear_attention(q, k, v):
            qf = jax.nn.elu(q) + 1.0
            kf = jax.nn.elu(k) + 1.0
            kv = jnp.einsum('bhnd,bhne->bhde', kf, v)
            z = jnp.einsum('bhnd,bhd->bhn', qf, kf.sum(axis=2))
            out = jnp.einsum('bhnd,bhde->bhne', qf, kv) / (z[..., None] + EPS)
            return out
        key = jax.random.key(seed)
        k1, k2, k3, k4 = jax.random.split(key, 4)
        x = jax.random.normal(k1, (B, N, C), dtype=jnp.float32)
        w_qkv = jax.random.normal(k2, (C, 3 * C), dtype=jnp.float32) * (1.0 / np.sqrt(C))
        w_proj = jax.random.normal(k3, (C, C), dtype=jnp.float32) * (1.0 / np.sqrt(C))
        b_proj = jax.random.normal(k4, (C,), dtype=jnp.float32) * 0.01
        return {'x': x, 'w_qkv': w_qkv, 'w_proj': w_proj, 'b_proj': b_proj}
    _L0_mix_all = _L0_mix_setup()
    _L0_mix_in = {k: v for k, v in _L0_mix_all.items() if k in ('w_qkv', 'w_proj', 'b_proj')}
    del _L0_mix_all

    def _L0_ffn_setup():
        import jax, jax.numpy as jnp
        import numpy as np
        B, S, D, E, H, TOP_K = (16, 512, 512, 8, 1024, 2)
        key = jax.random.key(seed)
        ks = jax.random.split(key, 6)
        x = jax.random.normal(ks[0], (B, S, D), jnp.float32)
        gate_w = jax.random.normal(ks[1], (D, E), jnp.float32) * 0.02
        gate_b = jnp.zeros((E,), jnp.float32)
        w1 = jax.random.normal(ks[2], (E, D, H), jnp.float32) * 0.02
        b1 = jnp.zeros((E, H), jnp.float32)
        w2 = jax.random.normal(ks[3], (E, H, D), jnp.float32) * 0.02
        b2 = jnp.zeros((E, D), jnp.float32)
        return {'x': x, 'gate_w': gate_w, 'gate_b': gate_b, 'w1': w1, 'b1': b1, 'w2': w2, 'b2': b2}
    _L0_ffn_all = _L0_ffn_setup()
    _L0_ffn_in = {k: v for k, v in _L0_ffn_all.items() if k in ('gate_w', 'gate_b', 'w1', 'b1', 'w2', 'b2')}
    del _L0_ffn_all

    def _L1_gnn_setup():
        import jax, jax.numpy as jnp
        import numpy as np

        def _gcn_conv(x, edge_index, W, b):
            N = x.shape[0]
            loops = jnp.arange(N, dtype=edge_index.dtype)
            src = jnp.concatenate([edge_index[0], loops])
            dst = jnp.concatenate([edge_index[1], loops])
            deg = jax.ops.segment_sum(jnp.ones_like(dst, dtype=x.dtype), dst, num_segments=N)
            dinv = jnp.where(deg > 0, jax.lax.rsqrt(deg), 0.0)
            norm = dinv[src] * dinv[dst]
            xw = x @ W
            msgs = norm[:, None] * xw[src]
            out = jax.ops.segment_sum(msgs, dst, num_segments=N)
            return out + b
        key = jax.random.key(seed)
        ks = jax.random.split(key, 8)
        N, E = (1250, 20000)
        IN, OUT, TC = (512, 512, 256)
        x = jax.random.normal(ks[0], (N, IN), dtype=jnp.float32)
        t_emb = jax.random.normal(ks[1], (TC,), dtype=jnp.float32)
        edge_index = jax.random.randint(ks[2], (2, E), 0, N, dtype=jnp.int64)
        W = jax.random.normal(ks[3], (IN, OUT), dtype=jnp.float32) / np.sqrt(IN)
        b = jnp.zeros((OUT,), dtype=jnp.float32)
        Wt = jax.random.normal(ks[4], (TC, OUT), dtype=jnp.float32) / np.sqrt(TC)
        bt = jnp.zeros((OUT,), dtype=jnp.float32)
        return {'x': x, 't_emb': t_emb, 'edge_index': edge_index, 'W': W, 'b': b, 'Wt': Wt, 'bt': bt}
    _L1_gnn_all = _L1_gnn_setup()
    _L1_gnn_in = {k: v for k, v in _L1_gnn_all.items() if k in ('t_emb', 'W', 'b', 'Wt', 'bt')}
    del _L1_gnn_all

    def _L1_mix_setup():
        import jax, jax.numpy as jnp
        import numpy as np
        key = jax.random.key(seed)
        k1, k2, k3 = jax.random.split(key, 3)
        B, S, E = (4, 512, 512)
        x = jax.random.normal(k1, (B, S, E), dtype=jnp.float32)
        lim_qkv = float(np.sqrt(6.0 / (E + 3 * E)))
        W_qkv = jax.random.uniform(k2, (3 * E, E), minval=-lim_qkv, maxval=lim_qkv, dtype=jnp.float32)
        b_qkv = jnp.zeros((3 * E,), dtype=jnp.float32)
        lim_out = float(np.sqrt(6.0 / (E + E)))
        W_out = jax.random.uniform(k3, (E, E), minval=-lim_out, maxval=lim_out, dtype=jnp.float32)
        b_out = jnp.zeros((E,), dtype=jnp.float32)
        return {'x': x, 'W_qkv': W_qkv, 'b_qkv': b_qkv, 'W_out': W_out, 'b_out': b_out}
    _L1_mix_all = _L1_mix_setup()
    _L1_mix_in = {k: v for k, v in _L1_mix_all.items() if k in ('W_qkv', 'b_qkv', 'W_out', 'b_out')}
    del _L1_mix_all

    def _L1_ffn_setup():
        import jax, jax.numpy as jnp
        import numpy as np
        B, S, D, E, O = (1024, 256, 512, 16, 512)
        key = jax.random.key(seed)
        k_x, k_wg, k_bg, k_we, k_be = jax.random.split(key, 5)
        scale_g = 1.0 / np.sqrt(D)
        scale_e = 1.0 / np.sqrt(D)
        return {'x': jax.random.normal(k_x, (B, S, D), dtype=jnp.float32), 'Wg': jax.random.uniform(k_wg, (D, E), jnp.float32, -scale_g, scale_g), 'bg': jax.random.uniform(k_bg, (E,), jnp.float32, -scale_g, scale_g), 'We': jax.random.uniform(k_we, (E, D, O), jnp.float32, -scale_e, scale_e), 'be': jax.random.uniform(k_be, (E, O), jnp.float32, -scale_e, scale_e)}
    _L1_ffn_all = _L1_ffn_setup()
    _L1_ffn_in = {k: v for k, v in _L1_ffn_all.items() if k in ('Wg', 'bg', 'We', 'be')}
    del _L1_ffn_all
    return {'x': x, 'src': src, 'dst': dst, 'L0_gnn_W_l': _L0_gnn_in['W_l'], 'L0_gnn_b_l': _L0_gnn_in['b_l'], 'L0_gnn_W_r': _L0_gnn_in['W_r'], 'L0_mix_w_qkv': _L0_mix_in['w_qkv'], 'L0_mix_w_proj': _L0_mix_in['w_proj'], 'L0_mix_b_proj': _L0_mix_in['b_proj'], 'L0_ffn_gate_w': _L0_ffn_in['gate_w'], 'L0_ffn_gate_b': _L0_ffn_in['gate_b'], 'L0_ffn_w1': _L0_ffn_in['w1'], 'L0_ffn_b1': _L0_ffn_in['b1'], 'L0_ffn_w2': _L0_ffn_in['w2'], 'L0_ffn_b2': _L0_ffn_in['b2'], 'L1_gnn_t_emb': _L1_gnn_in['t_emb'], 'L1_gnn_W': _L1_gnn_in['W'], 'L1_gnn_b': _L1_gnn_in['b'], 'L1_gnn_Wt': _L1_gnn_in['Wt'], 'L1_gnn_bt': _L1_gnn_in['bt'], 'L1_mix_W_qkv': _L1_mix_in['W_qkv'], 'L1_mix_b_qkv': _L1_mix_in['b_qkv'], 'L1_mix_W_out': _L1_mix_in['W_out'], 'L1_mix_b_out': _L1_mix_in['b_out'], 'L1_ffn_Wg': _L1_ffn_in['Wg'], 'L1_ffn_bg': _L1_ffn_in['bg'], 'L1_ffn_We': _L1_ffn_in['We'], 'L1_ffn_be': _L1_ffn_in['be']}

def reference(x, src, dst, L0_gnn_W_l, L0_gnn_b_l, L0_gnn_W_r, L0_mix_w_qkv, L0_mix_w_proj, L0_mix_b_proj, L0_ffn_gate_w, L0_ffn_gate_b, L0_ffn_w1, L0_ffn_b1, L0_ffn_w2, L0_ffn_b2, L1_gnn_t_emb, L1_gnn_W, L1_gnn_b, L1_gnn_Wt, L1_gnn_bt, L1_mix_W_qkv, L1_mix_b_qkv, L1_mix_W_out, L1_mix_b_out, L1_ffn_Wg, L1_ffn_bg, L1_ffn_We, L1_ffn_be):
    import jax
    import jax.numpy as jnp

    def _L0_gnn_ref(x, edge_index, W_l, b_l, W_r):
        import jax, jax.numpy as jnp
        import numpy as np
        N_NODES = 1250
        src, dst = (edge_index[0], edge_index[1])
        n = x.shape[0]
        summed = jax.ops.segment_sum(x[src], dst, num_segments=n)
        deg = jax.ops.segment_sum(jnp.ones_like(src, dtype=x.dtype), dst, num_segments=n)
        agg = summed / jnp.maximum(deg, 1.0)[:, None]
        out = agg @ W_l.T + b_l + x @ W_r.T
        out = jax.nn.relu(out)
        return out

    def _L0_mix_ref(x, w_qkv, w_proj, b_proj):
        import jax, jax.numpy as jnp
        import numpy as np
        B, N, C = (8, 1024, 512)
        H = 8
        D = C // H
        EPS = 1e-06

        def _linear_attention(q, k, v):
            qf = jax.nn.elu(q) + 1.0
            kf = jax.nn.elu(k) + 1.0
            kv = jnp.einsum('bhnd,bhne->bhde', kf, v)
            z = jnp.einsum('bhnd,bhd->bhn', qf, kf.sum(axis=2))
            out = jnp.einsum('bhnd,bhde->bhne', qf, kv) / (z[..., None] + EPS)
            return out
        b, n, c = x.shape
        qkv = x @ w_qkv
        qkv = qkv.reshape(b, n, 3, H, D).transpose(2, 0, 3, 1, 4)
        q, k, v = (qkv[0], qkv[1], qkv[2])
        attn = _linear_attention(q, k, v)
        y = attn.transpose(0, 2, 1, 3).reshape(b, n, c)
        return y @ w_proj + b_proj

    def _L0_ffn_ref(x, gate_w, gate_b, w1, b1, w2, b2):
        import jax, jax.numpy as jnp
        import numpy as np
        B, S, D, E, H, TOP_K = (16, 512, 512, 8, 1024, 2)
        orig_shape = x.shape
        xf = x.reshape(-1, orig_shape[-1])
        T = xf.shape[0]
        n_experts = gate_w.shape[-1]
        scores = jax.nn.softmax(xf @ gate_w + gate_b, axis=-1)
        top_w, top_i = jax.lax.top_k(scores, TOP_K)
        top_w = top_w / top_w.sum(axis=-1, keepdims=True)
        combine = jnp.zeros((T, n_experts), xf.dtype).at[jnp.arange(T)[:, None], top_i].add(top_w)
        out = jnp.zeros_like(xf)
        for e in range(n_experts):
            h = jax.nn.gelu(xf @ w1[e] + b1[e], approximate=False)
            out = out + combine[:, e:e + 1] * (h @ w2[e] + b2[e])
        return out.reshape(orig_shape)

    def _L1_gnn_ref(x, t_emb, edge_index, W, b, Wt, bt):
        import jax, jax.numpy as jnp
        import numpy as np

        def _gcn_conv(x, edge_index, W, b):
            N = x.shape[0]
            loops = jnp.arange(N, dtype=edge_index.dtype)
            src = jnp.concatenate([edge_index[0], loops])
            dst = jnp.concatenate([edge_index[1], loops])
            deg = jax.ops.segment_sum(jnp.ones_like(dst, dtype=x.dtype), dst, num_segments=N)
            dinv = jnp.where(deg > 0, jax.lax.rsqrt(deg), 0.0)
            norm = dinv[src] * dinv[dst]
            xw = x @ W
            msgs = norm[:, None] * xw[src]
            out = jax.ops.segment_sum(msgs, dst, num_segments=N)
            return out + b
        h = _gcn_conv(x, edge_index, W, b)
        time_emb = t_emb @ Wt + bt
        return h + time_emb

    def _L1_mix_ref(x, W_qkv, b_qkv, W_out, b_out):
        import jax, jax.numpy as jnp
        import numpy as np
        B, S, E = x.shape
        H = 8
        D = E // H
        qkv = x @ W_qkv.T + b_qkv
        qkv = qkv.reshape(B, S, H, 3 * D)
        q, k, v = jnp.split(qkv, 3, axis=-1)
        q = jax.nn.sigmoid(q)
        k = jax.nn.sigmoid(k)
        i = jnp.sum(q * jnp.sum(k, axis=1, keepdims=True), axis=3, keepdims=True)
        o = jnp.sum(k * jnp.sum(q, axis=1, keepdims=True), axis=3, keepdims=True)
        i_hat = jnp.sum(q * jnp.sum(k / o, axis=1, keepdims=True), axis=3, keepdims=True)
        o_hat = jnp.sum(k * jnp.sum(q / i, axis=1, keepdims=True), axis=3, keepdims=True)
        vw = v * jax.nn.softmax(o_hat, axis=1)
        kv = jnp.einsum('bshd,bshe->bsde', k, vw)
        r = jnp.einsum('bshd,bsde->bshe', q / i, kv) * jax.nn.sigmoid(i_hat)
        values = r.reshape(B, S, E)
        return values @ W_out.T + b_out

    def _L1_ffn_ref(x, Wg, bg, We, be):
        import jax, jax.numpy as jnp
        import numpy as np
        B, S, D, E, O = (1024, 256, 512, 16, 512)
        scores = jax.nn.softmax(jnp.mean(x, axis=1) @ Wg + bg, axis=-1)
        idx = jnp.argmax(scores, axis=-1)
        gate = jnp.take_along_axis(scores, idx[:, None], axis=-1)
        W_sel = We[idx]
        b_sel = be[idx]
        y = jnp.einsum('bsd,bdo->bso', x, W_sel) + b_sel[:, None, :]
        return gate[:, :, None] * y
    edge_index = jnp.stack([src, dst])
    xn = _layernorm(x, axis=-1)
    x = x + _L0_gnn_ref(xn, edge_index, L0_gnn_W_l, L0_gnn_b_l, L0_gnn_W_r) + _L0_mix_ref(xn[None], L0_mix_w_qkv, L0_mix_w_proj, L0_mix_b_proj)[0]
    x = x + _L0_ffn_ref(_layernorm(x, axis=-1)[None], L0_ffn_gate_w, L0_ffn_gate_b, L0_ffn_w1, L0_ffn_b1, L0_ffn_w2, L0_ffn_b2)[0]
    xn = _layernorm(x, axis=-1)
    x = x + _L1_gnn_ref(xn, L1_gnn_t_emb, edge_index, L1_gnn_W, L1_gnn_b, L1_gnn_Wt, L1_gnn_bt) + _L1_mix_ref(xn[None], L1_mix_W_qkv, L1_mix_b_qkv, L1_mix_W_out, L1_mix_b_out)[0]
    x = x + _L1_ffn_ref(_layernorm(x, axis=-1)[None], L1_ffn_Wg, L1_ffn_bg, L1_ffn_We, L1_ffn_be)[0]
    return x

_drawn_inputs = setup_inputs


def setup_inputs(seed=0):
    import zlib

    import numpy as np

    out = dict(_drawn_inputs(seed))
    spreads = {'L0_ffn_gate_b': (0.0, 0.1),
     'L0_ffn_b1': (0.0, 0.459),
     'L0_ffn_b2': (0.0, 0.1),
     'L1_gnn_b': (0.0, 0.1),
     'L1_gnn_bt': (0.0, 0.1),
     'L1_mix_b_qkv': (0.0, 2.0),
     'L1_mix_b_out': (0.0, 0.1)}
    factors = {'L0_mix_b_proj': 6.069,
     'L1_mix_W_qkv': 200.0,
     'L1_mix_W_out': 200.0,
     'L1_ffn_be': 34.892,
     'L1_ffn_bg': 8.0}
    for name, (base, spread) in spreads.items():
        noise = np.random.default_rng([zlib.crc32(name.encode()), seed]).standard_normal(out[name].shape)
        drawn = base * np.exp(spread * noise) if base else spread * noise
        out[name] = jnp.asarray(drawn.astype(out[name].dtype))
    for name, factor in factors.items():
        out[name] = (out[name] * factor).astype(out[name].dtype)
    return out
```

```python
from contextlib import ExitStack

import numpy as np

import concourse.bass as bass
from concourse import mybir

ALU = mybir.AluOpType
ACT = mybir.ActivationFunctionType
AX = mybir.AxisListType
F32 = mybir.dt.float32
F16 = mybir.dt.float16
BF16 = mybir.dt.bfloat16
I32 = mybir.dt.int32
U32 = mybir.dt.uint32

N, D, EDGES = 1250, 512, 20000
P = 128
TP = 125
NT = N // TP
KB = D // P
CHUNKS = [(0, 500), (500, 500), (1000, 250)]
QT = 4
STEPS = EDGES // (QT * TP)
H, HD = 8, 64
E0, F0, SLOT = 8, 1024, 128
FB = F0 // P
SLOTS = (2 * N - E0) // SLOT + E0 + 1
SLOTS_SURE = 2 * N // SLOT + 1
E1 = 16
EPS_LN, EPS_ATT = 1e-5, 1e-6
GROUP = 10
GW = GROUP * H
GROUPS = N // GROUP
BATCH = 5
BIG = 1000.0
HALF = NT // 2


class Count:

    def __init__(self, sem):
        self.sem, self.n = sem, 0

    def add(self, ins):
        self.n += 1
        ins.then_inc(self.sem, 1)
        return self.n


class Chain:

    def __init__(self, eng, count):
        self.eng, self.count = eng, count

    def __call__(self, ins):
        self.eng.wait_ge(self.count.sem, self.count.add(ins))


def blocks(w):
    return w.rearrange("(b p) n -> p b n", p=P)


def build(nc, t):
    with ExitStack() as top:
        def sb(name, shape, dt=F32, scope=top):
            return scope.enter_context(nc.sbuf_tensor(name, shape, dt))

        def sem(name):
            return top.enter_context(nc.semaphore(name))

        bank = top.enter_context(nc.psum_tensor("bank", [P, 8, 512], F32))
        x_res = sb("x_res", [TP, NT, D])
        xn = sb("xn", [P, NT * D])
        xn_r = xn[0:TP, :].rearrange("p (t d) -> p t d", t=NT)
        xn_c = sb("xn_c", [P, KB, N])
        adj = sb("adj", [P, NT * N])
        adj_t = adj[0:TP, 0:NT * N].rearrange("p (s n) -> p s n", s=NT)
        ident = sb("ident", [P, P])
        before = sb("before", [P, P])
        ones = sb("ones", [P, P])
        headmask = sb("headmask", [P, P])
        tokmask = sb("tokmask", [P, P])
        iota = sb("iota", [P, N], F16)
        smallc = sb("smallc", [P, 256])
        deg = sb("deg", [TP, NT])
        stats = sb("stats", [TP, NT, 6])
        moments = sb("moments", [TP, NT, 2])
        rstd, rs_var, rs_root, rs_tmp = (sb(n, [TP, NT]) for n in ("rstd", "rs_var", "rs_root", "rs_tmp"))

        s_x = [sem("x_loaded_0"), sem("x_loaded_1")]
        s_const, s_edges, s_zero, s_zfill = (sem(n) for n in ("const_loaded", "edges_loaded", "zero_set", "zero_filled"))
        s_w0, s_gate_w = sem("layer0_weights_loaded"), sem("gate_weights_loaded")
        s_normed, s_turned, s_evac = (sem(n) for n in ("normed", "turned", "columns_ready"))
        s_bn, s_var, s_sqrt = sem("stats_ready"), sem("variance_ready"), sem("root_ready")
        dve_n, act_n, pool_n = Count(sem("dve_step")), Count(sem("act_step")), Count(sem("pool_step"))
        pe_n = Count(sem("pe_step"))

        slots_x = nc.dram_tensor("slots_x", (SLOTS * SLOT, D), F32, kind="Internal").ap()
        slots_y = nc.dram_tensor("slots_y", (SLOTS * SLOT, D), F32, kind="Internal").ap()

        def refine_rsqrt(chain, out, v, root, tmp):
            chain(nc.vector.reciprocal(out, root))
            chain(nc.vector.tensor_tensor(tmp, out, out, ALU.mult))
            chain(nc.vector.tensor_tensor(tmp, tmp, v, ALU.mult))
            chain(nc.vector.tensor_scalar(tmp, tmp, -0.5, 1.5, ALU.mult, ALU.add))
            chain(nc.vector.tensor_tensor(out, out, tmp, ALU.mult))

        def layernorm(block, which):
            base = which * NT

            @block.vector
            def _(dve):
                chain = Chain(dve, dve_n)
                for i in range(NT):
                    if which == 0:
                        dve.wait_ge(s_x[i // HALF], 16)
                    nc.vector.bn_stats(stats[:, i], x_res[:, i]).then_inc(s_bn, 1)
                    dve.wait_ge(s_bn, base + i + 1)
                    ins = nc.vector.bn_aggr(moments[:, i], stats[:, i])
                    if i % HALF == HALF - 1:
                        chain(ins)
                        tiles = slice(i + 1 - HALF, i + 1)
                        nc.vector.tensor_scalar(rs_var[:, tiles], moments[:, tiles, 1], EPS_LN, None, ALU.add).then_inc(s_var, 1)
                for c in range(2):
                    tiles = slice(c * HALF, (c + 1) * HALF)
                    dve.wait_ge(s_sqrt, 2 * which + c + 1)
                    refine_rsqrt(chain, rstd[:, tiles], rs_var[:, tiles], rs_root[:, tiles], rs_tmp[:, tiles])
                    for i in range(c * HALF, (c + 1) * HALF):
                        nc.vector.tensor_scalar(xn_r[:, i], x_res[:, i], moments[:, i, 0:1], rstd[:, i:i + 1],
                                                ALU.subtract, ALU.mult).then_inc(s_normed, 1)

            @block.tensor
            def _(pe):
                if which == 0:
                    pe.wait_ge(s_const, 16 * N_CONST)
                for i in range(NT):
                    pe.wait_ge(s_normed, base + i + 1)
                    if i >= 2:
                        pe.wait_ge(s_evac, base + i - 1)
                    for b in range(KB):
                        ins = nc.tensor.transpose(bank[:, i % 2, b * P:b * P + TP], xn_r[:, i, b * P:(b + 1) * P],
                                                  ident[0:TP, 0:TP])
                    ins.then_inc(s_turned, 1)

            @block.scalar
            def _(act):
                for c in range(2):
                    tiles = slice(c * HALF, (c + 1) * HALF)
                    act.wait_ge(s_var, 2 * which + c + 1)
                    nc.scalar.activation(rs_root[:, tiles], rs_var[:, tiles], ACT.Sqrt).then_inc(s_sqrt, 1)
                for i in range(NT):
                    act.wait_ge(s_turned, base + i + 1)
                    nc.scalar.copy(xn_c[:, :, i * TP:(i + 1) * TP],
                                   bank[:, i % 2, :].rearrange("p (b n) -> p b n", b=KB)[:, :, 0:TP]).then_inc(s_evac, 1)

        N_CONST = 7
        layer0 = top.enter_context(ExitStack())
        wqkv0 = sb("wqkv0", [P, KB * 3 * D], scope=layer0)
        wqkv = wqkv0[:].rearrange("p (b n) -> p b n", b=KB)
        w_l, w_r, w_proj = (sb(n, [P, KB, D], scope=layer0) for n in ("w_l", "w_r", "w_proj"))
        b_l, b_proj = (sb(n, [TP, D], scope=layer0) for n in ("b_l", "b_proj"))

        with ExitStack() as scope:
            zeros = sb("zeros", [P, 4 * D], scope=scope)
            zeros16 = sb("zeros16", [P, 512], BF16, scope=scope)
            ones16 = sb("ones16", [P, 2], BF16, scope=scope)
            edge_i = sb("edge_i", [STEPS, 2, QT * TP], I32, scope=scope)
            edge_f = sb("edge_f", [STEPS, 2, QT * TP], scope=scope)
            edge_c = sb("edge_c", [TP, 2, QT, 2 * STEPS], scope=scope)
            span = sb("span", [STEPS, 2], scope=scope)
            span_w = sb("span_w", [STEPS, 2, NT], scope=scope)
            fl1, fl2, key = (sb(n, [NT, STEPS], scope=scope) for n in ("fl1", "fl2", "key"))
            plan = sb("plan", [NT, 4], scope=scope)
            plan_i = sb("plan_i", [NT, 4], I32, scope=scope)
            onehot_src = sb("onehot_src", [TP, QT, N], BF16, scope=scope)
            onehot_dst = sb("onehot_dst", [TP, QT, TP], BF16, scope=scope)
            s_hot = [sem(f"onehot_ready_{j}") for j in range(QT)]
            s_used = [sem(f"onehot_used_{j}") for j in range(QT)]
            s_adj = sem("window_copied")
            s_plan, s_edge_f = sem("plan_ready"), sem("edges_as_floats")
            s_span = sem("span_ready")
            s_spanp = sem("span_turned")

            with nc.Block() as block:
                layernorm(block, 0)

                @block.sync
                def _(sp):
                    for c in range(2):
                        sp.dma_start(x_res[:, c * HALF:(c + 1) * HALF],
                                     t["x"].rearrange("(t p) d -> p t d", p=TP)[:, c * HALF:(c + 1) * HALF]).then_inc(s_x[c], 16)
                    for n, (dst, src) in enumerate([(ident, t["c_ident"]), (before, t["c_before"]), (ones, t["c_ones"]),
                                                    (headmask, t["c_headmask"]), (tokmask, t["c_tokmask"]),
                                                    (iota, t["c_iota"]), (smallc, t["c_small"])]):
                        sp.dma_start(dst[:], src).then_inc(s_const, 16)
                    for n, name in enumerate(("src", "dst")):
                        sp.dma_start(edge_i[:, n], t[name].rearrange("(u e) -> u e", e=QT * TP)).then_inc(s_edges, 16)
                    sp.dma_start(wqkv, blocks(t["L0_mix_w_qkv"])).then_inc(s_w0, 16)
                    for dst, name in ((w_l, "L0_gnn_W_l"), (w_r, "L0_gnn_W_r"), (w_proj, "L0_mix_w_proj")):
                        sp.dma_start(dst[:], blocks(t[name])).then_inc(s_w0, 16)
                    for dst, name in ((b_l, "L0_gnn_b_l"), (b_proj, "L0_mix_b_proj")):
                        sp.dma_start(dst[:], t[name].partition_broadcast(TP)).then_inc(s_w0, 16)
                    sp.wait_ge(s_zero, 1)
                    fill = slots_x[0:SLOTS * SLOT].rearrange("(p a) d -> p (a d)", p=P)
                    width = 4 * D
                    for c in range(SLOTS // 4):
                        sp.dma_start(fill[:, c * width:(c + 1) * width], zeros[:]).then_inc(s_zfill, 16)
                    spare = slots_y[SLOTS_SURE * SLOT:].rearrange("(p a) d -> p (a d)", p=P)
                    for c in range((SLOTS - SLOTS_SURE) // 4):
                        sp.dma_start(spare[:, c * width:(c + 1) * width], zeros[:]).then_inc(s_zfill, 16)

                @block.gpsimd
                def _(pool):
                    nc.gpsimd.memset(zeros[:], 0.0).then_inc(s_zero, 1)

            with nc.Block() as block:
                @block.sync
                def _(sp):
                    sp.wait_ge(s_zfill, 16 * ((2 * SLOTS - SLOTS_SURE) // 4))

                @block.vector
                def _(dve):
                    chain = Chain(dve, dve_n)
                    nc.vector.memset(zeros16[:], 0.0)
                    chain(nc.vector.memset(ones16[:], 1.0))
                    dve.wait_ge(s_edges, 32)
                    nc.vector.tensor_copy(edge_f[:], edge_i[:]).then_inc(s_edge_f, 1)
                    dve.wait_ge(s_edge_f, 1)
                    chain(nc.vector.tensor_reduce(span[:, 0:1], edge_f[:, 1], AX.X, ALU.min))
                    chain(nc.vector.tensor_reduce(span[:, 1:2], edge_f[:, 1], AX.X, ALU.max))
                    for m in range(2):
                        nc.vector.tensor_scalar(span_w[:, m], ones[0:STEPS, 0:NT], span[:, m:m + 1], None,
                                                ALU.mult).then_inc(s_span, 1)
                    dve.wait_ge(s_spanp, 1)
                    spans = bank[0:NT, 1, :]
                    w_first, w_last = smallc[0:NT, 0:1], smallc[0:NT, 1:2]
                    step_no = smallc[0:NT, 8:8 + STEPS]
                    chain(nc.vector.tensor_scalar(fl1[:], spans[:, P:P + STEPS], w_first, None, ALU.is_ge))
                    chain(nc.vector.scalar_tensor_tensor(fl2[:], spans[:, 0:STEPS], w_last, fl1[:], ALU.is_le, ALU.mult))
                    chain(nc.vector.scalar_tensor_tensor(key[:], step_no, -BIG, fl2[:], ALU.add, ALU.mult))
                    chain(nc.vector.tensor_reduce(plan[:, 0:1], key[:], AX.X, ALU.min))
                    chain(nc.vector.scalar_tensor_tensor(key[:], step_no, 1.0, fl2[:], ALU.add, ALU.mult))
                    chain(nc.vector.tensor_reduce(plan[:, 1:2], key[:], AX.X, ALU.max))
                    chain(nc.vector.tensor_scalar(plan[:, 0:1], plan[:, 0:1], BIG, STEPS - 1.0, ALU.add, ALU.min))
                    chain(nc.vector.tensor_tensor(plan[:, 2:3], plan[:, 1:2], plan[:, 0:1], ALU.subtract))
                    nc.vector.tensor_scalar(plan[:, 2:3], plan[:, 2:3], 1.0, None, ALU.max).then_inc(s_span, 1)
                    dve.wait_ge(s_spanp, 2)
                    chain(nc.vector.tensor_copy(plan[:, 3:4], bank[0:NT, 2, 0:1]))
                    for m in range(2):
                        chain(nc.vector.tensor_copy(edge_c[:, m, :, 0:STEPS], bank[0:TP, 0, :].rearrange(
                            "p (m j u) -> p m j u", m=2, j=QT)[:, m, :, 0:STEPS]))
                    nc.vector.tensor_copy(plan_i[:], plan[:]).then_inc(s_plan, 1)
                    dve.wait_ge(s_plan, 1)
                    for w in range(NT):
                        first = dve.value_load(plan_i[w:w + 1, 0:1], min_val=0, max_val=STEPS - 1)
                        count = dve.value_load(plan_i[w:w + 1, 2:3], min_val=1, max_val=STEPS)
                        base = dve.value_load(plan_i[w:w + 1, 3:4], min_val=0, max_val=NT * STEPS)
                        with dve.Fori(0, count) as i:
                            for j in range(QT):
                                dve.wait_ge(s_used[j], base + i + 1)
                                nc.vector.tensor_scalar(onehot_dst[:, j], iota[0:TP, w * TP:(w + 1) * TP],
                                                        edge_c[:, 1, j, bass.ds(first + i, 1)], None,
                                                        ALU.is_equal).then_inc(s_hot[j], 1)
                                nc.vector.tensor_scalar(onehot_src[:, j], iota[0:TP, :],
                                                        edge_c[:, 0, j, bass.ds(first + i, 1)], None,
                                                        ALU.is_equal).then_inc(s_hot[j], 1)

                @block.tensor
                def _(pe):
                    for j in range(QT):
                        pe.sem_inc(s_used[j], 1)
                    pe.wait_ge(s_edge_f, 1)
                    for m in range(2):
                        for j in range(QT):
                            nc.tensor.transpose(bank[0:TP, 0, (QT * m + j) * 64:(QT * m + j) * 64 + STEPS],
                                                edge_f[:, m, j * TP:(j + 1) * TP], ident[0:STEPS, 0:STEPS])
                    pe.wait_ge(s_span, 2)
                    for m in range(2):
                        ins = nc.tensor.matmul(bank[0:NT, 1, m * P:m * P + STEPS], span_w[:, m],
                                               ident[0:STEPS, 0:STEPS], start=True, stop=True)
                    ins.then_inc(s_spanp, 1)
                    pe.wait_ge(s_span, 3)
                    nc.tensor.matmul(bank[0:NT, 2, 0:1], before[0:NT, 0:NT], plan[:, 2:3],
                                     start=True, stop=True).then_inc(s_spanp, 1)
                    pe.wait_ge(s_plan, 1)
                    for w in range(NT):
                        count = pe.value_load(plan_i[w:w + 1, 2:3], min_val=1, max_val=STEPS)
                        base = pe.value_load(plan_i[w:w + 1, 3:4], min_val=0, max_val=NT * STEPS)
                        bk = 3 * (w % 2)
                        if w >= 2:
                            pe.wait_ge(s_adj, w - 1)
                        for b in range(3):
                            nc.tensor.matmul(bank[0:TP, bk + b, :], zeros16[0:TP, 0:TP], zeros16[0:TP, :],
                                             start=True, stop=False, skip_group_check=True)
                        with pe.Fori(0, count) as i:
                            for j in range(QT):
                                pe.wait_ge(s_hot[j], 2 * (base + i) + 2)
                                nc.tensor.matmul(bank[0:TP, bk + 2, 2 * P - 1:2 * P], onehot_dst[:, j], ones16[0:TP, 0:1],
                                                 start=False, stop=False, skip_group_check=True)
                                for s in range(NT):
                                    ins = nc.tensor.matmul(
                                        bank[0:TP, bk + s // 4, (s % 4) * P:(s % 4) * P + TP],
                                        onehot_src[:, j, s * TP:(s + 1) * TP], onehot_dst[:, j],
                                        start=False, stop=False, skip_group_check=True)
                                ins.then_inc(s_used[j], 1)

                @block.scalar
                def _(act):
                    act.wait_ge(s_plan, 1)
                    for w in range(NT):
                        count = act.value_load(plan_i[w:w + 1, 2:3], min_val=1, max_val=STEPS)
                        base = act.value_load(plan_i[w:w + 1, 3:4], min_val=0, max_val=NT * STEPS)
                        bk = 3 * (w % 2)
                        act.wait_ge(s_used[QT - 1], base + count + 1)
                        win = bank[0:TP, bk:bk + 3, :].rearrange("p b (r n) -> p (b r) n", n=P)
                        nc.scalar.copy(adj_t[:, :, w * TP:(w + 1) * TP], win[:, 0:NT, 0:TP])
                        nc.scalar.copy(deg[:, w:w + 1], win[:, NT - 1, P - 1:P]).then_inc(s_adj, 1)

        with ExitStack() as scope:
            agg = wqkv0[:, 0:KB * N].rearrange("p (b n) -> p b n", b=KB)
            q_c = sb("q_c", [P, KB, N], scope=scope)
            qtmp = sb("qtmp", [P, 2, 512], scope=scope)
            kv_r = sb("kv_r", [TP, 2, 2 * D], scope=scope)
            ksum = sb("ksum", [P, KB], scope=scope)
            ksum_h = sb("ksum_h", [P, KB, P], scope=scope)
            kv_h = sb("kv_h", [P, KB, P], scope=scope)
            kvw = w_proj
            rdeg = sb("rdeg", [TP, NT], scope=scope)
            s_q, s_kv, s_min, s_exp, s_qf = (sem(n) for n in ("q_ready", "kv_ready", "min_ready", "exp_ready", "q_feature"))
            s_kf, s_vc, s_acc, s_agg, s_aggc, s_z, s_qz = (sem(n) for n in (
                "k_feature", "v_copied", "kv_summed", "agg_ready", "agg_copied", "z_ready", "q_scaled"))
            s_kvh, s_kvw, s_kvwc, s_out, s_outc = (sem(n) for n in ("kv_masked", "kvw_ready", "kvw_copied", "out_ready", "out_used"))
            s_bp = sem("bias_added")
            NQ = KB * len(CHUNKS)

            with nc.Block() as block:
                @block.gpsimd
                def _(pool):
                    pool.wait_ge(s_w0, 96)
                    for i in range(NT):
                        nc.gpsimd.tensor_tensor(x_res[:, i], x_res[:, i], b_proj[:], ALU.add).then_inc(s_bp, 1)

                @block.tensor
                def _(pe):
                    pe.wait_ge(s_w0, 96)
                    n = 0
                    for m in range(KB):
                        for a, w in CHUNKS:
                            if n >= 2:
                                pe.wait_ge(s_qf, n - 1)
                            for b in range(KB):
                                ins = nc.tensor.matmul(bank[:, n % 2, 0:w], wqkv[:, b, m * P:(m + 1) * P], xn_c[:, b, a:a + w],
                                                       start=b == 0, stop=b == KB - 1)
                            ins.then_inc(s_q, 1)
                            n += 1

                    def kv_sums(i):
                        pe.wait_ge(s_kf, i + 1)
                        pe.wait_ge(s_vc, i + 1)
                        k, v = kv_r[:, i % 2, 0:D], kv_r[:, i % 2, D:2 * D]
                        for m in range(KB):
                            nc.tensor.matmul(bank[:, 6, m * P:(m + 1) * P], v[:, m * P:(m + 1) * P], k[:, m * P:(m + 1) * P],
                                             start=i == 0 and m == 0, stop=i == NT - 1, skip_group_check=True)
                        for m in range(KB):
                            ins = nc.tensor.matmul(bank[:, 7, m:m + 1], k[:, m * P:(m + 1) * P], ones[0:TP, 0:1],
                                                   start=i == 0 and m == 0, stop=i == NT - 1, skip_group_check=True)
                        ins.then_inc(s_acc, 1)

                    for i in range(NT):
                        if i >= 2:
                            pe.wait_ge(s_kf, i - 1)
                            pe.wait_ge(s_vc, i - 1)
                        for g in range(2):
                            for b in range(KB):
                                ins = nc.tensor.matmul(bank[0:TP, 2 + 2 * (i % 2) + g, :], xn_c[:, b, i * TP:(i + 1) * TP],
                                                       wqkv[:, b, (1 + g) * D:(2 + g) * D], start=b == 0, stop=b == KB - 1)
                            ins.then_inc(s_kv, 1)
                        if i >= 1:
                            kv_sums(i - 1)
                    kv_sums(NT - 1)
                    n = 0
                    for m in range(KB):
                        for a, w in CHUNKS:
                            if n < 2:
                                pe.wait_ge(s_qf, NQ)
                            else:
                                pe.wait_ge(s_aggc, n - 1)
                            for s in range(NT):
                                ins = nc.tensor.matmul(bank[:, n % 2, 0:w], xn_r[:, s, m * P:(m + 1) * P], adj_t[:, s, a:a + w],
                                                       start=s == 0, stop=s == NT - 1)
                            ins.then_inc(s_agg, 1)
                            n += 1
                    pe.wait_ge(s_kvh, 2)
                    n = 0
                    for m in range(KB):
                        for a, w in CHUNKS:
                            if n >= 2:
                                pe.wait_ge(s_qz, n - 1)
                            nc.tensor.matmul(bank[:, 2 + n % 2, 0:w], ksum_h[:, m], q_c[:, m, a:a + w],
                                             start=True, stop=True).then_inc(s_z, 1)
                            n += 1
                    for m in range(KB):
                        if m >= 2:
                            pe.wait_ge(s_kvwc, m - 1)
                        nc.tensor.matmul(bank[:, 4 + m % 2, :], kv_h[:, m], w_proj[:, m], start=True, stop=True).then_inc(s_kvw, 1)
                    pe.wait_ge(s_kvwc, KB)
                    pe.wait_ge(s_qz, NQ)
                    pe.wait_ge(s_aggc, NQ)
                    for i in range(NT):
                        o = 3 * (i % 2)
                        if i >= 2:
                            pe.wait_ge(s_outc, i - 1)
                        tok = slice(i * TP, (i + 1) * TP)
                        for g, (left, right) in enumerate(((agg, w_l), (xn_c, w_r), (q_c, kvw))):
                            for b in range(KB):
                                ins = nc.tensor.matmul(bank[0:TP, o + g, :], left[:, b, tok], right[:, b],
                                                       start=b == 0, stop=b == KB - 1)
                        ins.then_inc(s_out, 1)

                @block.vector
                def _(dve):
                    chain = Chain(dve, dve_n)
                    chain(nc.vector.tensor_scalar(rdeg[:], deg[:], 1.0, None, ALU.max))
                    nc.vector.reciprocal(rdeg[:], rdeg[:]).then_inc(dve_n.sem, 1)
                    dve_n.n += 1
                    n = 0
                    for m in range(KB):
                        for a, w in CHUNKS:
                            dve.wait_ge(s_q, n + 1)
                            nc.vector.tensor_scalar(qtmp[:, n % 2, 0:w], bank[:, n % 2, 0:w], 0.0, None, ALU.min).then_inc(s_min, 1)
                            dve.wait_ge(s_exp, n + 1)
                            nc.vector.scalar_tensor_tensor(q_c[:, m, a:a + w], bank[:, n % 2, 0:w], 0.0, qtmp[:, n % 2, 0:w],
                                                           ALU.max, ALU.add).then_inc(s_qf, 1)
                            n += 1
                    dve.wait_ge(s_qf, n)
                    for i in range(NT):
                        dve.wait_ge(s_kv, 2 * i + 1)
                        if i >= 2:
                            dve.wait_ge(s_acc, i - 1)
                        k = kv_r[:, i % 2, 0:D]
                        kp = bank[0:TP, 2 + 2 * (i % 2), :]
                        nc.vector.tensor_scalar(qtmp[0:TP, i % 2, :], kp, 0.0, None, ALU.min).then_inc(s_min, 1)
                        dve.wait_ge(s_exp, NQ + i + 1)
                        nc.vector.scalar_tensor_tensor(k, kp, 0.0, qtmp[0:TP, i % 2, :], ALU.max, ALU.add).then_inc(s_kf, 1)
                    dve.wait_ge(s_acc, NT)
                    chain(nc.vector.tensor_copy(ksum[:], bank[:, 7, 0:KB]))
                    for m in range(KB):
                        nc.vector.tensor_tensor(kv_h[:, m], bank[:, 6, m * P:(m + 1) * P], headmask[:], ALU.mult)
                        ins = nc.vector.tensor_scalar(ksum_h[:, m], headmask[:], ksum[:, m:m + 1], None, ALU.mult)
                    ins.then_inc(s_kvh, 2)
                    n = 0
                    for m in range(KB):
                        for a, w in CHUNKS:
                            dve.wait_ge(s_z, n + 1)
                            chain(nc.vector.tensor_scalar(qtmp[:, n % 2, 0:w], bank[:, 2 + n % 2, 0:w], EPS_ATT, None, ALU.add))
                            chain(nc.vector.reciprocal(qtmp[:, n % 2, 0:w], qtmp[:, n % 2, 0:w]))
                            nc.vector.tensor_tensor(q_c[:, m, a:a + w], q_c[:, m, a:a + w], qtmp[:, n % 2, 0:w],
                                                    ALU.mult).then_inc(s_qz, 1)
                            n += 1
                    for i in range(NT):
                        o = 3 * (i % 2)
                        dve.wait_ge(s_out, i + 1)
                        dve.wait_ge(s_bp, i + 1)
                        y = qtmp[0:TP, i % 2]
                        chain(nc.vector.tensor_tensor(y, bank[0:TP, o + 1, :], b_l[:], ALU.add))
                        chain(nc.vector.scalar_tensor_tensor(y, bank[0:TP, o, :], rdeg[:, i:i + 1], y, ALU.mult, ALU.add))
                        chain(nc.vector.scalar_tensor_tensor(x_res[:, i], y, 0.0, x_res[:, i], ALU.max, ALU.add))
                        nc.vector.tensor_tensor(x_res[:, i], x_res[:, i], bank[0:TP, o + 2, :], ALU.add).then_inc(s_outc, 1)
                    dve.wait_ge(s_outc, NT)

                @block.scalar
                def _(act):
                    n = 0
                    for m in range(KB):
                        for a, w in CHUNKS:
                            act.wait_ge(s_min, n + 1)
                            nc.scalar.activation(qtmp[:, n % 2, 0:w], qtmp[:, n % 2, 0:w], ACT.Exp).then_inc(s_exp, 1)
                            n += 1
                    for i in range(NT):
                        act.wait_ge(s_min, NQ + i + 1)
                        nc.scalar.activation(qtmp[0:TP, i % 2, :], qtmp[0:TP, i % 2, :], ACT.Exp).then_inc(s_exp, 1)
                        act.wait_ge(s_kv, 2 * i + 2)
                        if i >= 2:
                            act.wait_ge(s_acc, i - 1)
                        nc.scalar.copy(kv_r[:, i % 2, D:2 * D], bank[0:TP, 3 + 2 * (i % 2), :]).then_inc(s_vc, 1)
                    n = 0
                    for m in range(KB):
                        for a, w in CHUNKS:
                            act.wait_ge(s_agg, n + 1)
                            nc.scalar.copy(agg[:, m, a:a + w], bank[:, n % 2, 0:w]).then_inc(s_aggc, 1)
                            n += 1
                    for m in range(KB):
                        act.wait_ge(s_kvw, m + 1)
                        nc.scalar.copy(kvw[:, m], bank[:, 4 + m % 2, :]).then_inc(s_kvwc, 1)
        layer0.close()

        with ExitStack() as moe:
            ex_b = moe
            choice = sb("choice", [TP, 2, NT], scope=moe)
            place_i = sb("place_i", [TP, 2, NT], U32, scope=moe)
            table_i = sb("table_i", [1, 2, E0 + 1], I32, scope=moe)
            w1_sb = sb("w1_sb", [P, 2, KB, F0], scope=moe)
            w2_sb = sb("w2_sb", [P, 2, FB, D], scope=moe)
            b1_sb = sb("b1_sb", [P, 2, FB], scope=moe)
            b2_sb = sb("b2_sb", [P, 2, D], scope=moe)
            s_w = [sem(f"expert_loaded_{e}") for e in range(E0)]
            s_hd, s_gelu, s_yd, s_ye, s_yst, s_xl, s_xt, s_xr = (sem(n) for n in (
                "hidden_ready", "gelu_ready", "y_ready", "y_added", "y_stored", "slot_loaded", "slot_turned", "slot_columns"))

            def load_expert(eng, e):
                q = e % 2
                eng.dma_start(w1_sb[:, q], blocks(t["L0_ffn_w1"][e])).then_inc(s_w[e], 16)
                eng.dma_start(w2_sb[:, q], blocks(t["L0_ffn_w2"][e])).then_inc(s_w[e], 16)
                eng.dma_start(b1_sb[:, q], t["L0_ffn_b1"][e]).then_inc(s_w[e], 16)
                eng.dma_start(b2_sb[:, q], t["L0_ffn_b2"][e].partition_broadcast(P)).then_inc(s_w[e], 16)

            with ExitStack() as scope:
                gate_w = sb("gate_w", [P, KB, E0], scope=scope)
                gate_b = sb("gate_b", [TP, E0], scope=scope)
                pr, ex, oh1, oh2, ky, p2, m01, rank = (sb(n, [TP, NT, E0], scope=scope) for n in (
                    "probs", "eq", "first_hot", "second_hot", "keys", "probs_2", "chosen", "rank"))
                mx, sm, r1, r2 = (sb(n, [TP, NT], scope=scope) for n in ("mx", "sm", "r1", "r2"))
                tot = sb("tot", [TP, NT + 1, E0], scope=scope)
                gt = sb("gt", [TP, E0, NT], scope=scope)
                tbl = sb("tbl", [TP, 2, E0 + 1], scope=scope)
                place = sb("place", [TP, 2, NT], scope=scope)
                s_lg, s_oh, s_pre, s_pl, s_sc = (sem(n) for n in ("logits_ready", "chosen_ready", "counts_ready", "places_ready", "scattered"))

                with nc.Block() as block:
                    layernorm(block, 1)

                with nc.Block() as block:
                    @block.sync
                    def _(sp):
                        sp.dma_start(gate_w[:], blocks(t["L0_ffn_gate_w"])).then_inc(s_gate_w, 16)
                        sp.dma_start(gate_b[:], t["L0_ffn_gate_b"].partition_broadcast(TP)).then_inc(s_gate_w, 16)
                        load_expert(sp, 0)
                        load_expert(sp, 1)

                    @block.tensor
                    def _(pe):
                        pe.wait_ge(s_gate_w, 32)
                        for i in range(NT):
                            for b in range(KB):
                                ins = nc.tensor.matmul(bank[0:TP, 0, i * E0:(i + 1) * E0], xn_c[:, b, i * TP:(i + 1) * TP],
                                                       gate_w[:, b], start=b == 0, stop=b == KB - 1)
                        ins.then_inc(s_lg, 1)
                        pe.wait_ge(s_oh, 2)
                        hot = m01[:].rearrange("p t e -> p (t e)")
                        nc.tensor.matmul(bank[0:TP, 1, 0:NT * E0], before[0:TP, 0:TP], hot, start=True, stop=True)
                        nc.tensor.matmul(bank[0:TP, 2, 0:NT * E0], ones[0:TP, 0:TP], hot, start=True, stop=True).then_inc(s_pre, 1)

                    @block.vector
                    def _(dve):
                        chain = Chain(dve, dve_n)
                        V = nc.vector
                        full = [TP, NT, E0]

                        def over_e(a):
                            return a.unsqueeze(2).to_broadcast(full)

                        def over_t(a):
                            return a.unsqueeze(1).to_broadcast(full)
                        iota_e = over_t(smallc[0:TP, 128:128 + E0])
                        dve.wait_ge(s_gate_w, 32)
                        dve.wait_ge(s_lg, 1)
                        lg = bank[0:TP, 0, 0:NT * E0].rearrange("p (t e) -> p t e", e=E0)
                        chain(V.tensor_tensor(pr[:], lg, over_t(gate_b[:]), ALU.add))
                        chain(V.tensor_reduce(mx[:], pr[:], AX.X, ALU.max))
                        V.tensor_tensor(pr[:], pr[:], over_e(mx[:]), ALU.subtract).then_inc(s_oh, 1)
                        dve.wait_ge(act_n.sem, act_n.n + 1)
                        chain(V.tensor_reduce(sm[:], pr[:], AX.X, ALU.add))
                        chain(V.reciprocal(sm[:], sm[:]))
                        chain(V.tensor_tensor(pr[:], pr[:], over_e(sm[:]), ALU.mult))

                        def pick(probs, best, hot):
                            chain(V.tensor_reduce(best, probs, AX.X, ALU.max))
                            chain(V.tensor_tensor(ex[:], probs, over_e(best), ALU.is_equal))
                            chain(V.scalar_tensor_tensor(ky[:], ex[:], -float(E0), iota_e, ALU.mult, ALU.add))
                            chain(V.tensor_reduce(mx[:], ky[:], AX.X, ALU.min))
                            chain(V.tensor_tensor(hot, ky[:], over_e(mx[:]), ALU.is_equal))
                        pick(pr[:], r1[:], oh1[:])
                        chain(V.scalar_tensor_tensor(p2[:], oh1[:], -2.0, pr[:], ALU.mult, ALU.add))
                        pick(p2[:], r2[:], oh2[:])
                        V.tensor_tensor(m01[:], oh1[:], oh2[:], ALU.add).then_inc(s_oh, 1)
                        chain(V.tensor_tensor(sm[:], r1[:], r2[:], ALU.add))
                        chain(V.reciprocal(sm[:], sm[:]))
                        chain(V.tensor_tensor(choice[:, 0], r1[:], sm[:], ALU.mult))
                        chain(V.tensor_tensor(choice[:, 1], r2[:], sm[:], ALU.mult))
                        chain(V.memset(tot[:, 0], 0.0))
                        dve.wait_ge(s_pre, 1)
                        for i in range(NT):
                            chain(V.tensor_tensor(tot[:, i + 1], tot[:, i], bank[0:TP, 2, i * E0:(i + 1) * E0], ALU.add))
                        steps = smallc[0:TP, 144:144 + NT].unsqueeze(1).to_broadcast([TP, E0, NT])
                        chain(V.tensor_tensor(gt[:], tot[:, NT].unsqueeze(2).to_broadcast([TP, E0, NT]), steps, ALU.is_gt))
                        chain(V.tensor_reduce(tbl[:, 0, 0:E0], gt[:], AX.X, ALU.add))
                        chain(V.tensor_scalar(tbl[:, 0, 0:E0], tbl[:, 0, 0:E0], 1.0, None, ALU.max))
                        chain(V.memset(tbl[:, 1, 0:1], 0.0))
                        chain(V.memset(tbl[:, 0, E0:E0 + 1], 0.0))
                        for e in range(E0):
                            chain(V.tensor_tensor(tbl[:, 1, e + 1:e + 2], tbl[:, 1, e:e + 1], tbl[:, 0, e:e + 1], ALU.add))
                        chain(V.tensor_copy(table_i[:], tbl[0:1]))
                        pre = bank[0:TP, 1, 0:NT * E0].rearrange("p (t e) -> p t e", e=E0)
                        chain(V.tensor_tensor(rank[:], tot[:, 0:NT], pre, ALU.add))
                        chain(V.scalar_tensor_tensor(rank[:], over_t(tbl[:, 1, 0:E0]), float(SLOT), rank[:], ALU.mult, ALU.add))
                        for c, hot in enumerate((oh1, oh2)):
                            chain(V.tensor_tensor(ky[:], hot[:], rank[:], ALU.mult))
                            chain(V.tensor_reduce(place[:, c], ky[:], AX.X, ALU.add))
                        V.tensor_copy(place_i[:], place[:]).then_inc(s_pl, 1)

                    @block.scalar
                    def _(act):
                        act.wait_ge(s_oh, 1)
                        act_n.add(nc.scalar.activation(pr[:], pr[:], ACT.Exp))

                    @block.gpsimd
                    def _(pool):
                        pool.wait_ge(s_pl, 1)
                        for i in range(NT):
                            for c in range(2):
                                pool.indirect_dma_start(
                                    out=slots_x, out_offset=bass.IndirectOffsetOnAxis(ap=place_i[:, c, i:i + 1], axis=0),
                                    in_=xn_r[:, i], in_offset=None).then_inc(s_sc, 16)
                        pool.wait_ge(s_sc, 16 * 2 * NT)

            with ExitStack() as scope:
                s_free, s_stored = sem("expert_buffers_free"), sem("results_stored")
                slot_r = sb("slot_r", [P, D], scope=scope)
                slot_c = sb("slot_c", [P, KB, P], scope=scope)
                hid = sb("hid", [P, FB, P], scope=scope)
                y_sb = sb("y_sb", [P, D], scope=scope)
                hid_p = bank[:, 4:8, 0:P]
                turn_p = bank[:, 2, :].rearrange("p (b n) -> p b n", b=KB)
                y_p = bank[:, 3, :]

                def expert_slots(eng, e):
                    count = eng.value_load(table_i[0:1, 0, e:e + 1], min_val=1, max_val=NT)
                    base = eng.value_load(table_i[0:1, 1, e:e + 1], min_val=0, max_val=SLOTS - 1)
                    return count, base

                def slot_rows(dram, g):
                    if not isinstance(g, int):
                        g = nc.s_assert_within(g, 0, SLOTS - 1, skip_runtime_bounds_check_because=(
                            "the experts' slots number SLOTS - 1 at most, as their sizes sum to 2 N"))
                    return dram.rearrange("(s p) d -> s p d", p=SLOT)[bass.ds(g, 1)].rearrange("a p d -> (a p) d")

                with nc.Block() as block:
                    @block.gpsimd
                    def _(pool):
                        for e in range(2, E0):
                            count, base = expert_slots(pool, e - 2)
                            pool.wait_ge(s_ye, base + count + 1)
                            pool.sem_inc(s_free, 1)
                            pool.wait_ge(s_free, e - 1)
                            load_expert(pool, e)

                    @block.sync
                    def _(sp):
                        sp.sem_inc(s_yst, 16)
                        sp.dma_start(slot_r[:], slot_rows(slots_x, 0)).then_inc(s_xl, 16)
                        for e in range(E0):
                            count, base = expert_slots(sp, e)
                            with sp.Fori(0, count) as i:
                                g = base + i
                                sp.wait_ge(s_xt, g + 1)
                                sp.dma_start(slot_r[:], slot_rows(slots_x, g + 1)).then_inc(s_xl, 16)
                                sp.wait_ge(s_ye, g + 2)
                                sp.dma_start(slot_rows(slots_y, g), y_sb[:]).then_inc(s_yst, 16)
                        total = sp.value_load(table_i[0:1, 1, E0:E0 + 1], min_val=E0, max_val=SLOTS - 1)
                        sp.wait_ge(s_yst, 16 * total + 16)
                        sp.sem_inc(s_stored, 1)
                        sp.wait_ge(s_stored, 1)

                    @block.tensor
                    def _(pe):
                        def turn(g):
                            pe.wait_ge(s_xl, 16 * (g + 1))
                            for b in range(KB):
                                ins = nc.tensor.transpose(turn_p[:, b], slot_r[:, b * P:(b + 1) * P], ident[:])
                            ins.then_inc(s_xt, 1)

                        pe.sem_inc(s_yd, 1)
                        turn(0)
                        for e in range(E0):
                            q = e % 2
                            pe.wait_ge(s_w[e], 64)
                            count, base = expert_slots(pe, e)
                            with pe.Fori(0, count) as i:
                                g = base + i
                                pe.wait_ge(s_xr, g + 1)
                                for f in range(FB):
                                    if f >= 4:
                                        pe.wait_ge(s_gelu, g * FB + f - 3)
                                    for b in range(KB):
                                        ins = nc.tensor.matmul(hid_p[:, f % 4], w1_sb[:, q, b, f * P:(f + 1) * P], slot_c[:, b],
                                                               start=b == 0, stop=b == KB - 1)
                                    ins.then_inc(s_hd, 1)
                                turn(g + 1)
                                pe.wait_ge(s_ye, g + 1)
                                for f in range(FB):
                                    pe.wait_ge(s_gelu, g * FB + f + 1)
                                    ins = nc.tensor.matmul(y_p, hid[:, f], w2_sb[:, q, f], start=f == 0, stop=f == FB - 1)
                                ins.then_inc(s_yd, 1)

                    @block.scalar
                    def _(act):
                        for e in range(E0):
                            q = e % 2
                            act.wait_ge(s_w[e], 64)
                            count, base = expert_slots(act, e)
                            with act.Fori(0, count) as i:
                                g = base + i
                                act.wait_ge(s_yd, g + 1)
                                for f in range(FB):
                                    act.wait_ge(s_hd, g * FB + f + 1)
                                    nc.scalar.activation(hid[:, f], hid_p[:, f % 4], ACT.Gelu,
                                                         bias=b1_sb[:, q, f:f + 1]).then_inc(s_gelu, 1)

                    @block.vector
                    def _(dve):
                        dve.sem_inc(s_ye, 1)
                        dve.wait_ge(s_xt, 1)
                        nc.vector.tensor_copy(slot_c[:], turn_p).then_inc(s_xr, 1)
                        for e in range(E0):
                            q = e % 2
                            dve.wait_ge(s_w[e], 64)
                            count, base = expert_slots(dve, e)
                            with dve.Fori(0, count) as i:
                                g = base + i
                                dve.wait_ge(s_xt, g + 2)
                                nc.vector.tensor_copy(slot_c[:], turn_p).then_inc(s_xr, 1)
                                dve.wait_ge(s_yd, g + 2)
                                dve.wait_ge(s_yst, 16 * g + 16)
                                nc.vector.tensor_tensor(y_sb[:], y_p, b2_sb[:, q], ALU.add).then_inc(s_ye, 1)

            with ExitStack() as scope:
                got = sb("got", [TP, 4, D], scope=scope)
                s_got = [sem(f"gathered_{q}") for q in range(4)]
                s_mix = sem("gathered_used")
                with nc.Block() as block:
                    @block.gpsimd
                    def _(pool):
                        for n in range(2 * NT):
                            i, c = n // 2, n % 2
                            if n >= 4:
                                pool.wait_ge(s_mix, n - 3)
                            pool.indirect_dma_start(
                                out=got[:, n % 4], out_offset=None, in_=slots_y,
                                in_offset=bass.IndirectOffsetOnAxis(ap=place_i[:, c, i:i + 1], axis=0)).then_inc(s_got[n % 4], 16)

                    @block.vector
                    def _(dve):
                        for n in range(2 * NT):
                            i, c = n // 2, n % 2
                            dve.wait_ge(s_got[n % 4], 16 * (n // 4 + 1))
                            nc.vector.scalar_tensor_tensor(x_res[:, i], got[:, n % 4], choice[:, c, i:i + 1], x_res[:, i],
                                                           ALU.mult, ALU.add).then_inc(s_mix, 1)
                            dve.wait_ge(s_mix, n + 1)

        with ExitStack() as layer1:
            qi = sb("qi", [P, H * N], scope=layer1)
            qi_h = qi[:].rearrange("p (h n) -> p h n", h=H)
            wqkv1 = qi[:, 0:KB * 3 * D].rearrange("p (b n) -> p b n", b=KB)
            w_out = sb("w_out", [P, KB, D], scope=layer1)
            bias_c = sb("bias_c", [P, H + KB], scope=layer1)
            s_w1l, s_wg = sem("layer1_mix_weights"), sem("layer1_gnn_weights")

            with ExitStack() as scope:
                w_g = sb("w_g", [P, KB, D], scope=scope)
                w_t = sb("w_t", [P, 2, D], scope=scope)
                t_emb = sb("t_emb", [P, 2], scope=scope)
                t_rep = sb("t_rep", [P, 2, TP], scope=scope)
                bias3 = sb("bias3", [TP, 3, D], scope=scope)
                bias_r = sb("bias_r", [TP, D], scope=scope)
                dinv = sb("dinv", [TP, NT], scope=scope)
                xw = sb("xw", [TP, NT, D], scope=scope)
                utmp = bias3
                s_dinv, s_te, s_xw, s_xwc, s_hop, s_hopc, s_trep, s_b3 = (sem(n) for n in (
                    "dinv_ready", "time_ready", "xw_ready", "xw_copied", "hop_ready", "hop_used", "time_repeated", "bias_summed"))
                with nc.Block() as block:
                    layernorm(block, 2)

                    @block.sync
                    def _(sp):
                        sp.dma_start(w_g[:], blocks(t["L1_gnn_W"])).then_inc(s_wg, 16)
                        sp.dma_start(w_t[:], blocks(t["L1_gnn_Wt"])).then_inc(s_wg, 16)
                        sp.dma_start(t_emb[:], t["L1_gnn_t_emb"]).then_inc(s_wg, 16)
                        for c, name in enumerate(("L1_gnn_b", "L1_gnn_bt", "L1_mix_b_out")):
                            sp.dma_start(bias3[:, c], t[name].partition_broadcast(TP)).then_inc(s_wg, 16)
                        sp.dma_start(wqkv1, blocks(t["L1_mix_W_qkv"])).then_inc(s_w1l, 16)
                        sp.dma_start(w_out[:], blocks(t["L1_mix_W_out"])).then_inc(s_w1l, 16)
                        sp.dma_start(bias_c[:], t["L1_mix_b_qkv"]).then_inc(s_w1l, 16)

                with nc.Block() as block:
                    @block.tensor
                    def _(pe):
                        pe.wait_ge(s_wg, 96)
                        for i in range(NT):
                            if i >= 2:
                                pe.wait_ge(s_xwc, i - 1)
                            for b in range(KB):
                                ins = nc.tensor.matmul(bank[0:TP, i % 2, :], xn_c[:, b, i * TP:(i + 1) * TP], w_g[:, b],
                                                       start=b == 0, stop=b == KB - 1)
                            ins.then_inc(s_xw, 1)
                        pe.wait_ge(s_trep, 1)
                        for b in range(2):
                            ins = nc.tensor.matmul(bank[0:TP, 2, :], t_rep[:, b], w_t[:, b], start=b == 0, stop=b == 1)
                        ins.then_inc(s_te, 1)
                        pe.wait_ge(s_xwc, NT)
                        for i in range(NT):
                            if i >= 2:
                                pe.wait_ge(s_hopc, i - 1)
                            for s in range(NT):
                                ins = nc.tensor.matmul(bank[0:TP, 3 + i % 2, :], adj_t[:, s, i * TP:(i + 1) * TP], xw[:, s],
                                                       start=s == 0, stop=s == NT - 1)
                            ins.then_inc(s_hop, 1)

                    @block.scalar
                    def _(act):
                        act.wait_ge(s_dinv, 1)
                        nc.scalar.activation(rs_root[:], rs_var[:], ACT.Sqrt).then_inc(s_dinv, 1)
                        act.wait_ge(s_dinv, 3)
                        for i in range(NT):
                            act.wait_ge(s_xw, i + 1)
                            nc.scalar.activation(xw[:, i], bank[0:TP, i % 2, :], ACT.Copy, scale=dinv[:, i:i + 1]).then_inc(s_xwc, 1)

                    @block.vector
                    def _(dve):
                        chain = Chain(dve, dve_n)
                        nc.vector.tensor_scalar(rs_var[:], deg[:], 1.0, None, ALU.add).then_inc(s_dinv, 1)
                        dve.wait_ge(s_dinv, 2)
                        refine_rsqrt(chain, dinv[:], rs_var[:], rs_root[:], rs_tmp[:])
                        dve.engine_nop().then_inc(s_dinv, 1)
                        dve.wait_ge(s_wg, 96)
                        nc.vector.tensor_scalar(t_rep[:, 0], ones[:, 0:TP], t_emb[:, 0:1], None, ALU.mult)
                        nc.vector.tensor_scalar(t_rep[:, 1], ones[:, 0:TP], t_emb[:, 1:2], None, ALU.mult).then_inc(s_trep, 1)
                        chain(nc.vector.tensor_tensor(bias_r[:], bias3[:, 0], bias3[:, 1], ALU.add))
                        chain(nc.vector.tensor_tensor(bias_r[:], bias_r[:], bias3[:, 2], ALU.add))
                        dve.wait_ge(s_te, 1)
                        chain(nc.vector.tensor_tensor(bias_r[:], bias_r[:], bank[0:TP, 2, :], ALU.add))
                        for i in range(NT):
                            chain(nc.vector.tensor_tensor(x_res[:, i], x_res[:, i], bias_r[:], ALU.add))
                        dve.wait_ge(s_xwc, NT)
                        for i in range(NT):
                            dve.wait_ge(s_hop, i + 1)
                            y = utmp[:, i % 2]
                            chain(nc.vector.tensor_tensor(y, bank[0:TP, 3 + i % 2, :], xw[:, i], ALU.add))
                            nc.vector.scalar_tensor_tensor(x_res[:, i], y, dinv[:, i:i + 1], x_res[:, i],
                                                           ALU.mult, ALU.add).then_inc(s_hopc, 1)
                        dve.wait_ge(s_hopc, NT)

            with ExitStack() as scope:
                NC5, CW = 5, 250
                qk = sb("qk", [P, H, N], scope=scope)
                kv = adj[:, 0:H * N].rearrange("p (g h s) -> p g h s", g=GROUPS, h=H)
                r_c = xn[:, 0:KB * N].rearrange("p (b n) -> p b n", b=KB)
                free = xn_c[:].rearrange("p b n -> p (b n)")
                inv, sg = free[:, 0:N], free[:, N:2 * N]
                sums, sums2, smx, sme = (sb(n, [P, H], scope=scope) for n in ("sums", "sums2", "smx", "sme"))
                sw = sb("sw", [P, H], scope=scope)
                lh = free[:, 2 * N:2 * N + H * P].rearrange("p (h n) -> p h n", h=H)
                pm_sb = free[:, 2 * N + H * P:2 * N + H * P + 2 * BATCH * GW].rearrange("p (q n) -> p q n", q=2)
                vg_sb = sb("vg_sb", [P, 2, BATCH * HD], scope=scope)
                swap = sb("swap", [P, P], scope=scope)
                (s_qk, s_qkc, s_v, s_vcp, s_sw, s_swr, s_lh, s_io, s_ioc, s_hat, s_sig, s_mx, s_ex, s_kt, s_qt,
                 s_pm, s_pmc, s_vgc, s_r, s_rc, s_o, s_oc) = (sem(n) for n in (
                     "qk_ready", "qk_sigmoid", "v_ready", "v_biased", "sums_swapped", "sums_ready", "heads_ready", "io_ready",
                     "io_used", "hat_ready", "sig_ready", "max_ready", "exp_hat_ready", "k_weighted", "q_weighted",
                     "pm_ready", "pm_masked", "v_turned", "r_ready", "r_copied", "out1_ready", "out1_used"))

                def banks3(q):
                    return bank[:, 3 * q:3 * q + 3, :].rearrange("p b (r n) -> p (b r) n", n=256)

                def head_chunks(q):
                    return banks3(q)[:, 0:NC5, 0:CW]

                def by5(a):
                    return a.rearrange("p (c n) -> p c n", c=NC5)

                def by_group(a):
                    return a.rearrange("p (g s) -> p g s", s=GROUP)

                with nc.Block() as block:
                    @block.tensor
                    def _(pe):
                        pe.wait_ge(s_w1l, 48)
                        for h in range(H):
                            if h >= 2:
                                pe.wait_ge(s_qkc, h - 1)
                            for c in range(NC5):
                                for b in range(KB):
                                    ins = nc.tensor.matmul(banks3(h % 2)[:, c, 0:CW], wqkv1[:, b, h * P:(h + 1) * P],
                                                           xn_c[:, b, c * CW:(c + 1) * CW], start=b == 0, stop=b == KB - 1)
                            ins.then_inc(s_qk, 1)
                        for m in range(KB):
                            if m < 2:
                                pe.wait_ge(s_qkc, H - 1 + m)
                            else:
                                pe.wait_ge(s_vcp, 2 * m - 2)
                            for c in range(NC5):
                                for b in range(KB):
                                    ins = nc.tensor.matmul(banks3(m % 2)[:, c, 0:CW], wqkv1[:, b, 2 * D + m * P:2 * D + (m + 1) * P],
                                                           xn_c[:, b, c * CW:(c + 1) * CW], start=b == 0, stop=b == KB - 1)
                            ins.then_inc(s_v, 1)
                        pe.wait_ge(s_qkc, H)
                        nc.tensor.matmul(bank[:, 6, 0:H], swap[:], sums[:], start=True, stop=True).then_inc(s_sw, 1)
                        for h in range(H):
                            pe.wait_ge(s_lh, h + 1)
                            if h < 2:
                                pe.wait_ge(s_vcp, 2 * KB - 2 + 2 * h)
                            else:
                                pe.wait_ge(s_ioc, h - 1)
                            for c in range(NC5):
                                ins = nc.tensor.matmul(banks3(h % 2)[:, c, 0:CW], lh[:, h], qk[:, h, c * CW:(c + 1) * CW],
                                                       start=True, stop=True)
                            ins.then_inc(s_io, 1)
                        pe.wait_ge(s_swr, 1)
                        nc.tensor.matmul(bank[:, 6, 0:H], swap[:], sums2[:], start=True, stop=True).then_inc(s_sw, 1)
                        for h in range(H):
                            pe.wait_ge(s_lh, H + h + 1)
                            if h < 2:
                                pe.wait_ge(s_ioc, H - 1 + h)
                            else:
                                pe.wait_ge(s_ex, h - 1)
                            for c in range(NC5):
                                ins = nc.tensor.matmul(banks3(h % 2)[:, c, 0:CW], lh[:, h], qk[:, h, c * CW:(c + 1) * CW],
                                                       start=True, stop=True)
                            ins.then_inc(s_hat, 1)

                    @block.scalar
                    def _(act):
                        for h in range(H):
                            act.wait_ge(s_qk, h + 1)
                            nc.scalar.activation(by5(qk[:, h, 0:N]), head_chunks(h % 2), ACT.Sigmoid, bias=bias_c[:, h:h + 1],
                                                 accum_out=sums[:, h:h + 1]).then_inc(s_qkc, 1)
                        for h in range(H):
                            act.wait_ge(s_hat, h + 1)
                            if h >= 1:
                                act.wait_ge(s_qt, h)
                                act.wait_ge(s_kt, h)
                            nc.scalar.activation(by5(sg[0:HD]), head_chunks(h % 2)[0:HD], ACT.Sigmoid).then_inc(s_sig, 1)
                            act.wait_ge(s_mx, h + 1)
                            nc.scalar.activation(by5(sg[HD:P]), head_chunks(h % 2)[HD:P], ACT.Exp, bias=smx[HD:P, h:h + 1],
                                                 accum_out=sme[HD:P, h:h + 1]).then_inc(s_ex, 1)

                    @block.vector
                    def _(dve):
                        chain = Chain(dve, dve_n)
                        V = nc.vector
                        V.tensor_copy(swap[:, 0:HD], ident[:, HD:P])
                        chain(V.tensor_copy(swap[:, HD:P], ident[:, 0:HD]))
                        for m in range(KB):
                            dve.wait_ge(s_v, m + 1)
                            for c in range(2):
                                rows = slice(c * HD, (c + 1) * HD)
                                V.tensor_scalar(kv[HD:P, :, 2 * m + c].rearrange("p (c g) s -> p c g s", c=NC5),
                                                head_chunks(m % 2)[rows].rearrange("p c (g s) -> p c g s", s=GROUP),
                                                bias_c[rows, H + m:H + m + 1], None, ALU.add).then_inc(s_vcp, 1)

                        def heads(n):
                            dve.wait_ge(s_sw, n)
                            chain(V.tensor_copy(sw[:], bank[:, 6, 0:H]))
                            for h in range(H):
                                if n == 2:
                                    dve.wait_ge(s_io, H)
                                V.tensor_scalar(lh[:, h], headmask[:], sw[:, h:h + 1], None, ALU.mult).then_inc(s_lh, 1)
                        heads(1)
                        for h in range(H):
                            dve.wait_ge(s_io, h + 1)
                            chain(V.reciprocal(by5(inv), head_chunks(h % 2)))
                            V.tensor_tensor_reduce(qi_h[:, h, 0:N], qk[:, h, 0:N], inv, 1.0, 0.0, ALU.mult, ALU.add,
                                                   sums2[:, h:h + 1]).then_inc(s_ioc, 1)
                            dve.wait_ge(s_ioc, h + 1)
                        V.engine_nop().then_inc(s_swr, 1)
                        heads(2)
                        for h in range(H):
                            dve.wait_ge(s_hat, h + 1)
                            chain(V.tensor_reduce(smx[HD:P, h:h + 1], head_chunks(h % 2)[HD:P], AX.XY, ALU.max))
                            V.tensor_scalar(smx[HD:P, h:h + 1], smx[HD:P, h:h + 1], -1.0, None, ALU.mult).then_inc(s_mx, 1)
                            dve.wait_ge(s_sig, h + 1)
                            V.tensor_tensor(qi_h[0:HD, h, 0:N], qi_h[0:HD, h, 0:N], sg[0:HD], ALU.mult).then_inc(s_qt, 1)
                            dve.wait_ge(s_ex, h + 1)
                            chain(V.reciprocal(sme[HD:P, h:h + 1], sme[HD:P, h:h + 1]))
                            V.scalar_tensor_tensor(kv[0:HD, :, h], by_group(sg[HD:P]), sme[HD:P, h:h + 1],
                                                   by_group(qk[HD:P, h]),
                                                   ALU.mult, ALU.mult).then_inc(s_kt, 1)
                        dve.wait_ge(s_kt, H)

                with nc.Block() as block:
                    NB = GROUPS // BATCH

                    def score_bank(q):
                        return bank[0:GW, q, 0:BATCH * GW].rearrange("p (j n) -> p j n", n=GW)

                    @block.tensor
                    def _(pe):
                        def scores(n):
                            if n >= 2:
                                pe.wait_ge(s_pmc, n - 1)
                                pe.wait_ge(s_vgc, n - 1)
                            for j in range(BATCH):
                                g = n * BATCH + j
                                tok = slice(g * GROUP, (g + 1) * GROUP)
                                nc.tensor.matmul(bank[0:GW, n % 2, j * GW:(j + 1) * GW],
                                                 kv[0:HD, g].rearrange("p h s -> p (h s)"), qi_h[0:HD, :, tok],
                                                 start=True, stop=True)
                                ins = nc.tensor.transpose(bank[0:GW, 2 + n % 2, j * HD:(j + 1) * HD],
                                                          kv[HD:P, g].rearrange("p h s -> p (h s)"), ident[HD:P, HD:P])
                            ins.then_inc(s_pm, 1)

                        def values(n):
                            pe.wait_ge(s_pmc, n + 1)
                            pe.wait_ge(s_vgc, n + 1)
                            if n >= 2:
                                pe.wait_ge(s_rc, n - 1)
                            for j in range(BATCH):
                                ins = nc.tensor.matmul(bank[0:HD, 4 + n % 2, j * GW:(j + 1) * GW],
                                                       vg_sb[0:GW, n % 2, j * HD:(j + 1) * HD],
                                                       pm_sb[0:GW, n % 2, j * GW:(j + 1) * GW], start=True, stop=True)
                            ins.then_inc(s_r, 1)
                        for n in range(NB):
                            scores(n)
                            if n >= 1:
                                values(n - 1)
                        values(NB - 1)
                        pe.wait_ge(s_rc, NB)
                        for i in range(NT):
                            if i >= 2:
                                pe.wait_ge(s_oc, i - 1)
                            for b in range(KB):
                                ins = nc.tensor.matmul(bank[0:TP, 6 + i % 2, :], r_c[:, b, i * TP:(i + 1) * TP], w_out[:, b],
                                                       start=b == 0, stop=b == KB - 1)
                            ins.then_inc(s_o, 1)

                    def r_in(n, par):
                        return bank[0:HD, 4 + n % 2, 0:BATCH * GW].rearrange("p (j b c s) -> p c b j s", j=BATCH, b=KB, c=2)[:, par]

                    def r_out(n, par):
                        cols = r_c[par * HD:(par + 1) * HD, :, n * BATCH * GROUP:(n + 1) * BATCH * GROUP]
                        return cols.rearrange("p b (j s) -> p b j s", j=BATCH)

                    @block.vector
                    def _(dve):
                        mask4 = tokmask[0:GW, 0:GW].unsqueeze(1).to_broadcast([GW, BATCH, GW])
                        for n in range(NB):
                            dve.wait_ge(s_pm, n + 1)
                            if n >= 2:
                                dve.wait_ge(s_r, n - 1)
                            nc.vector.tensor_tensor(pm_sb[0:GW, n % 2].rearrange("p (j n) -> p j n", n=GW), score_bank(n % 2), mask4,
                                                    ALU.mult).then_inc(s_pmc, 1)
                            nc.vector.tensor_copy(vg_sb[0:GW, n % 2], bank[0:GW, 2 + n % 2, 0:BATCH * HD]).then_inc(s_vgc, 1)
                        for i in range(NT):
                            dve.wait_ge(s_o, i + 1)
                            nc.vector.tensor_tensor(x_res[:, i], x_res[:, i], bank[0:TP, 6 + i % 2, :], ALU.add).then_inc(s_oc, 1)
                        dve.wait_ge(s_oc, NT)

                    @block.scalar
                    def _(act):
                        for n in range(NB):
                            act.wait_ge(s_r, n + 1)
                            nc.scalar.copy(r_out(n, 0), r_in(n, 0))
                            nc.scalar.copy(r_out(n, 1), r_in(n, 1)).then_inc(s_rc, 1)

            with ExitStack() as scope:
                wg = sb("wg", [P, KB, E1], scope=scope)
                bg = sb("bg", [TP, E1], scope=scope)
                mean_c = sb("mean_c", [P, KB], scope=scope)
                mean_rep = sb("mean_rep", [P, KB, TP], scope=scope)
                lg, eg, kg = (sb(n, [TP, E1], scope=scope) for n in ("lg", "eg", "kg"))
                sc = sb("sc", [TP, 8], scope=scope)
                pick_i = sb("pick_i", [1, 1], I32, scope=scope)
                w_e = sb("w_e", [P, KB, D], scope=scope)
                b_e = sb("b_e", [TP, D], scope=scope)
                ytmp = sb("ytmp", [TP, 2, D], scope=scope)
                s_g1, s_mean, s_l1, s_e1, s_pick, s_we, s_y, s_yc, s_st = (sem(n) for n in (
                    "gate1_weights", "mean_ready", "logits1_ready", "exp1_ready", "pick_ready", "picked_loaded", "y1_ready", "x_done", "x_stored"))
                with nc.Block() as block:
                    layernorm(block, 3)

                    @block.sync
                    def _(sp):
                        sp.dma_start(wg[:], blocks(t["L1_ffn_Wg"])).then_inc(s_g1, 16)
                        sp.dma_start(bg[:], t["L1_ffn_bg"].partition_broadcast(TP)).then_inc(s_g1, 16)

                with nc.Block() as block:
                    @block.sync
                    def _(sp):
                        sp.wait_ge(s_pick, 1)
                        e = sp.value_load(pick_i[0:1, 0:1], min_val=0, max_val=E1 - 1)
                        sp.dma_start(w_e[:], t["L1_ffn_We"][bass.ds(e, 1)].rearrange("a (b p) n -> p (a b) n", p=P)).then_inc(s_we, 16)
                        sp.dma_start(b_e[:], t["L1_ffn_be"][bass.ds(e, 1)].rearrange("a n -> (a n)").partition_broadcast(TP)).then_inc(s_we, 16)
                        for i in range(NT):
                            sp.wait_ge(s_yc, i + 1)
                            sp.dma_start(t["out"][i * TP:(i + 1) * TP, :], x_res[:, i]).then_inc(s_st, 16)
                        sp.wait_ge(s_st, 16 * NT)

                    @block.tensor
                    def _(pe):
                        pe.wait_ge(s_mean, 1)
                        pe.wait_ge(s_g1, 32)
                        for b in range(KB):
                            ins = nc.tensor.matmul(bank[0:TP, 0, 0:E1], mean_rep[:, b], wg[:, b], start=b == 0, stop=b == KB - 1)
                        ins.then_inc(s_l1, 1)
                        pe.wait_ge(s_we, 32)
                        for i in range(NT):
                            if i >= 2:
                                pe.wait_ge(s_yc, i - 1)
                            for b in range(KB):
                                ins = nc.tensor.matmul(bank[0:TP, 1 + i % 2, :], xn_c[:, b, i * TP:(i + 1) * TP], w_e[:, b],
                                                       start=b == 0, stop=b == KB - 1)
                            ins.then_inc(s_y, 1)

                    @block.scalar
                    def _(act):
                        act.wait_ge(s_e1, 1)
                        nc.scalar.activation(eg[:], lg[:], ACT.Exp, bias=sc[:, 0:1], accum_out=sc[:, 1:2]).then_inc(s_e1, 1)

                    @block.vector
                    def _(dve):
                        chain = Chain(dve, dve_n)
                        V = nc.vector
                        chain(V.tensor_reduce(mean_c[:], xn_c[:], AX.X, ALU.add))
                        chain(V.tensor_scalar(mean_c[:], mean_c[:], 1.0 / N, None, ALU.mult))
                        for b in range(KB):
                            ins = V.tensor_scalar(mean_rep[:, b], ones[:, 0:TP], mean_c[:, b:b + 1], None, ALU.mult)
                        ins.then_inc(s_mean, 1)
                        dve.wait_ge(s_l1, 1)
                        dve.wait_ge(s_g1, 32)
                        chain(V.tensor_tensor(lg[:], bank[0:TP, 0, 0:E1], bg[:], ALU.add))
                        chain(V.tensor_reduce(sc[:, 2:3], lg[:], AX.X, ALU.max))
                        V.tensor_scalar(sc[:, 0:1], sc[:, 2:3], -1.0, None, ALU.mult).then_inc(s_e1, 1)
                        dve.wait_ge(s_e1, 2)
                        chain(V.reciprocal(sc[:, 3:4], sc[:, 1:2]))
                        chain(V.tensor_reduce(sc[:, 4:5], eg[:], AX.X, ALU.max))
                        chain(V.tensor_tensor(sc[:, 5:6], sc[:, 4:5], sc[:, 3:4], ALU.mult))
                        chain(V.tensor_scalar(kg[:], eg[:], sc[:, 4:5], -float(E1), ALU.is_equal, ALU.mult))
                        chain(V.tensor_tensor(kg[:], kg[:], smallc[0:TP, 128:128 + E1], ALU.add))
                        chain(V.tensor_reduce(sc[:, 6:7], kg[:], AX.X, ALU.min))
                        chain(V.tensor_scalar(sc[:, 6:7], sc[:, 6:7], float(E1), None, ALU.add))
                        V.tensor_copy(pick_i[:], sc[0:1, 6:7]).then_inc(s_pick, 1)
                        dve.wait_ge(s_we, 32)
                        for i in range(NT):
                            dve.wait_ge(s_y, i + 1)
                            y = ytmp[:, i % 2]
                            chain(V.tensor_tensor(y, bank[0:TP, 1 + i % 2, :], b_e[:], ALU.add))
                            V.scalar_tensor_tensor(x_res[:, i], y, sc[:, 5:6], x_res[:, i], ALU.mult, ALU.add).then_inc(s_yc, 1)


def host_constants():
    i = np.arange(P)
    small = np.zeros((P, 256), np.float32)
    small[:NT, 0] = np.arange(NT) * TP
    small[:NT, 1] = np.arange(NT) * TP + TP - 1
    small[:, 8:8 + STEPS] = np.arange(STEPS)
    small[:, 128:144] = np.arange(16)
    small[:, 144:144 + NT] = np.arange(NT) * SLOT
    return {
        "c_ident": np.eye(P, dtype=np.float32),
        "c_before": (i[:, None] < i[None, :]).astype(np.float32),
        "c_ones": np.ones((P, P), np.float32),
        "c_headmask": (i[:, None] // HD == i[None, :] // HD).astype(np.float32),
        "c_tokmask": (i[:, None] % GROUP == i[None, :] % GROUP).astype(np.float32),
        "c_iota": np.broadcast_to(np.arange(N), (P, N)).astype(np.float16),
        "c_small": small,
    }


def kernel(**inputs):
    import concourse.bacc as bacc
    from concourse.bass_utils import run_bass_kernel_spmd

    a = {k: np.asarray(v) for k, v in inputs.items()}
    for name in ("L0_gnn_W_l", "L0_gnn_W_r", "L1_mix_W_out", "L1_mix_W_qkv"):
        a[name] = a[name].T
    order = np.arange(3 * D).reshape(H, 3, HD)
    order = np.concatenate([order[:, 0:2].reshape(-1), order[:, 2].reshape(-1)])
    a["L1_mix_W_qkv"] = a["L1_mix_W_qkv"][:, order]
    a["L1_mix_b_qkv"] = a["L1_mix_b_qkv"][order].reshape(-1, P).T
    a["L1_gnn_t_emb"] = a["L1_gnn_t_emb"].reshape(-1, P).T
    a["L0_ffn_b1"] = a["L0_ffn_b1"].reshape(E0, FB, P).transpose(0, 2, 1)
    a.update(host_constants())
    nc = bacc.Bacc("TRN2", target_bir_lowering=False, num_devices=1)
    arrays, t = {}, {}
    for name, v in a.items():
        v = np.ascontiguousarray(v)
        arrays["in_" + name] = v
        t[name] = nc.dram_tensor("in_" + name, v.shape, mybir.dt.from_np(v.dtype), kind="ExternalInput").ap()
    t["out"] = nc.dram_tensor("out_x", (N, D), F32, kind="ExternalOutput").ap()
    build(nc, t)
    r = run_bass_kernel_spmd(nc, [arrays], core_ids=[0])
    return r.results[0]["out_x"]
```

```python
from contextlib import ExitStack

import numpy as np

import concourse.bass as bass
from concourse import mybir

ALU = mybir.AluOpType
ACT = mybir.ActivationFunctionType
AX = mybir.AxisListType
F32 = mybir.dt.float32
F32R = mybir.dt.float32r
F16 = mybir.dt.float16
BF16 = mybir.dt.bfloat16
I32 = mybir.dt.int32
U32 = mybir.dt.uint32

N, D, EDGES = 1250, 512, 20000
P = 128
TP = 125
NT = N // TP
KB = D // P
CHUNKS = [(0, 500), (500, 500), (1000, 250)]
QT = 4
STEPS = EDGES // (QT * TP)
H, HD = 8, 64
E0, F0, SLOT = 8, 1024, 128
FB = F0 // P
SLOTS = (2 * N - E0) // SLOT + E0 + 1
SLOTS_SURE = 2 * N // SLOT + 1
E1 = 16
EPS_LN, EPS_ATT = 1e-5, 1e-6
GROUP = 10
GW = GROUP * H
GROUPS = N // GROUP
BATCH = 5
BIG = 1000.0
HALF = NT // 2


class Count:

    def __init__(self, sem):
        self.sem, self.n = sem, 0

    def add(self, ins):
        self.n += 1
        ins.then_inc(self.sem, 1)
        return self.n


class Chain:

    def __init__(self, eng, count):
        self.eng, self.count = eng, count

    def __call__(self, ins):
        self.eng.wait_ge(self.count.sem, self.count.add(ins))


def blocks(w):
    return w.rearrange("(b p) n -> p b n", p=P)


def build(nc, t):
    with ExitStack() as top:
        def sb(name, shape, dt=F32, scope=top):
            return scope.enter_context(nc.sbuf_tensor(name, shape, dt))

        def arena(name, nbytes, scope):
            base = -(-nc.sbuf_base // 32) * 32
            scope.enter_context(nc.sbuf_tensor(name, [P, nbytes // 4 + 8], F32))

            def place(tensor, shape, offset, dt=F32):
                size = mybir.dt.size(dt) * int(np.prod(shape[1:]))
                assert offset % 32 == 0 and offset + size <= nbytes, (tensor, offset, size)
                return nc.alloc_sbuf_tensor_at(tensor, shape, dt, offset=base + offset)
            return place

        def sem(name):
            return top.enter_context(nc.semaphore(name))

        bank = top.enter_context(nc.psum_tensor("bank", [P, 8, 512], F32))
        x_res = sb("x_res", [TP, NT, D])
        place_adj = arena("adj_room", 4 * NT * N, top)
        adj = place_adj("adj", [P, NT * N], 0)
        adj_t = adj[0:TP, :].rearrange("p (s n) -> p s n", s=NT)
        adj_12 = place_adj("adj_12", [P, NT * N], 0, F32R)[0:TP, :].rearrange("p (s n) -> p s n", s=NT)
        ident = sb("ident", [P, P])
        before = sb("before", [P, P])
        ones = sb("ones", [P, P])
        headmask = sb("headmask", [P, P])
        tokmask = sb("tokmask", [P, P])
        smallc = sb("smallc", [P, 256])
        select = sb("select", [2 * H, H, P], F32R)
        deg = sb("deg", [TP, NT])
        large_i = sb("large_i", [1, 1], I32)
        stats = sb("stats", [TP, NT, 6])
        moments = sb("moments", [TP, NT, 2])
        rstd, rs_var, rs_root, rs_tmp = (sb(n, [TP, NT]) for n in ("rstd", "rs_var", "rs_root", "rs_tmp"))

        s_x = [sem("x_loaded_0"), sem("x_loaded_1")]
        s_const, s_edges, s_zero, s_zfill = (sem(n) for n in ("const_loaded", "edges_loaded", "zero_set", "zero_filled"))
        s_kvw_in, s_w0, s_gate_w = sem("kv_weights_loaded"), sem("layer0_weights_loaded"), sem("gate_weights_loaded")
        s_normed, s_turned, s_evac = (sem(n) for n in ("normed", "turned", "columns_ready"))
        s_high, s_low = sem("high_parts_taken"), sem("low_parts_taken")
        s_bn, s_var, s_sqrt = sem("stats_ready"), sem("variance_ready"), sem("root_ready")
        dve_n, act_n, pool_n = Count(sem("dve_step")), Count(sem("act_step")), Count(sem("pool_step"))
        pe_n = Count(sem("pe_step"))

        slots_x = nc.dram_tensor("slots_x", (SLOTS * SLOT, D), F32, kind="Internal").ap()
        slots_y = nc.dram_tensor("slots_y", (SLOTS * SLOT, D), F32, kind="Internal").ap()

        def exact_counts(pe, large, products):
            with pe.If_eq(large.val, 0):
                products(adj_12, lambda a: a)
            with pe.If_eq(large.val, 1):
                products(adj_t, lambda a: a.bitcast(F32))

        def refine_rsqrt(chain, out, v, root, tmp):
            chain(nc.vector.reciprocal(out, root))
            chain(nc.vector.tensor_tensor(tmp, out, out, ALU.mult))
            chain(nc.vector.tensor_tensor(tmp, tmp, v, ALU.mult))
            chain(nc.vector.tensor_scalar(tmp, tmp, -0.5, 1.5, ALU.mult, ALU.add))
            chain(nc.vector.tensor_tensor(out, out, tmp, ALU.mult))

        def norm_stats(dve, which, i):
            nc.vector.bn_stats(stats[:, i], x_res[:, i]).then_inc(s_bn, 1)
            dve.wait_ge(s_bn, which * NT + i + 1)
            return nc.vector.bn_aggr(moments[:, i], stats[:, i])

        def norm_variance(c):
            tiles = slice(c * HALF, (c + 1) * HALF)
            nc.vector.tensor_scalar(rs_var[:, tiles], moments[:, tiles, 1], EPS_LN, None, ALU.add).then_inc(s_var, 1)

        def norm_root(act, which, c):
            tiles = slice(c * HALF, (c + 1) * HALF)
            act.wait_ge(s_var, 2 * which + c + 1)
            nc.scalar.activation(rs_root[:, tiles], rs_var[:, tiles], ACT.Sqrt).then_inc(s_sqrt, 1)

        def norm_apply(dve, chain, which, c, rows, parts=None):
            base, kept = which * NT, rows.shape[1]
            tiles = slice(c * HALF, (c + 1) * HALF)
            dve.wait_ge(s_sqrt, 2 * which + c + 1)
            refine_rsqrt(chain, rstd[:, tiles], rs_var[:, tiles], rs_root[:, tiles], rs_tmp[:, tiles])
            for i in range(c * HALF, (c + 1) * HALF):
                if i >= kept:
                    dve.wait_ge(s_turned, base + i - kept + 1)
                    if parts:
                        dve.wait_ge(s_high, base + i - kept + 1)
                nc.vector.tensor_scalar(rows[:, i % kept], x_res[:, i], moments[:, i, 0:1], rstd[:, i:i + 1],
                                        ALU.subtract, ALU.mult).then_inc(s_normed, 1)
                if parts:
                    dve.wait_ge(s_high, base + i + 1)
                    nc.vector.tensor_tensor(parts[1][0:TP, i], rows[:, i % kept], parts[0][0:TP, i].bitcast(F32),
                                            ALU.subtract).then_inc(s_low, 1)

        def norm_turn(pe, which, i, rows):
            base, kept = which * NT, rows.shape[1]
            pe.wait_ge(s_normed, base + i + 1)
            if i >= 2:
                pe.wait_ge(s_evac, base + i - 1)
            for b in range(KB):
                ins = nc.tensor.transpose(bank[:, i % 2, b * P:b * P + TP], rows[:, i % kept, b * P:(b + 1) * P],
                                          ident[0:TP, 0:TP])
            ins.then_inc(s_turned, 1)

        def norm_columns(act, which, i, rows, cols, parts=None):
            base, kept = which * NT, rows.shape[1]
            if parts:
                act.wait_ge(s_normed, base + i + 1)
                nc.scalar.copy(parts[0][0:TP, i], rows[:, i % kept]).then_inc(s_high, 1)
            act.wait_ge(s_turned, base + i + 1)
            nc.scalar.copy(cols[:, :, i * TP:(i + 1) * TP],
                           bank[:, i % 2, :].rearrange("p (b n) -> p b n", b=KB)[:, :, 0:TP]).then_inc(s_evac, 1)

        def layernorm(block, which, rows, cols, parts=None, use_tile=None):
            @block.vector
            def _(dve):
                chain = Chain(dve, dve_n)
                for c in range(2):
                    for i in range(c * HALF, (c + 1) * HALF):
                        if which == 0:
                            dve.wait_ge(s_x[c], 16)
                        ins = norm_stats(dve, which, i)
                    chain(ins)
                    norm_variance(c)
                    norm_apply(dve, chain, which, c, rows, parts)

            @block.tensor
            def _(pe):
                if which == 0:
                    pe.wait_ge(s_const, 16 * N_CONST)
                for i in range(NT + 1):
                    if i < NT:
                        norm_turn(pe, which, i, rows)
                    if use_tile and i >= 1:
                        pe.wait_ge(s_evac, which * NT + i)
                        use_tile(pe, i - 1)

            @block.scalar
            def _(act):
                for c in range(2):
                    norm_root(act, which, c)
                    for i in range(c * HALF, (c + 1) * HALF):
                        norm_columns(act, which, i, rows, cols, parts)

        N_CONST = 8
        layer0 = top.enter_context(ExitStack())
        K = 1024
        place = arena("layer0_room", 124 * K, layer0)
        xn_c = place("xn_c0", [P, KB, N], 0)
        xn_hi = place("xn_hi", [P, NT, D], 20 * K, F32R)
        xn_lo = place("xn_lo", [P, NT, D], 40 * K, F32R)
        q_c = place("q_c", [P, KB, N], 40 * K)
        w_kv = place("w_kv", [P, KB, 2 * D], 60 * K)
        kv_r = place("kv_r", [TP, 2, 2 * D], 76 * K)
        agg = place("agg", [P, KB, N], 60 * K)
        w_q, w_l, w_r, w_proj = (place(n, [P, KB, D], (84 + 8 * i) * K) for i, n in enumerate(("w_q", "w_l", "w_r", "w_proj")))
        b_l, b_proj = (place(n, [TP, D], (116 + 2 * i) * K) for i, n in enumerate(("b_l", "b_proj")))
        qtmp = place("qtmp", [P, 2, D], 120 * K)
        kv_h = place("kv_h", [P, KB, P], 84 * K)
        zi_hi, zi_lo = (place(n, [H, N], (20 + 5 * i) * K, F32R) for i, n in enumerate(("zi_hi", "zi_lo")))

        with ExitStack() as scope:
            room_used = [0]

            def scratch(name, shape, dt=F32):
                room_used[0] = -(-room_used[0] // 32) * 32
                size = mybir.dt.size(dt) * int(np.prod(shape[1:]))
                at, room_used[0] = room_used[0], room_used[0] + size
                assert room_used[0] <= 36 * K
                return place(name, shape, 84 * K + at, dt)
            zeros = scratch("zeros", [P, 4 * D])
            iota = scratch("iota", [P, N], F16)
            select_f = place("select_f", [2 * H, H * P], 76 * K)
            zeros16 = scratch("zeros16", [P, 512], BF16)
            ones16 = scratch("ones16", [P, 2], BF16)
            edge_i = scratch("edge_i", [STEPS, 2, QT * TP], I32)
            edge_f = scratch("edge_f", [STEPS, 2, QT * TP])
            edge_c = scratch("edge_c", [TP, 2, QT, 2 * STEPS])
            span = scratch("span", [STEPS, 2])
            span_w = scratch("span_w", [STEPS, 2, NT])
            fl1, fl2, key = (scratch(n, [NT, STEPS]) for n in ("fl1", "fl2", "key"))
            plan = scratch("plan", [NT, 4])
            plan_i = scratch("plan_i", [NT, 4], I32)
            onehot_src = scratch("onehot_src", [TP, QT, N], BF16)
            onehot_dst = scratch("onehot_dst", [TP, QT, TP], BF16)
            dmax = scratch("dmax", [TP, 1])
            s_hot = [sem(f"onehot_ready_{j}") for j in range(QT)]
            s_used = [sem(f"onehot_used_{j}") for j in range(QT)]
            s_adj = sem("window_copied")
            s_deg, s_large, s_all = sem("degree_greatest"), sem("large_known"), sem("degrees_turned")
            s_plan, s_edge_f = sem("plan_ready"), sem("edges_as_floats")
            s_span = sem("span_ready")
            s_spanp = sem("span_turned")

            with nc.Block() as block:
                layernorm(block, 0, qtmp[0:TP], xn_c, (xn_hi, xn_lo))

                @block.sync
                def _(sp):
                    for c in range(2):
                        sp.dma_start(x_res[:, c * HALF:(c + 1) * HALF],
                                     t["x"].rearrange("(t p) d -> p t d", p=TP)[:, c * HALF:(c + 1) * HALF]).then_inc(s_x[c], 16)
                    for n, (dst, src) in enumerate([(ident, t["c_ident"]), (before, t["c_before"]), (ones, t["c_ones"]),
                                                    (headmask, t["c_headmask"]), (tokmask, t["c_tokmask"]),
                                                    (iota, t["c_iota"]), (smallc, t["c_small"]),
                                                    (select_f, t["c_select"])]):
                        sp.dma_start(dst[:], src).then_inc(s_const, 16)
                    for n, name in enumerate(("src", "dst")):
                        sp.dma_start(edge_i[:, n], t[name].rearrange("(u e) -> u e", e=QT * TP)).then_inc(s_edges, 16)
                    sp.dma_start(w_kv[:], blocks(t["L0_mix_w_qkv"])[:, :, D:3 * D]).then_inc(s_kvw_in, 16)
                    sp.wait_ge(s_zero, 1)
                    fill = slots_x[0:SLOTS * SLOT].rearrange("(p a) d -> p (a d)", p=P)
                    width = 4 * D
                    for c in range(SLOTS // 4):
                        sp.dma_start(fill[:, c * width:(c + 1) * width], zeros[:]).then_inc(s_zfill, 16)
                    spare = slots_y[SLOTS_SURE * SLOT:].rearrange("(p a) d -> p (a d)", p=P)
                    for c in range((SLOTS - SLOTS_SURE) // 4):
                        sp.dma_start(spare[:, c * width:(c + 1) * width], zeros[:]).then_inc(s_zfill, 16)

                @block.gpsimd
                def _(pool):
                    nc.gpsimd.memset(zeros[:], 0.0).then_inc(s_zero, 1)

            def window(eng, w):
                return (eng.value_load(plan_i[w:w + 1, 0:1], min_val=0, max_val=STEPS - 1),
                        eng.value_load(plan_i[w:w + 1, 2:3], min_val=1, max_val=STEPS),
                        eng.value_load(plan_i[w:w + 1, 3:4], min_val=0, max_val=NT * STEPS))

            with nc.Block() as block:
                @block.sync
                def _(sp):
                    sp.wait_ge(s_zfill, 16 * ((2 * SLOTS - SLOTS_SURE) // 4))

                @block.vector
                def _(dve):
                    chain = Chain(dve, dve_n)
                    nc.vector.tensor_copy(select[:], select_f[:].rearrange("k (h p) -> k h p", h=H))
                    nc.vector.memset(zeros16[:], 0.0)
                    chain(nc.vector.memset(ones16[:], 1.0))
                    dve.wait_ge(s_edges, 32)
                    nc.vector.tensor_copy(edge_f[:], edge_i[:]).then_inc(s_edge_f, 1)
                    dve.wait_ge(s_edge_f, 1)
                    chain(nc.vector.tensor_reduce(span[:, 0:1], edge_f[:, 1], AX.X, ALU.min))
                    chain(nc.vector.tensor_reduce(span[:, 1:2], edge_f[:, 1], AX.X, ALU.max))
                    for m in range(2):
                        nc.vector.tensor_scalar(span_w[:, m], ones[0:STEPS, 0:NT], span[:, m:m + 1], None,
                                                ALU.mult).then_inc(s_span, 1)
                    dve.wait_ge(s_spanp, 1)
                    spans = bank[0:NT, 1, :]
                    w_first, w_last = smallc[0:NT, 0:1], smallc[0:NT, 1:2]
                    step_no = smallc[0:NT, 8:8 + STEPS]
                    chain(nc.vector.tensor_scalar(fl1[:], spans[:, P:P + STEPS], w_first, None, ALU.is_ge))
                    chain(nc.vector.scalar_tensor_tensor(fl2[:], spans[:, 0:STEPS], w_last, fl1[:], ALU.is_le, ALU.mult))
                    chain(nc.vector.scalar_tensor_tensor(key[:], step_no, -BIG, fl2[:], ALU.add, ALU.mult))
                    chain(nc.vector.tensor_reduce(plan[:, 0:1], key[:], AX.X, ALU.min))
                    chain(nc.vector.scalar_tensor_tensor(key[:], step_no, 1.0, fl2[:], ALU.add, ALU.mult))
                    chain(nc.vector.tensor_reduce(plan[:, 1:2], key[:], AX.X, ALU.max))
                    chain(nc.vector.tensor_scalar(plan[:, 0:1], plan[:, 0:1], BIG, STEPS - 1.0, ALU.add, ALU.min))
                    chain(nc.vector.tensor_tensor(plan[:, 2:3], plan[:, 1:2], plan[:, 0:1], ALU.subtract))
                    nc.vector.tensor_scalar(plan[:, 2:3], plan[:, 2:3], 1.0, None, ALU.max).then_inc(s_span, 1)
                    dve.wait_ge(s_spanp, 2)
                    chain(nc.vector.tensor_copy(plan[:, 3:4], bank[0:NT, 2, 0:1]))
                    for m in range(2):
                        chain(nc.vector.tensor_copy(edge_c[:, m, :, 0:STEPS], bank[0:TP, 0, :].rearrange(
                            "p (m j u) -> p m j u", m=2, j=QT)[:, m, :, 0:STEPS]))
                    nc.vector.tensor_copy(plan_i[:], plan[:]).then_inc(s_plan, 1)
                    dve.wait_ge(s_plan, 1)
                    for w in range(NT):
                        first, count, base = window(dve, w)
                        with dve.Fori(0, count) as i:
                            for j in range(QT):
                                dve.wait_ge(s_used[j], base + i + 1)
                                nc.vector.tensor_scalar(onehot_src[:, j], iota[0:TP, :],
                                                        edge_c[:, 0, j, bass.ds(first + i, 1)], None,
                                                        ALU.is_equal).then_inc(s_hot[j], 1)
                                nc.vector.tensor_scalar(onehot_dst[:, j], iota[0:TP, w * TP:(w + 1) * TP],
                                                        edge_c[:, 1, j, bass.ds(first + i, 1)], None,
                                                        ALU.is_equal).then_inc(s_hot[j], 1)
                    dve.wait_ge(s_adj, NT)
                    nc.vector.tensor_reduce(dmax[:], deg[:], AX.X, ALU.max).then_inc(s_deg, 1)
                    dve.wait_ge(s_all, 1)
                    nc.vector.tensor_reduce(dmax[0:1], bank[0:1, 6, 0:TP], AX.X, ALU.max).then_inc(s_deg, 1)
                    dve.wait_ge(s_deg, 2)
                    nc.vector.tensor_scalar(large_i[:], dmax[0:1], 4095.0, None, ALU.is_gt).then_inc(s_large, 1)

                @block.tensor
                def _(pe):
                    for j in range(QT):
                        pe.sem_inc(s_used[j], 1)
                    pe.wait_ge(s_edge_f, 1)
                    for m in range(2):
                        for j in range(QT):
                            nc.tensor.transpose(bank[0:TP, 0, (QT * m + j) * 64:(QT * m + j) * 64 + STEPS],
                                                edge_f[:, m, j * TP:(j + 1) * TP], ident[0:STEPS, 0:STEPS])
                    pe.wait_ge(s_span, 2)
                    for m in range(2):
                        ins = nc.tensor.matmul(bank[0:NT, 1, m * P:m * P + STEPS], span_w[:, m],
                                               ident[0:STEPS, 0:STEPS], start=True, stop=True)
                    ins.then_inc(s_spanp, 1)
                    pe.wait_ge(s_span, 3)
                    nc.tensor.matmul(bank[0:NT, 2, 0:1], before[0:NT, 0:NT], plan[:, 2:3],
                                     start=True, stop=True).then_inc(s_spanp, 1)
                    pe.wait_ge(s_plan, 1)
                    for w in range(NT):
                        _, count, base = window(pe, w)
                        bk = 3 * (w % 2)
                        if w >= 2:
                            pe.wait_ge(s_adj, w - 1)
                        for b in range(3):
                            nc.tensor.matmul(bank[0:TP, bk + b, :], zeros16[0:TP, 0:TP], zeros16[0:TP, :],
                                             start=True, stop=False, skip_group_check=True)
                        with pe.Fori(0, count) as i:
                            for j in range(QT):
                                pe.wait_ge(s_hot[j], 2 * (base + i) + 2)
                                nc.tensor.matmul(bank[0:TP, bk + 2, 2 * P - 1:2 * P], onehot_dst[:, j], ones16[0:TP, 0:1],
                                                 start=False, stop=False, skip_group_check=True)
                                for s in range(NT):
                                    ins = nc.tensor.matmul(
                                        bank[0:TP, bk + s // 4, (s % 4) * P:(s % 4) * P + TP],
                                        onehot_src[:, j, s * TP:(s + 1) * TP], onehot_dst[:, j],
                                        start=False, stop=False, skip_group_check=True)
                                ins.then_inc(s_used[j], 1)
                    pe.wait_ge(s_deg, 1)
                    nc.tensor.transpose(bank[0:1, 6, 0:TP], dmax[:], ident[0:TP, 0:TP]).then_inc(s_all, 1)

                @block.scalar
                def _(act):
                    act.wait_ge(s_plan, 1)
                    for w in range(NT):
                        _, count, base = window(act, w)
                        bk = 3 * (w % 2)
                        act.wait_ge(s_used[QT - 1], base + count + 1)
                        win = bank[0:TP, bk:bk + 3, :].rearrange("p b (r n) -> p (b r) n", n=P)
                        nc.scalar.copy(adj_t[:, :, w * TP:(w + 1) * TP], win[:, 0:NT, 0:TP])
                        nc.scalar.copy(deg[:, w:w + 1], win[:, NT - 1, P - 1:P]).then_inc(s_adj, 1)

        with ExitStack() as scope:
            ksum = sb("ksum", [P, KB], scope=scope)
            ksum_z = sb("ksum_z", [P, KB, H], scope=scope)
            zrow = sb("zrow", [TP, NT * H], scope=scope)
            kvw = w_proj
            rdeg = sb("rdeg", [TP, NT], scope=scope)
            s_q, s_kv, s_min, s_exp, s_qf = (sem(n) for n in ("q_ready", "kv_ready", "min_ready", "exp_ready", "q_feature"))
            s_kf, s_vc, s_acc, s_agg, s_aggc, s_z, s_qz = (sem(n) for n in (
                "k_feature", "v_copied", "kv_summed", "agg_ready", "agg_copied", "z_spread", "q_scaled"))
            s_zrow, s_zinv, s_zturn, s_zhi, s_zlo = (sem(n) for n in ("z_ready", "z_inverse", "z_turned", "z_high", "z_low"))
            s_ksum, s_adj_12 = sem("k_sum_placed"), sem("counts_rewritten")
            s_kvh, s_kvw, s_kvwc, s_out, s_outc = (sem(n) for n in ("kv_masked", "kvw_ready", "kvw_copied", "out_ready", "out_used"))
            s_bp = sem("bias_added")
            NQ = KB * len(CHUNKS)

            with nc.Block() as block:
                @block.sync
                def _(sp):
                    sp.dma_start(w_q[:], blocks(t["L0_mix_w_qkv"])[:, :, 0:D]).then_inc(s_w0, 16)
                    for dst, name in ((w_l, "L0_gnn_W_l"), (w_r, "L0_gnn_W_r"), (w_proj, "L0_mix_w_proj")):
                        sp.dma_start(dst[:], blocks(t[name])).then_inc(s_w0, 16)
                    for dst, name in ((b_l, "L0_gnn_b_l"), (b_proj, "L0_mix_b_proj")):
                        sp.dma_start(dst[:], t[name].partition_broadcast(TP)).then_inc(s_w0, 16)

                @block.gpsimd
                def _(pool):
                    large = pool.value_load(large_i[0:1, 0:1], min_val=0, max_val=1)
                    with pool.If_eq(large.val, 0):
                        for s in range(NT):
                            nc.gpsimd.tensor_copy(adj_12[:, s], adj_t[:, s])
                    pool.engine_nop().then_inc(s_adj_12, 1)
                    pool.wait_ge(s_w0, 96)
                    for i in range(NT):
                        nc.gpsimd.tensor_tensor(x_res[:, i], x_res[:, i], b_proj[:], ALU.add).then_inc(s_bp, 1)

                @block.tensor
                def _(pe):
                    pe.wait_ge(s_kvw_in, 16)
                    def kv_sums(i):
                        pe.wait_ge(s_kf, i + 1)
                        pe.wait_ge(s_vc, i + 1)
                        k, v = kv_r[:, i % 2, 0:D], kv_r[:, i % 2, D:2 * D]
                        for m in range(KB):
                            nc.tensor.matmul(bank[:, 6, m * P:(m + 1) * P], v[:, m * P:(m + 1) * P], k[:, m * P:(m + 1) * P],
                                             start=i == 0 and m == 0, stop=i == NT - 1, skip_group_check=True)
                        for m in range(KB):
                            ins = nc.tensor.matmul(bank[:, 7, m:m + 1], k[:, m * P:(m + 1) * P], ones[0:TP, 0:1],
                                                   start=i == 0 and m == 0, stop=i == NT - 1, skip_group_check=True)
                        ins.then_inc(s_acc, 1)

                    for i in range(NT):
                        if i >= 2:
                            pe.wait_ge(s_kf, i - 1)
                            pe.wait_ge(s_vc, i - 1)
                        for g in range(2):
                            for b in range(KB):
                                ins = nc.tensor.matmul(bank[0:TP, 2 + 2 * (i % 2) + g, :], xn_c[:, b, i * TP:(i + 1) * TP],
                                                       w_kv[:, b, g * D:(g + 1) * D], start=b == 0, stop=b == KB - 1)
                            ins.then_inc(s_kv, 1)
                        if i >= 1:
                            kv_sums(i - 1)
                    kv_sums(NT - 1)
                    pe.wait_ge(s_w0, 96)
                    pe.wait_ge(s_adj_12, 1)
                    large = pe.value_load(large_i[0:1, 0:1], min_val=0, max_val=1)
                    n = 0
                    for m in range(KB):
                        for a, w in CHUNKS:
                            if n >= 2:
                                pe.wait_ge(s_aggc, n - 1)
                            feats = slice(m * P, (m + 1) * P)

                            def neighbours(adjacency, cast):
                                for s in range(NT):
                                    for k, part in enumerate((xn_hi, xn_lo)):
                                        ins = nc.tensor.matmul(bank[:, n % 2, 0:w], cast(part[0:TP, s, feats]), adjacency[:, s, a:a + w],
                                                               start=s == 0 and k == 0, stop=s == NT - 1 and k == 1)
                                ins.then_inc(s_agg, 1)
                            exact_counts(pe, large, neighbours)
                            n += 1
                    n = 0
                    for m in range(KB):
                        for a, w in CHUNKS:
                            if n >= 2:
                                pe.wait_ge(s_qf, n - 1)
                            else:
                                pe.wait_ge(s_aggc, NQ - 1 + n)
                            for b in range(KB):
                                ins = nc.tensor.matmul(bank[:, n % 2, 0:w], w_q[:, b, m * P:(m + 1) * P], xn_c[:, b, a:a + w],
                                                       start=b == 0, stop=b == KB - 1)
                            ins.then_inc(s_q, 1)
                            n += 1

                    pe.wait_ge(s_ksum, 1)
                    pe.wait_ge(s_qf, NQ)
                    for i in range(NT):
                        for m in range(KB):
                            ins = nc.tensor.matmul(bank[0:TP, 2, i * H:(i + 1) * H], q_c[:, m, i * TP:(i + 1) * TP], ksum_z[:, m],
                                                   start=m == 0, stop=m == KB - 1)
                    ins.then_inc(s_zrow, 1)
                    pe.wait_ge(s_kvh, 1)
                    for m in range(KB):
                        if m >= 2:
                            pe.wait_ge(s_kvwc, m - 1)
                        nc.tensor.matmul(bank[:, 3 + m % 2, :], kv_h[:, m], w_proj[:, m], start=True, stop=True).then_inc(s_kvw, 1)
                    pe.wait_ge(s_zinv, 1)
                    for c, (a, w) in enumerate(CHUNKS):
                        for i in range(a // TP, (a + w) // TP):
                            ins = nc.tensor.transpose(bank[0:H, 5 + c, i * TP - a:(i + 1) * TP - a], zrow[:, i * H:(i + 1) * H],
                                                      ident[0:TP, 0:TP])
                        ins.then_inc(s_zturn, 1)

                    def tile_products(i, parts):
                        o = 3 * (i % 2)
                        tok = slice(i * TP, (i + 1) * TP)
                        for g, left, right in parts:
                            for b in range(KB):
                                ins = nc.tensor.matmul(bank[0:TP, o + g, :], left[:, b, tok], right[:, b],
                                                       start=b == 0, stop=b == KB - 1)
                        return ins
                    graph_parts, attention_part = ((0, agg, w_l), (1, xn_c, w_r)), ((2, q_c, kvw),)
                    pe.wait_ge(s_aggc, NQ)
                    tile_products(0, graph_parts)
                    pe.wait_ge(s_zlo, len(CHUNKS))
                    n = 0
                    for c, (a, w) in enumerate(CHUNKS):
                        for m in range(KB):
                            if n >= 2:
                                pe.wait_ge(s_qz, n - 1)
                            for k, part in enumerate((zi_hi, zi_lo)):
                                ins = nc.tensor.matmul(bank[:, 6 + n % 2, 0:w], select[0:H, m], part[:, a:a + w],
                                                       start=k == 0, stop=k == 1)
                            ins.then_inc(s_z, 1)
                            n += 1
                        if c == 0:
                            pe.wait_ge(s_kvwc, KB)
                            tile_products(1, graph_parts)
                    for i in range(NT):
                        if i >= 2:
                            pe.wait_ge(s_outc, i - 1)
                            tile_products(i, graph_parts)
                        pe.wait_ge(s_qz, KB * min(len(CHUNKS), i * TP // CHUNKS[0][1] + 1))
                        tile_products(i, attention_part).then_inc(s_out, 1)

                @block.vector
                def _(dve):
                    chain = Chain(dve, dve_n)
                    chain(nc.vector.tensor_scalar(rdeg[:], deg[:], 1.0, None, ALU.max))
                    nc.vector.reciprocal(rdeg[:], rdeg[:]).then_inc(dve_n.sem, 1)
                    dve_n.n += 1
                    for i in range(NT):
                        dve.wait_ge(s_kv, 2 * i + 1)
                        if i >= 2:
                            dve.wait_ge(s_acc, i - 1)
                        k = kv_r[:, i % 2, 0:D]
                        kp = bank[0:TP, 2 + 2 * (i % 2), :]
                        nc.vector.tensor_scalar(qtmp[0:TP, i % 2, :], kp, 0.0, None, ALU.min).then_inc(s_min, 1)
                        dve.wait_ge(s_exp, i + 1)
                        nc.vector.scalar_tensor_tensor(k, kp, 0.0, qtmp[0:TP, i % 2, :], ALU.max, ALU.add).then_inc(s_kf, 1)
                    chain(nc.vector.memset(ksum_z[:], 0.0))
                    dve.wait_ge(s_acc, NT)
                    chain(nc.vector.tensor_copy(ksum[:], bank[:, 7, 0:KB]))
                    for m in range(KB):
                        ins = nc.vector.tensor_scalar(ksum_z[:, m, 2 * m:2 * m + 2], headmask[:, 0:P:HD], ksum[:, m:m + 1], None,
                                                      ALU.mult)
                    ins.then_inc(s_ksum, 1)
                    n = 0
                    for m in range(KB):
                        for a, w in CHUNKS:
                            dve.wait_ge(s_q, n + 1)
                            nc.vector.tensor_scalar(qtmp[:, n % 2, 0:w], bank[:, n % 2, 0:w], 0.0, None, ALU.min).then_inc(s_min, 1)
                            dve.wait_ge(s_exp, NT + n + 1)
                            nc.vector.scalar_tensor_tensor(q_c[:, m, a:a + w], bank[:, n % 2, 0:w], 0.0, qtmp[:, n % 2, 0:w],
                                                           ALU.max, ALU.add).then_inc(s_qf, 1)
                            n += 1
                    for m in range(KB):
                        ins = nc.vector.tensor_tensor(kv_h[:, m], bank[:, 6, m * P:(m + 1) * P], headmask[:], ALU.mult)
                    ins.then_inc(s_kvh, 1)
                    dve.wait_ge(s_zrow, 1)
                    chain(nc.vector.tensor_scalar(zrow[:], bank[0:TP, 2, 0:NT * H], EPS_ATT, None, ALU.add))
                    nc.vector.reciprocal(zrow[:], zrow[:]).then_inc(s_zinv, 1)
                    for c, (a, w) in enumerate(CHUNKS):
                        dve.wait_ge(s_zhi, c + 1)
                        nc.vector.tensor_tensor(zi_lo[:, a:a + w], bank[0:H, 5 + c, 0:w], zi_hi[:, a:a + w].bitcast(F32),
                                                ALU.subtract).then_inc(s_zlo, 1)
                    dve.wait_ge(s_qf, NQ)
                    n = 0
                    for a, w in CHUNKS:
                        for m in range(KB):
                            dve.wait_ge(s_z, n + 1)
                            nc.vector.tensor_tensor(q_c[:, m, a:a + w], q_c[:, m, a:a + w], bank[:, 6 + n % 2, 0:w],
                                                    ALU.mult).then_inc(s_qz, 1)
                            n += 1
                    for i in range(NT):
                        o = 3 * (i % 2)
                        dve.wait_ge(s_out, i + 1)
                        dve.wait_ge(s_bp, i + 1)
                        y = qtmp[0:TP, i % 2]
                        chain(nc.vector.tensor_tensor(y, bank[0:TP, o + 1, :], b_l[:], ALU.add))
                        chain(nc.vector.scalar_tensor_tensor(y, bank[0:TP, o, :], rdeg[:, i:i + 1], y, ALU.mult, ALU.add))
                        chain(nc.vector.scalar_tensor_tensor(x_res[:, i], y, 0.0, x_res[:, i], ALU.max, ALU.add))
                        nc.vector.tensor_tensor(x_res[:, i], x_res[:, i], bank[0:TP, o + 2, :], ALU.add).then_inc(s_outc, 1)
                    dve.wait_ge(s_outc, NT)

                @block.scalar
                def _(act):
                    for i in range(NT):
                        act.wait_ge(s_min, i + 1)
                        nc.scalar.activation(qtmp[0:TP, i % 2, :], qtmp[0:TP, i % 2, :], ACT.Exp).then_inc(s_exp, 1)
                        act.wait_ge(s_kv, 2 * i + 2)
                        if i >= 2:
                            act.wait_ge(s_acc, i - 1)
                        nc.scalar.copy(kv_r[:, i % 2, D:2 * D], bank[0:TP, 3 + 2 * (i % 2), :]).then_inc(s_vc, 1)
                    n = 0
                    for m in range(KB):
                        for a, w in CHUNKS:
                            act.wait_ge(s_agg, n + 1)
                            nc.scalar.copy(agg[:, m, a:a + w], bank[:, n % 2, 0:w]).then_inc(s_aggc, 1)
                            n += 1
                    n = 0
                    for m in range(KB):
                        for a, w in CHUNKS:
                            act.wait_ge(s_min, NT + n + 1)
                            nc.scalar.activation(qtmp[:, n % 2, 0:w], qtmp[:, n % 2, 0:w], ACT.Exp).then_inc(s_exp, 1)
                            n += 1
                    for m in range(KB):
                        act.wait_ge(s_kvw, m + 1)
                        nc.scalar.copy(kvw[:, m], bank[:, 3 + m % 2, :]).then_inc(s_kvwc, 1)
                    for c, (a, w) in enumerate(CHUNKS):
                        act.wait_ge(s_zturn, c + 1)
                        nc.scalar.copy(zi_hi[:, a:a + w], bank[0:H, 5 + c, 0:w]).then_inc(s_zhi, 1)
        layer0.close()

        choice = sb("choice", [TP, 2, NT])
        place_i = sb("place_i", [TP, 2, NT], U32)
        with ExitStack() as moe:
            table_i = sb("table_i", [1, 2, E0 + 1], I32, scope=moe)
            w1_sb = sb("w1_sb", [P, 2, KB, F0], scope=moe)
            place_w2 = arena("w2_room", 4 * 2 * FB * D, moe)
            w2_sb = place_w2("w2_sb", [P, 2, FB, D], 0)
            b1_sb = sb("b1_sb", [P, 2, FB], scope=moe)
            b2_sb = sb("b2_sb", [P, 2, D], scope=moe)
            s_w = [sem(f"expert_loaded_{e}") for e in range(E0)]
            s_hd, s_gelu, s_yd, s_ye, s_yst, s_xl, s_xt, s_xr = (sem(n) for n in (
                "hidden_ready", "gelu_ready", "y_ready", "y_added", "y_stored", "slot_loaded", "slot_turned", "slot_columns"))

            def read_table(eng):
                eng.wait_ge(s_table, 1)
                return [(eng.value_load(table_i[0:1, 0, e:e + 1], min_val=1, max_val=NT),
                         eng.value_load(table_i[0:1, 1, e:e + 1], min_val=0, max_val=SLOTS - 1)) for e in range(E0)]

            tables = {}
            s_table = sem("table_ready")

            def load_expert(eng, e):
                q = e % 2
                eng.dma_start(w1_sb[:, q], blocks(t["L0_ffn_w1"][e])).then_inc(s_w[e], 16)
                eng.dma_start(w2_sb[:, q], blocks(t["L0_ffn_w2"][e])).then_inc(s_w[e], 16)
                eng.dma_start(b1_sb[:, q], t["L0_ffn_b1"][e]).then_inc(s_w[e], 16)
                eng.dma_start(b2_sb[:, q], t["L0_ffn_b2"][e].partition_broadcast(P)).then_inc(s_w[e], 16)

            with ExitStack() as scope:
                gate_w = sb("gate_w", [P, KB, E0], scope=scope)
                gate_b = sb("gate_b", [TP, E0], scope=scope)
                pr, ex, oh1, oh2, ky, p2, m01, rank = (sb(n, [TP, NT, E0], scope=scope) for n in (
                    "probs", "eq", "first_hot", "second_hot", "keys", "probs_2", "chosen", "rank"))
                mx, sm, r1, r2 = (sb(n, [TP, NT], scope=scope) for n in ("mx", "sm", "r1", "r2"))
                tot = sb("tot", [TP, NT + 1, E0], scope=scope)
                gt = sb("gt", [TP, E0, NT], scope=scope)
                tbl = sb("tbl", [TP, 2, E0 + 1], scope=scope)
                place = sb("place", [TP, 2, NT], scope=scope)
                s_lg, s_oh, s_pre, s_pl, s_sc = (sem(n) for n in ("logits_ready", "chosen_ready", "counts_ready", "places_ready", "scattered"))

                xn_rows = sb("xn_rows", [TP, NT, D], scope=scope)
                xn_c = sb("xn_c1", [P, KB, N], scope=scope)
                logits_c = sb("logits_c", [E0, N], scope=scope)
                s_lgc, s_lgs = sem("logit_columns"), sem("logit_columns_kept")

                def gate_logits(pe, i):
                    for c, (a, w) in enumerate(CHUNKS):
                        if (i + 1) * TP == a + w:
                            if c == 0:
                                pe.wait_ge(s_gate_w, 32)
                            for b in range(KB):
                                ins = nc.tensor.matmul(bank[0:E0, 3 + c, 0:w], gate_w[:, b], xn_c[:, b, a:a + w],
                                                       start=b == 0, stop=b == KB - 1)
                            ins.then_inc(s_lgc, 1)

                with nc.Block() as block:
                    layernorm(block, 1, xn_rows, xn_c, use_tile=gate_logits)

                    @block.sync
                    def _(sp):
                        sp.dma_start(gate_w[:], blocks(t["L0_ffn_gate_w"])).then_inc(s_gate_w, 16)
                        sp.dma_start(gate_b[:], t["L0_ffn_gate_b"].partition_broadcast(TP)).then_inc(s_gate_w, 16)
                        load_expert(sp, 0)
                        load_expert(sp, 1)

                with nc.Block() as block:
                    @block.sync
                    def _(sp):
                        tables["sp"] = read_table(sp)

                    @block.tensor
                    def _(pe):
                        for c, (a, w) in enumerate(CHUNKS):
                            pe.wait_ge(s_lgs, c + 1)
                            for i in range(a // TP, (a + w) // TP):
                                ins = nc.tensor.transpose(bank[0:TP, 6, i * E0:(i + 1) * E0], logits_c[:, i * TP:(i + 1) * TP],
                                                          ident[0:E0, 0:E0])
                        ins.then_inc(s_lg, 1)
                        pe.wait_ge(s_oh, 2)
                        hot = m01[:].rearrange("p t e -> p (t e)")
                        nc.tensor.matmul(bank[0:TP, 1, 0:NT * E0], before[0:TP, 0:TP], hot, start=True, stop=True)
                        nc.tensor.matmul(bank[0:TP, 2, 0:NT * E0], ones[0:TP, 0:TP], hot, start=True, stop=True).then_inc(s_pre, 1)
                        tables["pe"] = read_table(pe)

                    @block.vector
                    def _(dve):
                        chain = Chain(dve, dve_n)
                        V = nc.vector
                        full = [TP, NT, E0]

                        def over_e(a):
                            return a.unsqueeze(2).to_broadcast(full)

                        def over_t(a):
                            return a.unsqueeze(1).to_broadcast(full)
                        iota_e = over_t(smallc[0:TP, 128:128 + E0])
                        for c, (a, w) in enumerate(CHUNKS):
                            dve.wait_ge(s_lgc, c + 1)
                            nc.vector.tensor_copy(logits_c[:, a:a + w], bank[0:E0, 3 + c, 0:w]).then_inc(s_lgs, 1)
                        dve.wait_ge(s_gate_w, 32)
                        dve.wait_ge(s_lg, 1)
                        lg = bank[0:TP, 6, 0:NT * E0].rearrange("p (t e) -> p t e", e=E0)
                        chain(V.tensor_tensor(pr[:], lg, over_t(gate_b[:]), ALU.add))
                        chain(V.tensor_reduce(mx[:], pr[:], AX.X, ALU.max))
                        V.tensor_tensor(pr[:], pr[:], over_e(mx[:]), ALU.subtract).then_inc(s_oh, 1)
                        dve.wait_ge(act_n.sem, act_n.n + 1)
                        chain(V.tensor_reduce(sm[:], pr[:], AX.X, ALU.add))
                        chain(V.reciprocal(sm[:], sm[:]))
                        chain(V.tensor_tensor(pr[:], pr[:], over_e(sm[:]), ALU.mult))

                        def pick(probs, best, hot):
                            chain(V.tensor_reduce(best, probs, AX.X, ALU.max))
                            chain(V.tensor_tensor(ex[:], probs, over_e(best), ALU.is_equal))
                            chain(V.scalar_tensor_tensor(ky[:], ex[:], -float(E0), iota_e, ALU.mult, ALU.add))
                            chain(V.tensor_reduce(mx[:], ky[:], AX.X, ALU.min))
                            chain(V.tensor_tensor(hot, ky[:], over_e(mx[:]), ALU.is_equal))
                        pick(pr[:], r1[:], oh1[:])
                        chain(V.scalar_tensor_tensor(p2[:], oh1[:], -2.0, pr[:], ALU.mult, ALU.add))
                        pick(p2[:], r2[:], oh2[:])
                        V.tensor_tensor(m01[:], oh1[:], oh2[:], ALU.add).then_inc(s_oh, 1)
                        chain(V.tensor_tensor(sm[:], r1[:], r2[:], ALU.add))
                        chain(V.reciprocal(sm[:], sm[:]))
                        chain(V.tensor_tensor(choice[:, 0], r1[:], sm[:], ALU.mult))
                        chain(V.tensor_tensor(choice[:, 1], r2[:], sm[:], ALU.mult))
                        chain(V.memset(tot[:, 0], 0.0))
                        dve.wait_ge(s_pre, 1)
                        for i in range(NT):
                            chain(V.tensor_tensor(tot[:, i + 1], tot[:, i], bank[0:TP, 2, i * E0:(i + 1) * E0], ALU.add))
                        steps = smallc[0:TP, 144:144 + NT].unsqueeze(1).to_broadcast([TP, E0, NT])
                        chain(V.tensor_tensor(gt[:], tot[:, NT].unsqueeze(2).to_broadcast([TP, E0, NT]), steps, ALU.is_gt))
                        chain(V.tensor_reduce(tbl[:, 0, 0:E0], gt[:], AX.X, ALU.add))
                        chain(V.tensor_scalar(tbl[:, 0, 0:E0], tbl[:, 0, 0:E0], 1.0, None, ALU.max))
                        chain(V.memset(tbl[:, 1, 0:1], 0.0))
                        chain(V.memset(tbl[:, 0, E0:E0 + 1], 0.0))
                        for e in range(E0):
                            chain(V.tensor_tensor(tbl[:, 1, e + 1:e + 2], tbl[:, 1, e:e + 1], tbl[:, 0, e:e + 1], ALU.add))
                        V.tensor_copy(table_i[:], tbl[0:1]).then_inc(s_table, 1)
                        pre = bank[0:TP, 1, 0:NT * E0].rearrange("p (t e) -> p t e", e=E0)
                        chain(V.tensor_tensor(rank[:], tot[:, 0:NT], pre, ALU.add))
                        chain(V.scalar_tensor_tensor(rank[:], over_t(tbl[:, 1, 0:E0]), float(SLOT), rank[:], ALU.mult, ALU.add))
                        for c, hot in enumerate((oh1, oh2)):
                            chain(V.tensor_tensor(ky[:], hot[:], rank[:], ALU.mult))
                            chain(V.tensor_reduce(place[:, c], ky[:], AX.X, ALU.add))
                        V.tensor_copy(place_i[:], place[:]).then_inc(s_pl, 1)
                        tables["dve"] = read_table(dve)

                    @block.scalar
                    def _(act):
                        act.wait_ge(s_oh, 1)
                        act_n.add(nc.scalar.activation(pr[:], pr[:], ACT.Exp))
                        tables["act"] = read_table(act)

                    @block.gpsimd
                    def _(pool):
                        pool.wait_ge(s_pl, 1)
                        for i in range(NT):
                            for c in range(2):
                                pool.indirect_dma_start(
                                    out=slots_x, out_offset=bass.IndirectOffsetOnAxis(ap=place_i[:, c, i:i + 1], axis=0),
                                    in_=xn_rows[:, i], in_offset=None).then_inc(s_sc, 16)
                        tables["pool"] = read_table(pool)
                        pool.wait_ge(s_sc, 16 * 2 * NT)

            with ExitStack() as scope:
                s_free, s_stored = sem("expert_buffers_free"), sem("results_stored")
                slot_r = sb("slot_r", [P, D], scope=scope)
                slot_c = sb("slot_c", [P, KB, P], scope=scope)
                hid = sb("hid", [P, FB, P], scope=scope)
                hid_hi, hid_lo = (sb(n, [P, FB, P], F32R, scope=scope) for n in ("hid_hi", "hid_lo"))
                w2_hi = sb("w2_hi", [P, 2, FB, D], F32R, scope=scope)
                w2_lo = place_w2("w2_lo", [P, 2, FB, D], 0, F32R)
                s_hhi, s_hlo, s_whi, s_wlo = (sem(n) for n in ("hidden_high", "hidden_low", "w2_high", "w2_low"))
                y_sb = sb("y_sb", [P, D], scope=scope)
                hid_p = bank[:, 4:8, 0:P]
                turn_p = bank[:, 2, :].rearrange("p (b n) -> p b n", b=KB)
                y_p = bank[:, 3, :]

                def slot_rows(dram, g):
                    if not isinstance(g, int):
                        g = nc.s_assert_within(g, 0, SLOTS - 1, skip_runtime_bounds_check_because=(
                            "the experts' slots number SLOTS - 1 at most, as their sizes sum to 2 N"))
                    return dram.rearrange("(s p) d -> s p d", p=SLOT)[bass.ds(g, 1)].rearrange("a p d -> (a p) d")

                with nc.Block() as block:
                    @block.gpsimd
                    def _(pool):
                        def w2_low(e):
                            for f in range(FB):
                                pool.wait_ge(s_whi, e * FB + f + 1)
                                nc.gpsimd.tensor_tensor(w2_lo[:, e % 2, f], w2_sb[:, e % 2, f], w2_hi[:, e % 2, f].bitcast(F32),
                                                        ALU.subtract).then_inc(s_wlo, 1)

                        w2_low(0)
                        table = tables["pool"]
                        for e in range(1, E0):
                            w2_low(e)
                            if e + 1 < E0:
                                count, base = table[e - 1]
                                pool.wait_ge(s_ye, base + count + 1)
                                pool.sem_inc(s_free, 1)
                                pool.wait_ge(s_free, e)
                                load_expert(pool, e + 1)

                    @block.sync
                    def _(sp):
                        sp.sem_inc(s_yst, 16)
                        sp.dma_start(slot_r[:], slot_rows(slots_x, 0)).then_inc(s_xl, 16)
                        table = tables["sp"]
                        for e in range(E0):
                            count, base = table[e]
                            with sp.Fori(0, count) as i:
                                g = base + i
                                sp.wait_ge(s_xt, g + 1)
                                sp.dma_start(slot_r[:], slot_rows(slots_x, g + 1)).then_inc(s_xl, 16)
                                sp.wait_ge(s_ye, g + 2)
                                sp.dma_start(slot_rows(slots_y, g), y_sb[:]).then_inc(s_yst, 16)
                        total = sp.value_load(table_i[0:1, 1, E0:E0 + 1], min_val=E0, max_val=SLOTS - 1)
                        sp.wait_ge(s_yst, 16 * total + 16)
                        sp.sem_inc(s_stored, 1)
                        sp.wait_ge(s_stored, 1)

                    @block.tensor
                    def _(pe):
                        def turn(g):
                            pe.wait_ge(s_xl, 16 * (g + 1))
                            for b in range(KB):
                                ins = nc.tensor.transpose(turn_p[:, b], slot_r[:, b * P:(b + 1) * P], ident[:])
                            ins.then_inc(s_xt, 1)

                        turn(0)
                        table = tables["pe"]
                        pe.sem_inc(s_yd, 1)
                        for e in range(E0):
                            q = e % 2
                            pe.wait_ge(s_w[e], 64)
                            count, base = table[e]
                            with pe.Fori(0, count) as i:
                                g = base + i
                                pe.wait_ge(s_xr, g + 1)
                                for f in range(FB):
                                    if f >= 4:
                                        pe.wait_ge(s_gelu, g * FB + f - 3)
                                    for b in range(KB):
                                        ins = nc.tensor.matmul(hid_p[:, f % 4], w1_sb[:, q, b, f * P:(f + 1) * P], slot_c[:, b],
                                                               start=b == 0, stop=b == KB - 1)
                                    ins.then_inc(s_hd, 1)
                                turn(g + 1)
                                pe.wait_ge(s_ye, g + 1)
                                for f in range(FB):
                                    pe.wait_ge(s_wlo, e * FB + f + 1)
                                    pe.wait_ge(s_hlo, g * FB + f + 1)
                                    for k, (left, right) in enumerate(((hid_hi, w2_hi), (hid_lo, w2_hi), (hid_hi, w2_lo))):
                                        ins = nc.tensor.matmul(y_p, left[:, f], right[:, q, f], start=f == 0 and k == 0,
                                                               stop=f == FB - 1 and k == 2)
                                ins.then_inc(s_yd, 1)

                    @block.scalar
                    def _(act):
                        def w2_high(e):
                            act.wait_ge(s_w[e], 64)
                            for f in range(FB):
                                nc.scalar.copy(w2_hi[:, e % 2, f], w2_sb[:, e % 2, f]).then_inc(s_whi, 1)

                        w2_high(0)
                        table = tables["act"]
                        for e in range(E0):
                            q = e % 2
                            count, base = table[e]
                            with act.Fori(0, count) as i:
                                g = base + i
                                act.wait_ge(s_yd, g + 1)
                                for f in range(FB):
                                    act.wait_ge(s_hd, g * FB + f + 1)
                                    nc.scalar.activation(hid[:, f], hid_p[:, f % 4], ACT.Gelu,
                                                         bias=b1_sb[:, q, f:f + 1]).then_inc(s_gelu, 1)
                            if e + 1 < E0:
                                w2_high(e + 1)

                    @block.vector
                    def _(dve):
                        dve.sem_inc(s_ye, 1)
                        dve.wait_ge(s_xt, 1)
                        nc.vector.tensor_copy(slot_c[:], turn_p).then_inc(s_xr, 1)
                        table = tables["dve"]
                        for e in range(E0):
                            q = e % 2
                            dve.wait_ge(s_w[e], 64)
                            count, base = table[e]
                            with dve.Fori(0, count) as i:
                                g = base + i
                                for f in range(FB):
                                    dve.wait_ge(s_gelu, g * FB + f + 1)
                                    nc.vector.tensor_copy(hid_hi[:, f], hid[:, f]).then_inc(s_hhi, 1)
                                    dve.wait_ge(s_hhi, g * FB + f + 1)
                                    nc.vector.tensor_tensor(hid_lo[:, f], hid[:, f], hid_hi[:, f].bitcast(F32),
                                                            ALU.subtract).then_inc(s_hlo, 1)
                                dve.wait_ge(s_xt, g + 2)
                                nc.vector.tensor_copy(slot_c[:], turn_p).then_inc(s_xr, 1)
                                dve.wait_ge(s_yd, g + 2)
                                dve.wait_ge(s_yst, 16 * g + 16)
                                nc.vector.tensor_tensor(y_sb[:], y_p, b2_sb[:, q], ALU.add).then_inc(s_ye, 1)

        with ExitStack() as layer1:
            qi = sb("qi", [P, H * N], scope=layer1)
            qi_h = qi[:].rearrange("p (h n) -> p h n", h=H)
            wqkv1 = qi[:, 0:KB * 3 * D].rearrange("p (b n) -> p b n", b=KB)
            w_out = sb("w_out", [P, KB, D], scope=layer1)
            bias_c = sb("bias_c", [P, H + KB], scope=layer1)
            s_w1l, s_wg = sem("layer1_mix_weights"), sem("layer1_gnn_weights")

            xn_c = sb("xn_c2", [P, KB, N], scope=layer1)
            place1 = arena("row_room", 4 * NT * D, layer1)
            xn_rows = place1("xn_rows2", [TP, NT, D], 0)
            xw_hi = place1("xw_hi", [P, NT, D], 0, F32R)
            r_c = place1("r_c", [P, KB, N], 0)

            with ExitStack() as scope:
                w_g = sb("w_g", [P, KB, D], scope=scope)
                w_t = sb("w_t", [P, 2, D], scope=scope)
                t_emb = sb("t_emb", [P, 2], scope=scope)
                t_rep = sb("t_rep", [P, 2, TP], scope=scope)
                bias3 = sb("bias3", [TP, 3, D], scope=scope)
                bias_r = sb("bias_r", [TP, D], scope=scope)
                dinv = sb("dinv", [TP, NT], scope=scope)
                place_lo = arena("xw_lo_room", 4 * NT * D, scope)
                xw_lo = place_lo("xw_lo", [P, NT, D], 0, F32R)
                got = place_lo("got", [TP, 4, D], 4 * (NT - 4) * D)
                s_got = [sem(f"gathered_{q}") for q in range(4)]
                s_mix = sem("gathered_used")
                utmp = bias3
                LAG = 3
                s_xws, s_xwh = sem("xw_scaled"), sem("xw_high")
                s_dinv, s_te, s_xw, s_xwc, s_hop, s_hopc, s_trep, s_b3 = (sem(n) for n in (
                    "dinv_ready", "time_ready", "xw_ready", "xw_copied", "hop_ready", "hop_used", "time_repeated", "bias_summed"))
                with nc.Block() as block:
                    @block.gpsimd
                    def _(pool):
                        for n in range(2 * NT):
                            i, c = n // 2, n % 2
                            if n >= 4:
                                pool.wait_ge(s_mix, n - 3)
                            pool.indirect_dma_start(
                                out=got[:, n % 4], out_offset=None, in_=slots_y,
                                in_offset=bass.IndirectOffsetOnAxis(ap=place_i[:, c, i:i + 1], axis=0)).then_inc(s_got[n % 4], 16)

                    @block.vector
                    def _(dve):
                        chain = Chain(dve, dve_n)
                        nc.vector.tensor_scalar(rs_var[:], deg[:], 1.0, None, ALU.add).then_inc(s_dinv, 1)
                        dve.wait_ge(s_dinv, 2)
                        refine_rsqrt(chain, dinv[:], rs_var[:], rs_root[:], rs_tmp[:])
                        for c in range(2):
                            for i in range(c * HALF, (c + 1) * HALF):
                                for n in (2 * i, 2 * i + 1):
                                    dve.wait_ge(s_got[n % 4], 16 * (n // 4 + 1))
                                    nc.vector.scalar_tensor_tensor(x_res[:, i], got[:, n % 4], choice[:, n % 2, i:i + 1], x_res[:, i],
                                                                   ALU.mult, ALU.add).then_inc(s_mix, 1)
                                    dve.wait_ge(s_mix, n + 1)
                                ins = norm_stats(dve, 2, i)
                            chain(ins)
                            norm_variance(c)
                            norm_apply(dve, chain, 2, c, xn_rows)
                            if c == 0:
                                dve.wait_ge(s_wg, 96)
                                nc.vector.tensor_scalar(t_rep[:, 0], ones[:, 0:TP], t_emb[:, 0:1], None, ALU.mult)
                                nc.vector.tensor_scalar(t_rep[:, 1], ones[:, 0:TP], t_emb[:, 1:2], None, ALU.mult).then_inc(s_trep, 1)
                                chain(nc.vector.tensor_tensor(bias_r[:], bias3[:, 0], bias3[:, 1], ALU.add))
                                nc.vector.tensor_tensor(bias_r[:], bias_r[:], bias3[:, 2], ALU.add).then_inc(s_b3, 1)
                        for i in range(NT):
                            dve.wait_ge(s_xwh, i + 1)
                            nc.vector.tensor_tensor(xw_lo[0:TP, i], utmp[:, i % 2], xw_hi[0:TP, i].bitcast(F32),
                                                    ALU.subtract).then_inc(s_xwc, 1)

                    @block.tensor
                    def _(pe):
                        def xw_product(i):
                            pe.wait_ge(s_evac, 2 * NT + i + 1)
                            if i >= 4:
                                pe.wait_ge(s_xws, i - 3)
                            for b in range(KB):
                                ins = nc.tensor.matmul(bank[0:TP, 2 + i % 4, :], xn_c[:, b, i * TP:(i + 1) * TP], w_g[:, b],
                                                       start=b == 0, stop=b == KB - 1)
                            ins.then_inc(s_xw, 1)
                        for i in range(HALF):
                            norm_turn(pe, 2, i, xn_rows)
                        pe.wait_ge(s_wg, 96)
                        for i in range(LAG):
                            xw_product(i)
                        for i in range(HALF, NT):
                            norm_turn(pe, 2, i, xn_rows)
                            xw_product(i - HALF + LAG)
                        for i in range(HALF + LAG, NT):
                            xw_product(i)

                    @block.scalar
                    def _(act):
                        def xw_scaled(i):
                            act.wait_ge(s_xw, i + 1)
                            if i >= 2:
                                act.wait_ge(s_xwc, i - 1)
                            nc.scalar.activation(utmp[:, i % 2], bank[0:TP, 2 + i % 4, :], ACT.Copy, scale=dinv[:, i:i + 1]).then_inc(s_xws, 1)
                            act.wait_ge(s_xws, i + 1)
                            nc.scalar.copy(xw_hi[0:TP, i], utmp[:, i % 2]).then_inc(s_xwh, 1)
                        act.wait_ge(s_dinv, 1)
                        nc.scalar.activation(rs_root[:], rs_var[:], ACT.Sqrt).then_inc(s_dinv, 1)
                        norm_root(act, 2, 0)
                        for i in range(HALF):
                            norm_columns(act, 2, i, xn_rows, xn_c)
                        norm_root(act, 2, 1)
                        act.wait_ge(s_b3, 1)
                        for i in range(2):
                            xw_scaled(i)
                        for i in range(HALF, NT):
                            norm_columns(act, 2, i, xn_rows, xn_c)
                            xw_scaled(i - HALF + 2)
                        for i in range(HALF + 2, NT):
                            xw_scaled(i)

                    @block.sync
                    def _(sp):
                        sp.wait_ge(s_mix, 2)
                        sp.dma_start(w_g[:], blocks(t["L1_gnn_W"])).then_inc(s_wg, 16)
                        sp.dma_start(w_t[:], blocks(t["L1_gnn_Wt"])).then_inc(s_wg, 16)
                        sp.dma_start(t_emb[:], t["L1_gnn_t_emb"]).then_inc(s_wg, 16)
                        for c, name in enumerate(("L1_gnn_b", "L1_gnn_bt", "L1_mix_b_out")):
                            sp.dma_start(bias3[:, c], t[name].partition_broadcast(TP)).then_inc(s_wg, 16)
                        sp.wait_ge(s_mix, 2 * NT - 2)
                        sp.dma_start(wqkv1, blocks(t["L1_mix_W_qkv"])).then_inc(s_w1l, 16)
                        sp.dma_start(w_out[:], blocks(t["L1_mix_W_out"])).then_inc(s_w1l, 16)
                        sp.dma_start(bias_c[:], t["L1_mix_b_qkv"]).then_inc(s_w1l, 16)

                with nc.Block() as block:
                    @block.tensor
                    def _(pe):
                        pe.wait_ge(s_trep, 1)
                        for b in range(2):
                            ins = nc.tensor.matmul(bank[0:TP, 2, :], t_rep[:, b], w_t[:, b], start=b == 0, stop=b == 1)
                        ins.then_inc(s_te, 1)
                        large = pe.value_load(large_i[0:1, 0:1], min_val=0, max_val=1)
                        pe.wait_ge(s_xwc, NT)
                        for i in range(NT):
                            if i >= 2:
                                pe.wait_ge(s_hopc, i - 1)
                            def neighbours(adjacency, cast):
                                for s in range(NT):
                                    for k, part in enumerate((xw_hi, xw_lo)):
                                        ins = nc.tensor.matmul(bank[0:TP, 3 + i % 2, :], adjacency[:, s, i * TP:(i + 1) * TP],
                                                               cast(part[0:TP, s]), start=s == 0 and k == 0, stop=s == NT - 1 and k == 1)
                                ins.then_inc(s_hop, 1)
                            exact_counts(pe, large, neighbours)

                    @block.vector
                    def _(dve):
                        chain = Chain(dve, dve_n)
                        dve.wait_ge(s_te, 1)
                        chain(nc.vector.tensor_tensor(bias_r[:], bias_r[:], bank[0:TP, 2, :], ALU.add))
                        for i in range(NT):
                            chain(nc.vector.tensor_tensor(x_res[:, i], x_res[:, i], bias_r[:], ALU.add))
                        dve.wait_ge(s_xwc, NT)
                        for i in range(NT):
                            dve.wait_ge(s_hop, i + 1)
                            y = utmp[:, i % 2]
                            chain(nc.vector.tensor_tensor(y, bank[0:TP, 3 + i % 2, :], xw_hi[0:TP, i].bitcast(F32), ALU.add))
                            chain(nc.vector.tensor_tensor(y, y, xw_lo[0:TP, i].bitcast(F32), ALU.add))
                            nc.vector.scalar_tensor_tensor(x_res[:, i], y, dinv[:, i:i + 1], x_res[:, i],
                                                           ALU.mult, ALU.add).then_inc(s_hopc, 1)
                        dve.wait_ge(s_hopc, NT)

            with ExitStack() as scope:
                NC5, CW = 5, 250
                qk = sb("qk", [P, H, N], scope=scope)
                kv = adj[:, 0:H * N].rearrange("p (g h s) -> p g h s", g=GROUPS, h=H)
                free = xn_c[:].rearrange("p b n -> p (b n)")
                pm_sb = free[:, 0:2 * BATCH * GW].rearrange("p (q n) -> p q n", q=2)
                H2, NC = 2 * H, len(CHUNKS)
                ROW = NT * D
                assert 4 * N <= ROW and ROW % 32 == 0
                row_hi, row_lo = (place1(n, [H2, N], i * ROW, F32R) for i, n in enumerate(("row_hi", "row_lo")))
                ex_hat, sig_hat = (place1(n, [H2, N], i * ROW) for i, n in ((2, "ex_hat"), (3, "sig_hat")))
                sums, sums2, sw = (sb(n, [P, H], scope=scope) for n in ("sums", "sums2", "sw"))
                sw2 = sb("sw2", [P, H * (H2 + 2)], scope=scope)
                inv = ex_hat
                mx3, sm3 = (sb(n, [H2, NC], scope=scope) for n in ("mx3", "sm3"))
                nmax, norm = (sb(n, [H2, 1], scope=scope) for n in ("nmax", "norm"))
                vg_sb = sb("vg_sb", [P, 2, BATCH * HD], scope=scope)
                swap = sb("swap", [P, P], scope=scope)
                (s_qk, s_qkc, s_v, s_vcp, s_sw, s_swr, s_lh, s_io, s_ioc, s_hat, s_sig, s_mx, s_ex, s_kt,
                 s_swap, s_rows, s_inv, s_hi, s_lo, s_fac,
                 s_pm, s_pmc, s_vgc, s_r, s_rc, s_o, s_oc) = (sem(n) for n in (
                     "qk_ready", "qk_sigmoid", "v_ready", "v_biased", "sums_swapped", "sums_ready", "heads_ready", "io_ready",
                     "io_used", "hat_ready", "sig_ready", "max_ready", "exp_hat_ready", "q_k_weighted",
                     "swap_made", "token_sums", "inverses_ready", "rows_high", "rows_low", "factors_ready",
                     "pm_ready", "pm_masked", "v_turned", "r_ready", "r_copied", "out1_ready", "out1_used"))

                def banks3(q):
                    return bank[:, 3 * q:3 * q + 3, :].rearrange("p b (r n) -> p (b r) n", n=256)

                def head_chunks(q):
                    return banks3(q)[:, 0:NC5, 0:CW]

                def by5(a):
                    return a.rearrange("p (c n) -> p c n", c=NC5)

                def by_group(a):
                    return a.rearrange("p (g s) -> p g s", s=GROUP)

                with nc.Block() as block:
                    @block.tensor
                    def _(pe):
                        pe.wait_ge(s_w1l, 48)
                        for h in range(H):
                            if h >= 2:
                                pe.wait_ge(s_qkc, h - 1)
                            for c in range(NC5):
                                for b in range(KB):
                                    ins = nc.tensor.matmul(banks3(h % 2)[:, c, 0:CW], wqkv1[:, b, h * P:(h + 1) * P],
                                                           xn_c[:, b, c * CW:(c + 1) * CW], start=b == 0, stop=b == KB - 1)
                            ins.then_inc(s_qk, 1)
                        def values_of(m):
                            if m < 2:
                                pe.wait_ge(s_qkc, H - 1 + m)
                            else:
                                pe.wait_ge(s_vcp, 2 * m - 2)
                            for c in range(NC5):
                                for b in range(KB):
                                    ins = nc.tensor.matmul(banks3(m % 2)[:, c, 0:CW], wqkv1[:, b, 2 * D + m * P:2 * D + (m + 1) * P],
                                                           xn_c[:, b, c * CW:(c + 1) * CW], start=b == 0, stop=b == KB - 1)
                            ins.then_inc(s_v, 1)

                        def token_sums(c, at):
                            a, w = CHUNKS[c]
                            for h in range(H):
                                ins = nc.tensor.matmul(bank[0:H2, at, 0:w], sw2[:, h * H2:(h + 1) * H2], qk[:, h, a:a + w],
                                                       start=h == 0, stop=h == H - 1)
                            ins.then_inc(s_rows, 1)

                        def spread_rows(h):
                            for c, (a, w) in enumerate(CHUNKS):
                                r = w // CW
                                for k, part in enumerate((row_hi, row_lo)):
                                    ins = nc.tensor.matmul(banks3(h % 2)[:, 2 * c:2 * c + r, 0:CW], select[:, h], part[:, a:a + w],
                                                           start=k == 0, stop=k == 1)
                            return ins
                        values_of(0)
                        pe.wait_ge(s_qkc, H)
                        pe.wait_ge(s_swap, 1)
                        nc.tensor.matmul(bank[:, 6, 0:H], swap[:], sums[:], start=True, stop=True).then_inc(s_sw, 1)
                        values_of(1)
                        values_of(2)
                        pe.wait_ge(s_lh, 1)
                        token_sums(0, 6)
                        token_sums(1, 7)
                        values_of(3)
                        pe.wait_ge(s_inv, 1)
                        token_sums(2, 6)
                        pe.wait_ge(s_lo, NC)
                        for h in range(H):
                            if h < 2:
                                pe.wait_ge(s_vcp, 2 * KB - 2 + 2 * h)
                            else:
                                pe.wait_ge(s_ioc, h - 1)
                            spread_rows(h).then_inc(s_io, 1)
                        pe.wait_ge(s_swr, 1)
                        nc.tensor.matmul(bank[:, 6, 0:H], swap[:], sums2[:], start=True, stop=True).then_inc(s_sw, 1)
                        pe.wait_ge(s_lh, 2)
                        pe.wait_ge(s_ioc, H)
                        for c in range(NC):
                            token_sums(c, c)
                        pe.wait_ge(s_lo, 2 * NC)
                        for h in range(H):
                            if h >= 2:
                                pe.wait_ge(s_kt, h - 1)
                            spread_rows(h).then_inc(s_hat, 1)

                    @block.scalar
                    def _(act):
                        for h in range(H):
                            act.wait_ge(s_qk, h + 1)
                            nc.scalar.activation(by5(qk[:, h, 0:N]), head_chunks(h % 2), ACT.Sigmoid, bias=bias_c[:, h:h + 1],
                                                 accum_out=sums[:, h:h + 1]).then_inc(s_qkc, 1)
                        for c, (a, w) in enumerate(CHUNKS):
                            act.wait_ge(s_inv, c + 1)
                            nc.scalar.copy(row_hi[:, a:a + w], inv[:, a:a + w]).then_inc(s_hi, 1)
                        for c, (a, w) in enumerate(CHUNKS):
                            act.wait_ge(s_mx, c + 1)
                            nc.scalar.activation(sig_hat[:, a:a + w], bank[0:H2, c, 0:w], ACT.Sigmoid).then_inc(s_sig, 1)
                        act.wait_ge(s_mx, NC + 1)
                        for c, (a, w) in enumerate(CHUNKS):
                            nc.scalar.activation(ex_hat[:, a:a + w], bank[0:H2, c, 0:w], ACT.Exp, bias=nmax[:],
                                                 accum_out=sm3[:, c:c + 1]).then_inc(s_ex, 1)
                        for c, (a, w) in enumerate(CHUNKS):
                            act.wait_ge(s_fac, c + 1)
                            nc.scalar.copy(row_hi[:, a:a + w], sig_hat[:, a:a + w]).then_inc(s_hi, 1)

                    @block.vector
                    def _(dve):
                        chain = Chain(dve, dve_n)
                        V = nc.vector
                        chain(V.memset(sw2[:], 0.0))
                        V.tensor_copy(swap[:, 0:HD], ident[:, HD:P])
                        V.tensor_copy(swap[:, HD:P], ident[:, 0:HD]).then_inc(s_swap, 1)

                        def v_bias(m):
                            dve.wait_ge(s_v, m + 1)
                            for c in range(2):
                                rows = slice(c * HD, (c + 1) * HD)
                                V.tensor_scalar(kv[HD:P, :, 2 * m + c].rearrange("p (c g) s -> p c g s", c=NC5),
                                                head_chunks(m % 2)[rows].rearrange("p c (g s) -> p c g s", s=GROUP),
                                                bias_c[rows, H + m:H + m + 1], None, ALU.add).then_inc(s_vcp, 1)

                        def place_sums(n):
                            dve.wait_ge(s_sw, n)
                            chain(V.tensor_copy(sw[:], bank[:, 6, 0:H]))
                            V.tensor_tensor(sw2[:].rearrange("p (h k) -> p h k", k=H2 + 2)[:, :, 0:2],
                                            sw[:].unsqueeze(2).to_broadcast([P, H, 2]),
                                            headmask[:, 0:P:HD].unsqueeze(1).to_broadcast([P, H, 2]), ALU.mult).then_inc(s_lh, 1)

                        def inverse(c, at):
                            a, w = CHUNKS[c]
                            dve.wait_ge(s_rows, c + 1)
                            V.reciprocal(inv[:, a:a + w], bank[0:H2, at, 0:w]).then_inc(s_inv, 1)

                        def low(c):
                            a, w = CHUNKS[c]
                            dve.wait_ge(s_hi, c + 1)
                            V.tensor_tensor(row_lo[:, a:a + w], inv[:, a:a + w], row_hi[:, a:a + w].bitcast(F32),
                                            ALU.subtract).then_inc(s_lo, 1)
                        v_bias(0)
                        place_sums(1)
                        v_bias(1)
                        v_bias(2)
                        inverse(0, 6)
                        inverse(1, 7)
                        low(0)
                        low(1)
                        v_bias(3)
                        inverse(2, 6)
                        low(2)
                        for h in range(H):
                            dve.wait_ge(s_io, h + 1)
                            V.tensor_tensor_reduce(by5(qi_h[:, h, 0:N]), by5(qk[:, h, 0:N]), head_chunks(h % 2), 1.0, 0.0,
                                                   ALU.mult, ALU.add, sums2[:, h:h + 1]).then_inc(s_ioc, 1)
                        dve.wait_ge(s_ioc, H)
                        dve.engine_nop().then_inc(s_swr, 1)
                        place_sums(2)
                        for c, (a, w) in enumerate(CHUNKS):
                            dve.wait_ge(s_rows, NC + c + 1)
                            V.tensor_reduce(mx3[:, c:c + 1], bank[0:H2, c, 0:w], AX.X, ALU.max).then_inc(s_mx, 1)
                        dve.wait_ge(s_mx, NC)
                        chain(V.tensor_reduce(nmax[:], mx3[:], AX.X, ALU.max))
                        V.tensor_scalar(nmax[:], nmax[:], -1.0, None, ALU.mult).then_inc(s_mx, 1)
                        even, odd = smallc[0:H2, 160:161], smallc[0:H2, 161:162]
                        for c, (a, w) in enumerate(CHUNKS):
                            dve.wait_ge(s_sig, c + 1)
                            chain(V.tensor_scalar(sig_hat[:, a:a + w], sig_hat[:, a:a + w], even, None, ALU.mult))
                        dve.wait_ge(s_ex, NC)
                        chain(V.tensor_reduce(norm[:], sm3[:], AX.X, ALU.add))
                        chain(V.reciprocal(norm[:], norm[:]))
                        chain(V.tensor_tensor(norm[:], norm[:], odd, ALU.mult))
                        for c, (a, w) in enumerate(CHUNKS):
                            V.scalar_tensor_tensor(sig_hat[:, a:a + w], ex_hat[:, a:a + w], norm[:], sig_hat[:, a:a + w],
                                                   ALU.mult, ALU.add).then_inc(s_fac, 1)
                        for c, (a, w) in enumerate(CHUNKS):
                            dve.wait_ge(s_hi, NC + c + 1)
                            V.tensor_tensor(row_lo[:, a:a + w], sig_hat[:, a:a + w], row_hi[:, a:a + w].bitcast(F32),
                                            ALU.subtract).then_inc(s_lo, 1)
                        for h in range(H):
                            dve.wait_ge(s_hat, h + 1)
                            V.tensor_tensor(by5(qi_h[0:HD, h, 0:N]), by5(qi_h[0:HD, h, 0:N]), head_chunks(h % 2)[0:HD], ALU.mult)
                            V.tensor_tensor(kv[0:HD, :, h].rearrange("p (c g) s -> p c g s", c=NC5),
                                            head_chunks(h % 2)[HD:P].rearrange("p c (g s) -> p c g s", s=GROUP),
                                            qk[HD:P, h].rearrange("p (c g s) -> p c g s", c=NC5, s=GROUP), ALU.mult).then_inc(s_kt, 1)
                        dve.wait_ge(s_kt, H)

                with nc.Block() as block:
                    NB = GROUPS // BATCH

                    def score_bank(q):
                        return bank[0:GW, q, 0:BATCH * GW].rearrange("p (j n) -> p j n", n=GW)

                    @block.tensor
                    def _(pe):
                        def scores(n):
                            if n >= 2:
                                pe.wait_ge(s_pmc, n - 1)
                                pe.wait_ge(s_vgc, n - 1)
                            for j in range(BATCH):
                                g = n * BATCH + j
                                tok = slice(g * GROUP, (g + 1) * GROUP)
                                nc.tensor.matmul(bank[0:GW, n % 2, j * GW:(j + 1) * GW],
                                                 kv[0:HD, g].rearrange("p h s -> p (h s)"), qi_h[0:HD, :, tok],
                                                 start=True, stop=True)
                                ins = nc.tensor.transpose(bank[0:GW, 2 + n % 2, j * HD:(j + 1) * HD],
                                                          kv[HD:P, g].rearrange("p h s -> p (h s)"), ident[HD:P, HD:P])
                            ins.then_inc(s_pm, 1)

                        def values(n):
                            pe.wait_ge(s_pmc, n + 1)
                            pe.wait_ge(s_vgc, n + 1)
                            if n >= 2:
                                pe.wait_ge(s_rc, n - 1)
                            for j in range(BATCH):
                                ins = nc.tensor.matmul(bank[0:HD, 4 + n % 2, j * GW:(j + 1) * GW],
                                                       vg_sb[0:GW, n % 2, j * HD:(j + 1) * HD],
                                                       pm_sb[0:GW, n % 2, j * GW:(j + 1) * GW], start=True, stop=True)
                            ins.then_inc(s_r, 1)
                        for n in range(NB):
                            scores(n)
                            if n >= 1:
                                values(n - 1)
                        values(NB - 1)
                        pe.wait_ge(s_rc, NB)
                        for i in range(NT):
                            if i >= 2:
                                pe.wait_ge(s_oc, i - 1)
                            for b in range(KB):
                                ins = nc.tensor.matmul(bank[0:TP, 6 + i % 2, :], r_c[:, b, i * TP:(i + 1) * TP], w_out[:, b],
                                                       start=b == 0, stop=b == KB - 1)
                            ins.then_inc(s_o, 1)

                    def r_in(n, par):
                        return bank[0:HD, 4 + n % 2, 0:BATCH * GW].rearrange("p (j b c s) -> p c b j s", j=BATCH, b=KB, c=2)[:, par]

                    def r_out(n, par):
                        cols = r_c[par * HD:(par + 1) * HD, :, n * BATCH * GROUP:(n + 1) * BATCH * GROUP]
                        return cols.rearrange("p b (j s) -> p b j s", j=BATCH)

                    @block.vector
                    def _(dve):
                        mask4 = tokmask[0:GW, 0:GW].unsqueeze(1).to_broadcast([GW, BATCH, GW])
                        for n in range(NB):
                            dve.wait_ge(s_pm, n + 1)
                            if n >= 2:
                                dve.wait_ge(s_r, n - 1)
                            nc.vector.tensor_tensor(pm_sb[0:GW, n % 2].rearrange("p (j n) -> p j n", n=GW), score_bank(n % 2), mask4,
                                                    ALU.mult).then_inc(s_pmc, 1)
                            nc.vector.tensor_copy(vg_sb[0:GW, n % 2], bank[0:GW, 2 + n % 2, 0:BATCH * HD]).then_inc(s_vgc, 1)
                        for i in range(NT):
                            dve.wait_ge(s_o, i + 1)
                            nc.vector.tensor_tensor(x_res[:, i], x_res[:, i], bank[0:TP, 6 + i % 2, :], ALU.add).then_inc(s_oc, 1)
                        dve.wait_ge(s_oc, NT)

                    @block.scalar
                    def _(act):
                        for n in range(NB):
                            act.wait_ge(s_r, n + 1)
                            nc.scalar.copy(r_out(n, 0), r_in(n, 0))
                            nc.scalar.copy(r_out(n, 1), r_in(n, 1)).then_inc(s_rc, 1)

            with ExitStack() as scope:
                wg = sb("wg", [P, KB, E1], scope=scope)
                bg = sb("bg", [TP, E1], scope=scope)
                mean_c = sb("mean_c", [P, KB], scope=scope)
                mean_rep = sb("mean_rep", [P, KB, TP], scope=scope)
                lg, eg, kg = (sb(n, [TP, E1], scope=scope) for n in ("lg", "eg", "kg"))
                sc = sb("sc", [TP, 8], scope=scope)
                pick_i = sb("pick_i", [1, 1], I32, scope=scope)
                w_e = sb("w_e", [P, KB, D], scope=scope)
                b_e = sb("b_e", [TP, D], scope=scope)
                ytmp = sb("ytmp", [TP, 2, D], scope=scope)
                s_g1, s_mean, s_l1, s_e1, s_pick, s_we, s_y, s_yc, s_st = (sem(n) for n in (
                    "gate1_weights", "mean_ready", "logits1_ready", "exp1_ready", "pick_ready", "picked_loaded", "y1_ready", "x_done", "x_stored"))
                with nc.Block() as block:
                    layernorm(block, 3, xn_rows, xn_c)

                    @block.sync
                    def _(sp):
                        sp.dma_start(wg[:], blocks(t["L1_ffn_Wg"])).then_inc(s_g1, 16)
                        sp.dma_start(bg[:], t["L1_ffn_bg"].partition_broadcast(TP)).then_inc(s_g1, 16)

                with nc.Block() as block:
                    @block.sync
                    def _(sp):
                        sp.wait_ge(s_pick, 1)
                        e = sp.value_load(pick_i[0:1, 0:1], min_val=0, max_val=E1 - 1)
                        sp.dma_start(w_e[:], t["L1_ffn_We"][bass.ds(e, 1)].rearrange("a (b p) n -> p (a b) n", p=P)).then_inc(s_we, 16)
                        sp.dma_start(b_e[:], t["L1_ffn_be"][bass.ds(e, 1)].rearrange("a n -> (a n)").partition_broadcast(TP)).then_inc(s_we, 16)
                        for i in range(NT):
                            sp.wait_ge(s_yc, i + 1)
                            sp.dma_start(t["out"][i * TP:(i + 1) * TP, :], x_res[:, i]).then_inc(s_st, 16)
                        sp.wait_ge(s_st, 16 * NT)

                    @block.tensor
                    def _(pe):
                        pe.wait_ge(s_mean, 1)
                        pe.wait_ge(s_g1, 32)
                        for b in range(KB):
                            ins = nc.tensor.matmul(bank[0:TP, 0, 0:E1], mean_rep[:, b], wg[:, b], start=b == 0, stop=b == KB - 1)
                        ins.then_inc(s_l1, 1)
                        pe.wait_ge(s_we, 32)
                        for i in range(NT):
                            if i >= 2:
                                pe.wait_ge(s_yc, i - 1)
                            for b in range(KB):
                                ins = nc.tensor.matmul(bank[0:TP, 1 + i % 2, :], xn_c[:, b, i * TP:(i + 1) * TP], w_e[:, b],
                                                       start=b == 0, stop=b == KB - 1)
                            ins.then_inc(s_y, 1)

                    @block.scalar
                    def _(act):
                        act.wait_ge(s_e1, 1)
                        nc.scalar.activation(eg[:], lg[:], ACT.Exp, bias=sc[:, 0:1], accum_out=sc[:, 1:2]).then_inc(s_e1, 1)

                    @block.vector
                    def _(dve):
                        chain = Chain(dve, dve_n)
                        V = nc.vector
                        chain(V.tensor_reduce(mean_c[:], xn_c[:], AX.X, ALU.add))
                        chain(V.tensor_scalar(mean_c[:], mean_c[:], 1.0 / N, None, ALU.mult))
                        for b in range(KB):
                            ins = V.tensor_scalar(mean_rep[:, b], ones[:, 0:TP], mean_c[:, b:b + 1], None, ALU.mult)
                        ins.then_inc(s_mean, 1)
                        dve.wait_ge(s_l1, 1)
                        dve.wait_ge(s_g1, 32)
                        chain(V.tensor_tensor(lg[:], bank[0:TP, 0, 0:E1], bg[:], ALU.add))
                        chain(V.tensor_reduce(sc[:, 2:3], lg[:], AX.X, ALU.max))
                        V.tensor_scalar(sc[:, 0:1], sc[:, 2:3], -1.0, None, ALU.mult).then_inc(s_e1, 1)
                        dve.wait_ge(s_e1, 2)
                        chain(V.reciprocal(sc[:, 3:4], sc[:, 1:2]))
                        chain(V.tensor_reduce(sc[:, 4:5], eg[:], AX.X, ALU.max))
                        chain(V.tensor_tensor(sc[:, 5:6], sc[:, 4:5], sc[:, 3:4], ALU.mult))
                        chain(V.tensor_scalar(kg[:], eg[:], sc[:, 4:5], -float(E1), ALU.is_equal, ALU.mult))
                        chain(V.tensor_tensor(kg[:], kg[:], smallc[0:TP, 128:128 + E1], ALU.add))
                        chain(V.tensor_reduce(sc[:, 6:7], kg[:], AX.X, ALU.min))
                        chain(V.tensor_scalar(sc[:, 6:7], sc[:, 6:7], float(E1), None, ALU.add))
                        V.tensor_copy(pick_i[:], sc[0:1, 6:7]).then_inc(s_pick, 1)
                        dve.wait_ge(s_we, 32)
                        for i in range(NT):
                            dve.wait_ge(s_y, i + 1)
                            y = ytmp[:, i % 2]
                            chain(V.tensor_tensor(y, bank[0:TP, 1 + i % 2, :], b_e[:], ALU.add))
                            V.scalar_tensor_tensor(x_res[:, i], y, sc[:, 5:6], x_res[:, i], ALU.mult, ALU.add).then_inc(s_yc, 1)


def host_constants():
    i = np.arange(P)
    small = np.zeros((P, 256), np.float32)
    small[:NT, 0] = np.arange(NT) * TP
    small[:NT, 1] = np.arange(NT) * TP + TP - 1
    small[:, 8:8 + STEPS] = np.arange(STEPS)
    small[:, 128:144] = np.arange(16)
    small[:, 160] = i % 2 == 0
    small[:, 161] = i % 2 == 1
    small[:, 144:144 + NT] = np.arange(NT) * SLOT
    return {
        "c_ident": np.eye(P, dtype=np.float32),
        "c_before": (i[:, None] < i[None, :]).astype(np.float32),
        "c_ones": np.ones((P, P), np.float32),
        "c_headmask": (i[:, None] // HD == i[None, :] // HD).astype(np.float32),
        "c_tokmask": (i[:, None] % GROUP == i[None, :] % GROUP).astype(np.float32),
        "c_iota": np.broadcast_to(np.arange(N), (P, N)).astype(np.float16),
        "c_small": small,
        "c_select": (np.arange(2 * H)[:, None] == 2 * (np.arange(H * P) // P) + np.arange(H * P) % P // HD).astype(np.float32),
    }


def kernel(**inputs):
    import concourse.bacc as bacc
    from concourse.bass_utils import run_bass_kernel_spmd

    a = {k: np.asarray(v) for k, v in inputs.items()}
    for name in ("L0_gnn_W_l", "L0_gnn_W_r", "L1_mix_W_out", "L1_mix_W_qkv"):
        a[name] = a[name].T
    order = np.arange(3 * D).reshape(H, 3, HD)
    order = np.concatenate([order[:, 0:2].reshape(-1), order[:, 2].reshape(-1)])
    a["L1_mix_W_qkv"] = a["L1_mix_W_qkv"][:, order]
    a["L1_mix_b_qkv"] = a["L1_mix_b_qkv"][order].reshape(-1, P).T
    a["L1_gnn_t_emb"] = a["L1_gnn_t_emb"].reshape(-1, P).T
    a["L0_ffn_b1"] = a["L0_ffn_b1"].reshape(E0, FB, P).transpose(0, 2, 1)
    a.update(host_constants())
    nc = bacc.Bacc("TRN2", target_bir_lowering=False, num_devices=1)
    arrays, t = {}, {}
    for name, v in a.items():
        v = np.ascontiguousarray(v)
        arrays["in_" + name] = v
        t[name] = nc.dram_tensor("in_" + name, v.shape, mybir.dt.from_np(v.dtype), kind="ExternalInput").ap()
    t["out"] = nc.dram_tensor("out_x", (N, D), F32, kind="ExternalOutput").ap()
    build(nc, t)
    r = run_bass_kernel_spmd(nc, [arrays], core_ids=[0])
    return r.results[0]["out_x"]
```

```python
from contextlib import ExitStack

import numpy as np

import concourse.bass as bass
from concourse import mybir

ALU = mybir.AluOpType
ACT = mybir.ActivationFunctionType
AX = mybir.AxisListType
F32 = mybir.dt.float32
F32R = mybir.dt.float32r
F16 = mybir.dt.float16
BF16 = mybir.dt.bfloat16
I32 = mybir.dt.int32
U32 = mybir.dt.uint32

N, D, EDGES = 1250, 512, 20000
P = 128
TP = 125
NT = N // TP
KB = D // P
CHUNKS = [(0, 500), (500, 500), (1000, 250)]
QT = 4
STEPS = EDGES // (QT * TP)
H, HD = 8, 64
E0, F0, SLOT = 8, 1024, 128
FB = F0 // P
SLOTS = (2 * N - E0) // SLOT + E0 + 1
SLOTS_SURE = 2 * N // SLOT + 1
E1 = 16
EPS_LN, EPS_ATT = 1e-5, 1e-6
GROUP = 10
GW = GROUP * H
GROUPS = N // GROUP
BATCH = 5
BIG = 1000.0
HALF = NT // 2


class Count:

    def __init__(self, sem):
        self.sem, self.n = sem, 0

    def add(self, ins):
        self.n += 1
        ins.then_inc(self.sem, 1)
        return self.n


class Chain:

    def __init__(self, eng, count):
        self.eng, self.count = eng, count

    def __call__(self, ins):
        self.eng.wait_ge(self.count.sem, self.count.add(ins))


def blocks(w):
    return w.rearrange("(b p) n -> p b n", p=P)


def build(nc, t):
    with ExitStack() as top:
        def sb(name, shape, dt=F32, scope=top):
            return scope.enter_context(nc.sbuf_tensor(name, shape, dt))

        def arena(name, nbytes, scope):
            base = -(-nc.sbuf_base // 32) * 32
            scope.enter_context(nc.sbuf_tensor(name, [P, nbytes // 4 + 8], F32))

            def place(tensor, shape, offset, dt=F32):
                size = mybir.dt.size(dt) * int(np.prod(shape[1:]))
                assert offset % 32 == 0 and offset + size <= nbytes, (tensor, offset, size)
                return nc.alloc_sbuf_tensor_at(tensor, shape, dt, offset=base + offset)
            return place

        def sem(name):
            return top.enter_context(nc.semaphore(name))

        bank = top.enter_context(nc.psum_tensor("bank", [P, 8, 512], F32))
        x_res = sb("x_res", [TP, NT, D])
        place_adj = arena("adj_room", 4 * NT * N, top)
        adj = place_adj("adj", [P, NT * N], 0)
        adj_t = adj[0:TP, :].rearrange("p (s n) -> p s n", s=NT)
        adj_12 = place_adj("adj_12", [P, NT * N], 0, F32R)[0:TP, :].rearrange("p (s n) -> p s n", s=NT)
        ident = sb("ident", [P, P])
        before = sb("before", [P, P])
        ones = sb("ones", [P, P])
        headmask = sb("headmask", [P, P])
        tokmask = sb("tokmask", [P, P])
        smallc = sb("smallc", [P, 256])
        select = sb("select", [2 * H, H, P], F32R)
        deg = sb("deg", [TP, NT])
        large_i = sb("large_i", [1, 1], I32)
        stats = sb("stats", [TP, NT, 6])
        moments = sb("moments", [TP, NT, 2])
        rstd, rs_var, rs_root, rs_tmp = (sb(n, [TP, NT]) for n in ("rstd", "rs_var", "rs_root", "rs_tmp"))

        s_x = [sem("x_loaded_0"), sem("x_loaded_1")]
        s_const, s_edges, s_zero, s_zfill = (sem(n) for n in ("const_loaded", "edges_loaded", "zero_set", "zero_filled"))
        s_kvw_in, s_w0, s_gate_w = sem("kv_weights_loaded"), sem("layer0_weights_loaded"), sem("gate_weights_loaded")
        s_normed, s_turned, s_evac = (sem(n) for n in ("normed", "turned", "columns_ready"))
        s_high, s_low = sem("high_parts_taken"), sem("low_parts_taken")
        s_bn, s_var, s_sqrt = sem("stats_ready"), sem("variance_ready"), sem("root_ready")
        dve_n, act_n = Count(sem("dve_step")), Count(sem("act_step"))

        slots_x = nc.dram_tensor("slots_x", (SLOTS * SLOT, D), F32, kind="Internal").ap()
        slots_y = nc.dram_tensor("slots_y", (SLOTS * SLOT, D), F32, kind="Internal").ap()

        def exact_counts(pe, large, products):
            with pe.If_eq(large.val, 0):
                products(adj_12, lambda a: a)
            with pe.If_eq(large.val, 1):
                products(adj_t, lambda a: a.bitcast(F32))

        def refine_rsqrt(chain, out, v, root, tmp):
            chain(nc.vector.reciprocal(out, root))
            chain(nc.vector.tensor_tensor(tmp, out, out, ALU.mult))
            chain(nc.vector.tensor_tensor(tmp, tmp, v, ALU.mult))
            chain(nc.vector.tensor_scalar(tmp, tmp, -0.5, 1.5, ALU.mult, ALU.add))
            chain(nc.vector.tensor_tensor(out, out, tmp, ALU.mult))

        def norm_stats(dve, which, i):
            nc.vector.bn_stats(stats[:, i], x_res[:, i]).then_inc(s_bn, 1)
            dve.wait_ge(s_bn, which * NT + i + 1)
            return nc.vector.bn_aggr(moments[:, i], stats[:, i])

        def norm_variance(c):
            tiles = slice(c * HALF, (c + 1) * HALF)
            nc.vector.tensor_scalar(rs_var[:, tiles], moments[:, tiles, 1], EPS_LN, None, ALU.add).then_inc(s_var, 1)

        def norm_root(act, which, c):
            tiles = slice(c * HALF, (c + 1) * HALF)
            act.wait_ge(s_var, 2 * which + c + 1)
            nc.scalar.activation(rs_root[:, tiles], rs_var[:, tiles], ACT.Sqrt).then_inc(s_sqrt, 1)

        def norm_apply(dve, chain, which, c, rows, parts=None):
            base, kept = which * NT, rows.shape[1]
            tiles = slice(c * HALF, (c + 1) * HALF)
            dve.wait_ge(s_sqrt, 2 * which + c + 1)
            refine_rsqrt(chain, rstd[:, tiles], rs_var[:, tiles], rs_root[:, tiles], rs_tmp[:, tiles])
            for i in range(c * HALF, (c + 1) * HALF):
                if i >= kept:
                    dve.wait_ge(s_turned, base + i - kept + 1)
                    if parts:
                        dve.wait_ge(s_high, base + i - kept + 1)
                nc.vector.tensor_scalar(rows[:, i % kept], x_res[:, i], moments[:, i, 0:1], rstd[:, i:i + 1],
                                        ALU.subtract, ALU.mult).then_inc(s_normed, 1)
                if parts:
                    dve.wait_ge(s_high, base + i + 1)
                    nc.vector.tensor_tensor(parts[1][0:TP, i], rows[:, i % kept], parts[0][0:TP, i].bitcast(F32),
                                            ALU.subtract).then_inc(s_low, 1)

        def turn_bank(which, i):
            return (6 if which == 1 else 0) + i % 2

        def norm_turn(pe, which, i, rows):
            base, kept = which * NT, rows.shape[1]
            pe.wait_ge(s_normed, base + i + 1)
            if i >= 2:
                pe.wait_ge(s_evac, base + i - 1)
            for b in range(KB):
                ins = nc.tensor.transpose(bank[:, turn_bank(which, i), b * P:b * P + TP], rows[:, i % kept, b * P:(b + 1) * P],
                                          ident[0:TP, 0:TP])
            ins.then_inc(s_turned, 1)

        def norm_columns(act, which, i, rows, cols, parts=None):
            base, kept = which * NT, rows.shape[1]
            if parts:
                act.wait_ge(s_normed, base + i + 1)
                nc.scalar.copy(parts[0][0:TP, i], rows[:, i % kept]).then_inc(s_high, 1)
            act.wait_ge(s_turned, base + i + 1)
            nc.scalar.copy(cols[:, :, i * TP:(i + 1) * TP],
                           bank[:, turn_bank(which, i), :].rearrange("p (b n) -> p b n", b=KB)[:, :, 0:TP]).then_inc(s_evac, 1)

        def layernorm(block, which, rows, cols, parts=None):
            @block.vector
            def _(dve):
                chain = Chain(dve, dve_n)
                for c in range(2):
                    for i in range(c * HALF, (c + 1) * HALF):
                        if which == 0:
                            dve.wait_ge(s_x[c], 16)
                        ins = norm_stats(dve, which, i)
                    chain(ins)
                    norm_variance(c)
                    norm_apply(dve, chain, which, c, rows, parts)

            @block.tensor
            def _(pe):
                if which == 0:
                    pe.wait_ge(s_const, 16 * N_CONST)
                for i in range(NT):
                    norm_turn(pe, which, i, rows)

            @block.scalar
            def _(act):
                for c in range(2):
                    norm_root(act, which, c)
                    for i in range(c * HALF, (c + 1) * HALF):
                        norm_columns(act, which, i, rows, cols, parts)

        N_CONST = 8
        gate_w, gate_b = sb("gate_w", [P, KB, E0]), sb("gate_b", [TP, E0])
        choice = sb("choice", [TP, 2, NT])
        place_i = sb("place_i", [TP, 2, NT], U32)
        layer0 = top.enter_context(ExitStack())
        K = 1024
        place = arena("layer0_room", 126 * K, layer0)
        xn_c = place("xn_c0", [P, KB, N], 0)
        xn_hi = place("xn_hi", [P, NT, D], 20 * K, F32R)
        xn_lo = place("xn_lo", [P, NT, D], 40 * K, F32R)
        q_c = place("q_c", [P, KB, N], 40 * K)
        w_kv = place("w_kv", [P, KB, 2 * D], 60 * K)
        kv_r = place("kv_r", [TP, 2, 2 * D], 76 * K)
        agg = place("agg", [P, KB, N], 60 * K)
        w_q, w_l, w_r, w_proj = (place(n, [P, KB, D], (84 + 8 * i) * K) for i, n in enumerate(("w_q", "w_l", "w_r", "w_proj")))
        b_l, b_proj = (place(n, [TP, D], (116 + 2 * i) * K) for i, n in enumerate(("b_l", "b_proj")))
        qtmp = place("qtmp", [P, 2, D], 120 * K)
        k_total = place("k_total", [TP, D], 124 * K)
        rows1 = place("rows1", [TP, NT, D], 20 * K)
        kv_h = place("kv_h", [P, KB, P], 84 * K)
        zinv = place("zinv", [H, N], 86 * K)
        zi_hi, zi_lo = (place(n, [H, N], (20 + 5 * i) * K, F32R) for i, n in enumerate(("zi_hi", "zi_lo")))

        s_kv, s_min, s_exp, s_kf, s_vc, s_acc, s_ks = (sem(n) for n in (
            "kv_ready", "min_ready", "exp_ready", "k_feature", "v_copied", "kv_summed", "k_summed"))

        def k_bank(i):
            return bank[0:TP, 3 + 2 * (i % 2), :]

        def kv_product(pe, i):
            if i == 0:
                pe.wait_ge(s_kvw_in, 16)
            if i >= 2:
                pe.wait_ge(s_kf, i - 1)
            if i >= 1:
                pe.wait_ge(s_vc, i)
            for g, out in enumerate((k_bank(i), bank[0:TP, 4, :])):
                for b in range(KB):
                    ins = nc.tensor.matmul(out, xn_c[:, b, i * TP:(i + 1) * TP], w_kv[:, b, g * D:(g + 1) * D],
                                           start=b == 0, stop=b == KB - 1)
                ins.then_inc(s_kv, 1)

        def kv_sums(pe, i):
            pe.wait_ge(s_kf, i + 1)
            pe.wait_ge(s_vc, i + 1)
            k, v = kv_r[:, i % 2, 0:D], kv_r[:, i % 2, D:2 * D]
            for m in range(KB):
                ins = nc.tensor.matmul(bank[:, 6, m * P:(m + 1) * P], v[:, m * P:(m + 1) * P], k[:, m * P:(m + 1) * P],
                                       start=i == 0 and m == 0, stop=i == NT - 1, skip_group_check=True)
            ins.then_inc(s_acc, 1)

        def k_sum(pool, i):
            pool.wait_ge(s_kf, i + 1)
            k = kv_r[:, i % 2, 0:D]
            if i == 0:
                nc.gpsimd.tensor_copy(k_total[:], k).then_inc(s_ks, 1)
            else:
                pool.wait_ge(s_ks, i)
                nc.gpsimd.tensor_tensor(k_total[:], k_total[:], k, ALU.add).then_inc(s_ks, 1)

        def k_feature(dve, i):
            dve.wait_ge(s_kv, 2 * i + 1)
            if i >= 2:
                dve.wait_ge(s_acc, i - 1)
                dve.wait_ge(s_ks, i - 1)
            nc.vector.tensor_scalar(qtmp[0:TP, i % 2, :], k_bank(i), 0.0, None, ALU.min).then_inc(s_min, 1)
            dve.wait_ge(s_exp, i + 1)
            nc.vector.scalar_tensor_tensor(kv_r[:, i % 2, 0:D], k_bank(i), 0.0, qtmp[0:TP, i % 2, :],
                                           ALU.max, ALU.add).then_inc(s_kf, 1)

        def k_exp(act, i):
            act.wait_ge(s_min, i + 1)
            nc.scalar.activation(qtmp[0:TP, i % 2, :], qtmp[0:TP, i % 2, :], ACT.Exp).then_inc(s_exp, 1)

        def v_copy(act, i):
            act.wait_ge(s_kv, 2 * i + 2)
            if i >= 2:
                act.wait_ge(s_acc, i - 1)
            nc.scalar.copy(kv_r[:, i % 2, D:2 * D], bank[0:TP, 4, :]).then_inc(s_vc, 1)

        s_lgc = sem("logit_columns")

        with ExitStack() as scope:
            room_used = [0]

            def scratch(name, shape, dt=F32, end=36 * K):
                room_used[0] = -(-room_used[0] // 32) * 32
                size = mybir.dt.size(dt) * int(np.prod(shape[1:]))
                at, room_used[0] = room_used[0], room_used[0] + size
                assert room_used[0] <= end
                return place(name, shape, 84 * K + at, dt)
            zeros = scratch("zeros", [P, 4 * D])
            iota = scratch("iota", [P, N], F16)
            select_f = place("select_f", [2 * H, H * P], 76 * K)
            zeros16 = scratch("zeros16", [P, 512], BF16)
            ones16 = scratch("ones16", [P, 2], BF16)
            edge_i = scratch("edge_i", [STEPS, 2, QT * TP], I32)
            edge_f = scratch("edge_f", [STEPS, 2, QT * TP])
            edge_c = scratch("edge_c", [TP, 2, QT, 2 * STEPS])
            span = scratch("span", [STEPS, 2])
            span_w = scratch("span_w", [STEPS, 2, NT])
            fl1, fl2, key = (scratch(n, [NT, STEPS]) for n in ("fl1", "fl2", "key"))
            plan = scratch("plan", [NT, 4])
            plan_i = scratch("plan_i", [NT, 4], I32)
            onehot_src = scratch("onehot_src", [TP, QT, N], BF16)
            onehot_dst = scratch("onehot_dst", [TP, QT, TP], BF16)
            dmax = scratch("dmax", [TP, 1])
            s_hot = [sem(f"onehot_ready_{j}") for j in range(QT)]
            s_used = [sem(f"onehot_used_{j}") for j in range(QT)]
            s_adj = sem("window_copied")
            s_deg, s_large, s_all = sem("degree_greatest"), sem("large_known"), sem("degrees_turned")
            s_plan, s_edge_f = sem("plan_ready"), sem("edges_as_floats")
            s_span = sem("span_ready")
            s_spanp = sem("span_turned")

            with nc.Block() as block:
                layernorm(block, 0, qtmp[0:TP], xn_c, (xn_hi, xn_lo))

                @block.sync
                def _(sp):
                    for c in range(2):
                        sp.dma_start(x_res[:, c * HALF:(c + 1) * HALF],
                                     t["x"].rearrange("(t p) d -> p t d", p=TP)[:, c * HALF:(c + 1) * HALF]).then_inc(s_x[c], 16)
                    for n, (dst, src) in enumerate([(ident, t["c_ident"]), (before, t["c_before"]), (ones, t["c_ones"]),
                                                    (headmask, t["c_headmask"]), (tokmask, t["c_tokmask"]),
                                                    (iota, t["c_iota"]), (smallc, t["c_small"]),
                                                    (select_f, t["c_select"])]):
                        sp.dma_start(dst[:], src).then_inc(s_const, 16)
                    for n, name in enumerate(("src", "dst")):
                        sp.dma_start(edge_i[:, n], t[name].rearrange("(u e) -> u e", e=QT * TP)).then_inc(s_edges, 16)
                    sp.dma_start(w_kv[:], blocks(t["L0_mix_w_qkv"])[:, :, D:3 * D]).then_inc(s_kvw_in, 16)
                    sp.wait_ge(s_zero, 1)
                    fill = slots_x[0:SLOTS * SLOT].rearrange("(p a) d -> p (a d)", p=P)
                    width = 4 * D
                    for c in range(SLOTS // 4):
                        sp.dma_start(fill[:, c * width:(c + 1) * width], zeros[:]).then_inc(s_zfill, 16)
                    spare = slots_y[SLOTS_SURE * SLOT:].rearrange("(p a) d -> p (a d)", p=P)
                    for c in range((SLOTS - SLOTS_SURE) // 4):
                        sp.dma_start(spare[:, c * width:(c + 1) * width], zeros[:]).then_inc(s_zfill, 16)

                @block.gpsimd
                def _(pool):
                    nc.gpsimd.memset(zeros[:], 0.0).then_inc(s_zero, 1)

            def window(eng, w):
                return (eng.value_load(plan_i[w:w + 1, 2:3], min_val=1, max_val=STEPS),
                        eng.value_load(plan_i[w:w + 1, 3:4], min_val=0, max_val=NT * STEPS))

            with nc.Block() as block:
                @block.sync
                def _(sp):
                    sp.wait_ge(s_zfill, 16 * ((2 * SLOTS - SLOTS_SURE) // 4))

                @block.vector
                def _(dve):
                    chain = Chain(dve, dve_n)
                    nc.vector.tensor_copy(select[:], select_f[:].rearrange("k (h p) -> k h p", h=H))
                    nc.vector.memset(zeros16[:], 0.0)
                    chain(nc.vector.memset(ones16[:], 1.0))
                    dve.wait_ge(s_edges, 32)
                    nc.vector.tensor_copy(edge_f[:], edge_i[:]).then_inc(s_edge_f, 1)
                    dve.wait_ge(s_edge_f, 1)
                    chain(nc.vector.tensor_reduce(span[:, 0:1], edge_f[:, 1], AX.X, ALU.min))
                    chain(nc.vector.tensor_reduce(span[:, 1:2], edge_f[:, 1], AX.X, ALU.max))
                    for m in range(2):
                        nc.vector.tensor_scalar(span_w[:, m], ones[0:STEPS, 0:NT], span[:, m:m + 1], None,
                                                ALU.mult).then_inc(s_span, 1)
                    dve.wait_ge(s_spanp, 1)
                    spans = bank[0:NT, 1, :]
                    w_first, w_last = smallc[0:NT, 0:1], smallc[0:NT, 1:2]
                    step_no = smallc[0:NT, 8:8 + STEPS]
                    chain(nc.vector.tensor_scalar(fl1[:], spans[:, P:P + STEPS], w_first, None, ALU.is_ge))
                    chain(nc.vector.scalar_tensor_tensor(fl2[:], spans[:, 0:STEPS], w_last, fl1[:], ALU.is_le, ALU.mult))
                    chain(nc.vector.scalar_tensor_tensor(key[:], step_no, -BIG, fl2[:], ALU.add, ALU.mult))
                    chain(nc.vector.tensor_reduce(plan[:, 0:1], key[:], AX.X, ALU.min))
                    chain(nc.vector.scalar_tensor_tensor(key[:], step_no, 1.0, fl2[:], ALU.add, ALU.mult))
                    chain(nc.vector.tensor_reduce(plan[:, 1:2], key[:], AX.X, ALU.max))
                    chain(nc.vector.tensor_scalar(plan[:, 0:1], plan[:, 0:1], BIG, STEPS - 1.0, ALU.add, ALU.min))
                    chain(nc.vector.tensor_tensor(plan[:, 2:3], plan[:, 1:2], plan[:, 0:1], ALU.subtract))
                    nc.vector.tensor_scalar(plan[:, 2:3], plan[:, 2:3], 1.0, None, ALU.max).then_inc(s_span, 1)
                    dve.wait_ge(s_spanp, 2)
                    chain(nc.vector.tensor_copy(plan[:, 3:4], bank[0:NT, 2, 0:1]))
                    for m in range(2):
                        chain(nc.vector.tensor_copy(edge_c[:, m, :, 0:STEPS], bank[0:TP, 0, :].rearrange(
                            "p (m j u) -> p m j u", m=2, j=QT)[:, m, :, 0:STEPS]))
                    nc.vector.tensor_copy(plan_i[:], plan[:]).then_inc(s_plan, 1)
                    dve.wait_ge(s_plan, 1)
                    for w in range(NT):
                        first = dve.value_load(plan_i[w:w + 1, 0:1], min_val=0, max_val=STEPS - 1)
                        count, base = window(dve, w)
                        with dve.Fori(0, count) as i:
                            for j in range(QT):
                                dve.wait_ge(s_used[j], base + i + 1)
                                nc.vector.tensor_scalar(onehot_src[:, j], iota[0:TP, :],
                                                        edge_c[:, 0, j, bass.ds(first + i, 1)], None,
                                                        ALU.is_equal).then_inc(s_hot[j], 1)
                                nc.vector.tensor_scalar(onehot_dst[:, j], iota[0:TP, w * TP:(w + 1) * TP],
                                                        edge_c[:, 1, j, bass.ds(first + i, 1)], None,
                                                        ALU.is_equal).then_inc(s_hot[j], 1)
                        if w >= 1:
                            k_feature(dve, w - 1)
                    dve.wait_ge(s_adj, NT)
                    nc.vector.tensor_reduce(dmax[:], deg[:], AX.X, ALU.max).then_inc(s_deg, 1)
                    dve.wait_ge(s_all, 1)
                    nc.vector.tensor_reduce(dmax[0:1], bank[0:1, 0, 0:TP], AX.X, ALU.max).then_inc(s_deg, 1)
                    dve.wait_ge(s_deg, 2)
                    nc.vector.tensor_scalar(large_i[:], dmax[0:1], 4095.0, None, ALU.is_gt).then_inc(s_large, 1)

                @block.tensor
                def _(pe):
                    for j in range(QT):
                        pe.sem_inc(s_used[j], 1)
                    pe.wait_ge(s_edge_f, 1)
                    for m in range(2):
                        for j in range(QT):
                            nc.tensor.transpose(bank[0:TP, 0, (QT * m + j) * 64:(QT * m + j) * 64 + STEPS],
                                                edge_f[:, m, j * TP:(j + 1) * TP], ident[0:STEPS, 0:STEPS])
                    pe.wait_ge(s_span, 2)
                    for m in range(2):
                        ins = nc.tensor.matmul(bank[0:NT, 1, m * P:m * P + STEPS], span_w[:, m],
                                               ident[0:STEPS, 0:STEPS], start=True, stop=True)
                    ins.then_inc(s_spanp, 1)
                    pe.wait_ge(s_span, 3)
                    nc.tensor.matmul(bank[0:NT, 2, 0:1], before[0:NT, 0:NT], plan[:, 2:3],
                                     start=True, stop=True).then_inc(s_spanp, 1)
                    pe.wait_ge(s_plan, 1)
                    for w in range(NT):
                        count, base = window(pe, w)
                        if w >= 1:
                            pe.wait_ge(s_adj, w)
                        for b in range(3):
                            nc.tensor.matmul(bank[0:TP, b, :], zeros16[0:TP, 0:TP], zeros16[0:TP, :],
                                             start=True, stop=False, skip_group_check=True)
                        with pe.Fori(0, count) as i:
                            for j in range(QT):
                                pe.wait_ge(s_hot[j], 2 * (base + i) + 2)
                                nc.tensor.matmul(bank[0:TP, 2, 2 * P - 1:2 * P], onehot_dst[:, j], ones16[0:TP, 0:1],
                                                 start=False, stop=False, skip_group_check=True)
                                for s in range(NT):
                                    ins = nc.tensor.matmul(
                                        bank[0:TP, s // 4, (s % 4) * P:(s % 4) * P + TP],
                                        onehot_src[:, j, s * TP:(s + 1) * TP], onehot_dst[:, j],
                                        start=False, stop=False, skip_group_check=True)
                                ins.then_inc(s_used[j], 1)
                        kv_product(pe, w)
                        if w >= 1:
                            kv_sums(pe, w - 1)
                    pe.wait_ge(s_deg, 1)
                    nc.tensor.transpose(bank[0:1, 0, 0:TP], dmax[:], ident[0:TP, 0:TP]).then_inc(s_all, 1)

                @block.gpsimd
                def _(pool):
                    for w in range(NT - 1):
                        k_sum(pool, w)

                @block.scalar
                def _(act):
                    act.wait_ge(s_plan, 1)
                    for w in range(NT):
                        count, base = window(act, w)
                        act.wait_ge(s_used[QT - 1], base + count + 1)
                        win = bank[0:TP, 0:3, :].rearrange("p b (r n) -> p (b r) n", n=P)
                        nc.scalar.copy(adj_t[:, :, w * TP:(w + 1) * TP], win[:, 0:NT, 0:TP])
                        nc.scalar.copy(deg[:, w:w + 1], win[:, NT - 1, P - 1:P]).then_inc(s_adj, 1)
                        if w >= 1:
                            k_exp(act, w - 1)
                        v_copy(act, w)

        with ExitStack() as scope:
            ksum = sb("ksum", [P, KB], scope=scope)
            ksum_z = sb("ksum_z", [P, KB, H], scope=scope)
            kvw = w_proj
            rdeg = sb("rdeg", [TP, NT], scope=scope)
            s_q, s_qf, s_agg, s_aggc, s_z, s_qz = (sem(n) for n in (
                "q_ready", "q_feature", "agg_ready", "agg_copied", "z_spread", "q_scaled"))
            s_zrow, s_zinv, s_zhi, s_zlo = (sem(n) for n in ("z_ready", "z_inverse", "z_high", "z_low"))
            s_ksum, s_adj_12 = sem("k_sum_placed"), sem("counts_rewritten")
            s_kvh, s_kvw, s_kvwc, s_out, s_outc = (sem(n) for n in ("kv_masked", "kvw_ready", "kvw_copied", "out_ready", "out_used"))
            s_bp = sem("bias_added")
            NQ = KB * len(CHUNKS)
            z_banks = (2, 5, 7)

            def rewrite_counts(eng, copy, sources):
                large = eng.value_load(large_i[0:1, 0:1], min_val=0, max_val=1)
                with eng.If_eq(large.val, 0):
                    for s in sources:
                        ins = copy(adj_12[:, s], adj_t[:, s])
                    ins.then_inc(s_adj_12, 1)
                with eng.If_eq(large.val, 1):
                    eng.sem_inc(s_adj_12, 1)

            with nc.Block() as block:
                @block.sync
                def _(sp):
                    sp.dma_start(w_q[:], blocks(t["L0_mix_w_qkv"])[:, :, 0:D]).then_inc(s_w0, 16)
                    for dst, name in ((w_l, "L0_gnn_W_l"), (w_r, "L0_gnn_W_r"), (w_proj, "L0_mix_w_proj")):
                        sp.dma_start(dst[:], blocks(t[name])).then_inc(s_w0, 16)
                    sp.dma_start(gate_w[:], blocks(t["L0_ffn_gate_w"])).then_inc(s_gate_w, 16)
                    sp.dma_start(gate_b[:], t["L0_ffn_gate_b"].partition_broadcast(TP)).then_inc(s_gate_w, 16)
                    for dst, name in ((b_l, "L0_gnn_b_l"), (b_proj, "L0_mix_b_proj")):
                        sp.dma_start(dst[:], t[name].partition_broadcast(TP)).then_inc(s_w0, 16)

                @block.gpsimd
                def _(pool):
                    k_sum(pool, NT - 1)
                    pool.wait_ge(s_w0, 96)
                    for i in range(NT):
                        nc.gpsimd.tensor_tensor(x_res[:, i], x_res[:, i], b_proj[:], ALU.add).then_inc(s_bp, 1)

                @block.tensor
                def _(pe):
                    kv_sums(pe, NT - 1)
                    pe.wait_ge(s_ks, NT)
                    for m in range(KB):
                        ins = nc.tensor.matmul(bank[:, 7, m:m + 1], k_total[:, m * P:(m + 1) * P], ones[0:TP, 0:1],
                                               start=True, stop=True)
                    ins.then_inc(s_acc, 1)
                    pe.wait_ge(s_adj_12, 2)
                    large = pe.value_load(large_i[0:1, 0:1], min_val=0, max_val=1)
                    n = 0
                    for m in range(KB):
                        for a, w in CHUNKS:
                            if n >= 2:
                                pe.wait_ge(s_aggc, n - 1)
                            feats = slice(m * P, (m + 1) * P)

                            def neighbours(adjacency, cast):
                                for s in range(NT):
                                    for k, part in enumerate((xn_hi, xn_lo)):
                                        ins = nc.tensor.matmul(bank[:, n % 2, 0:w], cast(part[0:TP, s, feats]), adjacency[:, s, a:a + w],
                                                               start=s == 0 and k == 0, stop=s == NT - 1 and k == 1)
                                ins.then_inc(s_agg, 1)
                            exact_counts(pe, large, neighbours)
                            n += 1
                    pe.wait_ge(s_w0, 96)
                    n = 0
                    for m in range(KB):
                        for a, w in CHUNKS:
                            if n >= 2:
                                pe.wait_ge(s_qf, n - 1)
                            else:
                                pe.wait_ge(s_aggc, NQ - 1 + n)
                            for b in range(KB):
                                ins = nc.tensor.matmul(bank[:, n % 2, 0:w], w_q[:, b, m * P:(m + 1) * P], xn_c[:, b, a:a + w],
                                                       start=b == 0, stop=b == KB - 1)
                            ins.then_inc(s_q, 1)
                            n += 1

                    pe.wait_ge(s_ksum, 1)
                    pe.wait_ge(s_qf, NQ)
                    for c, (a, w) in enumerate(CHUNKS):
                        for m in range(KB):
                            ins = nc.tensor.matmul(bank[0:H, z_banks[c], 0:w], ksum_z[:, m], q_c[:, m, a:a + w],
                                                   start=m == 0, stop=m == KB - 1)
                        ins.then_inc(s_zrow, 1)
                    pe.wait_ge(s_kvh, 1)
                    for m in range(KB):
                        if m >= 2:
                            pe.wait_ge(s_kvwc, m - 1)
                        nc.tensor.matmul(bank[:, 3 + m % 2, :], kv_h[:, m], w_proj[:, m], start=True, stop=True).then_inc(s_kvw, 1)

                    def tile_products(i, parts):
                        o = 3 * (i % 2)
                        tok = slice(i * TP, (i + 1) * TP)
                        for g, left, right in parts:
                            for b in range(KB):
                                ins = nc.tensor.matmul(bank[0:TP, o + g, :], left[:, b, tok], right[:, b],
                                                       start=b == 0, stop=b == KB - 1)
                        return ins
                    graph_parts, attention_part = ((0, agg, w_l), (1, xn_c, w_r)), ((2, q_c, kvw),)
                    pe.wait_ge(s_aggc, NQ)
                    tile_products(0, graph_parts)
                    pe.wait_ge(s_zlo, len(CHUNKS))
                    n = 0
                    for c, (a, w) in enumerate(CHUNKS):
                        for m in range(KB):
                            if n >= 2:
                                pe.wait_ge(s_qz, n - 1)
                            for k, part in enumerate((zi_hi, zi_lo)):
                                ins = nc.tensor.matmul(bank[:, 6 + n % 2, 0:w], select[0:H, m], part[:, a:a + w],
                                                       start=k == 0, stop=k == 1)
                            ins.then_inc(s_z, 1)
                            n += 1
                        if c == 0:
                            pe.wait_ge(s_kvwc, KB)
                            tile_products(1, graph_parts)
                    turned = 0
                    for i in range(NT):
                        if i >= HALF + 2:
                            for _ in range(2):
                                if turned < HALF:
                                    norm_turn(pe, 1, turned, rows1)
                                    turned += 1
                        if i >= 2:
                            pe.wait_ge(s_outc, i - 1)
                            tile_products(i, graph_parts)
                        pe.wait_ge(s_qz, KB * min(len(CHUNKS), i * TP // CHUNKS[0][1] + 1))
                        tile_products(i, attention_part).then_inc(s_out, 1)
                    pe.wait_ge(s_gate_w, 32)
                    pe.wait_ge(s_outc, NT - 1)
                    for c, (a, w) in enumerate(CHUNKS):
                        while turned * TP < a + w:
                            norm_turn(pe, 1, turned, rows1)
                            turned += 1
                        pe.wait_ge(s_evac, NT + (a + w) // TP)
                        for b in range(KB):
                            ins = nc.tensor.matmul(bank[0:E0, c, 0:w], gate_w[:, b], xn_c[:, b, a:a + w],
                                                   start=b == 0, stop=b == KB - 1)
                        ins.then_inc(s_lgc, 1)

                @block.vector
                def _(dve):
                    chain = Chain(dve, dve_n)
                    chain(nc.vector.tensor_scalar(rdeg[:], deg[:], 1.0, None, ALU.max))
                    nc.vector.reciprocal(rdeg[:], rdeg[:]).then_inc(dve_n.sem, 1)
                    dve_n.n += 1
                    k_feature(dve, NT - 1)
                    rewrite_counts(dve, nc.vector.tensor_copy, range(4, NT))
                    chain(nc.vector.memset(ksum_z[:], 0.0))
                    dve.wait_ge(s_acc, NT + 1)
                    chain(nc.vector.tensor_copy(ksum[:], bank[:, 7, 0:KB]))
                    for m in range(KB):
                        ins = nc.vector.tensor_scalar(ksum_z[:, m, 2 * m:2 * m + 2], headmask[:, 0:P:HD], ksum[:, m:m + 1], None,
                                                      ALU.mult)
                    ins.then_inc(s_ksum, 1)
                    n = 0
                    for m in range(KB):
                        for a, w in CHUNKS:
                            dve.wait_ge(s_q, n + 1)
                            nc.vector.tensor_scalar(qtmp[:, n % 2, 0:w], bank[:, n % 2, 0:w], 0.0, None, ALU.min).then_inc(s_min, 1)
                            dve.wait_ge(s_exp, NT + n + 1)
                            nc.vector.scalar_tensor_tensor(q_c[:, m, a:a + w], bank[:, n % 2, 0:w], 0.0, qtmp[:, n % 2, 0:w],
                                                           ALU.max, ALU.add).then_inc(s_qf, 1)
                            n += 1
                    for m in range(KB):
                        ins = nc.vector.tensor_tensor(kv_h[:, m], bank[:, 6, m * P:(m + 1) * P], headmask[:], ALU.mult)
                    ins.then_inc(s_kvh, 1)
                    for c, (a, w) in enumerate(CHUNKS):
                        dve.wait_ge(s_zrow, c + 1)
                        chain(nc.vector.tensor_scalar(zinv[:, a:a + w], bank[0:H, z_banks[c], 0:w], EPS_ATT, None, ALU.add))
                        nc.vector.reciprocal(zinv[:, a:a + w], zinv[:, a:a + w]).then_inc(s_zinv, 1)
                    for c, (a, w) in enumerate(CHUNKS):
                        dve.wait_ge(s_zhi, c + 1)
                        nc.vector.tensor_tensor(zi_lo[:, a:a + w], zinv[:, a:a + w], zi_hi[:, a:a + w].bitcast(F32),
                                                ALU.subtract).then_inc(s_zlo, 1)
                    dve.wait_ge(s_qf, NQ)
                    n = 0
                    for a, w in CHUNKS:
                        for m in range(KB):
                            dve.wait_ge(s_z, n + 1)
                            nc.vector.tensor_tensor(q_c[:, m, a:a + w], q_c[:, m, a:a + w], bank[:, 6 + n % 2, 0:w],
                                                    ALU.mult).then_inc(s_qz, 1)
                            n += 1
                    def out_tile(i):
                        o = 3 * (i % 2)
                        dve.wait_ge(s_out, i + 1)
                        dve.wait_ge(s_bp, i + 1)
                        y = qtmp[0:TP, i % 2]
                        chain(nc.vector.tensor_tensor(y, bank[0:TP, o + 1, :], b_l[:], ALU.add))
                        chain(nc.vector.scalar_tensor_tensor(y, bank[0:TP, o, :], rdeg[:, i:i + 1], y, ALU.mult, ALU.add))
                        chain(nc.vector.scalar_tensor_tensor(x_res[:, i], y, 0.0, x_res[:, i], ALU.max, ALU.add))
                        nc.vector.tensor_tensor(x_res[:, i], x_res[:, i], bank[0:TP, o + 2, :], ALU.add).then_inc(s_outc, 1)
                    for c in range(2):
                        for i in range(c * HALF, (c + 1) * HALF):
                            out_tile(i)
                            dve.wait_ge(s_outc, i + 1)
                            ins = norm_stats(dve, 1, i)
                        chain(ins)
                        norm_variance(c)
                        norm_apply(dve, chain, 1, c, rows1)

                @block.scalar
                def _(act):
                    k_exp(act, NT - 1)
                    rewrite_counts(act, nc.scalar.copy, range(4))
                    n = 0
                    for m in range(KB):
                        for a, w in CHUNKS:
                            act.wait_ge(s_agg, n + 1)
                            nc.scalar.copy(agg[:, m, a:a + w], bank[:, n % 2, 0:w]).then_inc(s_aggc, 1)
                            n += 1
                    n = 0
                    for m in range(KB):
                        for a, w in CHUNKS:
                            act.wait_ge(s_min, NT + n + 1)
                            nc.scalar.activation(qtmp[:, n % 2, 0:w], qtmp[:, n % 2, 0:w], ACT.Exp).then_inc(s_exp, 1)
                            n += 1
                    for m in range(KB):
                        act.wait_ge(s_kvw, m + 1)
                        nc.scalar.copy(kvw[:, m], bank[:, 3 + m % 2, :]).then_inc(s_kvwc, 1)
                    for c, (a, w) in enumerate(CHUNKS):
                        act.wait_ge(s_zinv, c + 1)
                        nc.scalar.copy(zi_hi[:, a:a + w], zinv[:, a:a + w]).then_inc(s_zhi, 1)
                    for c in range(2):
                        norm_root(act, 1, c)
                        for i in range(c * HALF, (c + 1) * HALF):
                            norm_columns(act, 1, i, rows1, xn_c)

        with ExitStack() as moe:
            table_i = sb("table_i", [1, 2, E0 + 1], I32, scope=moe)
            w1_sb = place("w1_sb", [P, 2, KB, F0], 40 * K)
            w2_sb = place("w2_sb", [P, 2, FB, D], 72 * K)
            b2_sb = place("b2_sb", [P, 2, D], 104 * K)
            b1_sb = place("b1_sb", [P, 2, FB], 108 * K)
            s_w = [sem(f"expert_loaded_{e}") for e in range(E0)]
            s_hd, s_gelu, s_yd, s_ye, s_yst, s_xl, s_xt, s_xr = (sem(n) for n in (
                "hidden_ready", "gelu_ready", "y_ready", "y_added", "y_stored", "slot_loaded", "slot_turned", "slot_columns"))

            def read_table(eng):
                eng.wait_ge(s_table, 1)
                return [(eng.value_load(table_i[0:1, 0, e:e + 1], min_val=1, max_val=NT),
                         eng.value_load(table_i[0:1, 1, e:e + 1], min_val=0, max_val=SLOTS - 1)) for e in range(E0)]

            tables = {}
            s_table = sem("table_ready")

            def load_expert(eng, e):
                q = e % 2
                eng.dma_start(w1_sb[:, q], blocks(t["L0_ffn_w1"][e])).then_inc(s_w[e], 16)
                eng.dma_start(w2_sb[:, q], blocks(t["L0_ffn_w2"][e])).then_inc(s_w[e], 16)
                eng.dma_start(b1_sb[:, q], t["L0_ffn_b1"][e]).then_inc(s_w[e], 16)
                eng.dma_start(b2_sb[:, q], t["L0_ffn_b2"][e].partition_broadcast(P)).then_inc(s_w[e], 16)

            with ExitStack() as scope:
                room_used[0] = 25 * K

                def gate_scratch(name, shape, dt=F32):
                    return scratch(name, shape, dt, end=40 * K)
                pr, ex, oh1, oh2, ky, p2, m01, rank = (gate_scratch(n, [TP, NT, E0]) for n in (
                    "probs", "eq", "first_hot", "second_hot", "keys", "probs_2", "chosen", "rank"))
                mx, sm, r1, r2 = (gate_scratch(n, [TP, NT]) for n in ("mx", "sm", "r1", "r2"))
                tot = gate_scratch("tot", [TP, NT + 1, E0])
                gt = gate_scratch("gt", [TP, E0, NT])
                tbl = gate_scratch("tbl", [TP, 2, E0 + 1])
                slot_row = gate_scratch("slot_row", [TP, 2, NT])
                s_lg, s_oh, s_pre, s_pl, s_sc = (sem(n) for n in ("logits_ready", "chosen_ready", "counts_ready", "places_ready", "scattered"))

                logits_c = gate_scratch("logits_c", [E0, N])
                s_lgs = sem("logit_columns_kept")

                with nc.Block() as block:
                    @block.sync
                    def _(sp):
                        load_expert(sp, 0)
                        tables["sp"] = read_table(sp)

                    @block.tensor
                    def _(pe):
                        for c, (a, w) in enumerate(CHUNKS):
                            pe.wait_ge(s_lgs, c + 1)
                            for i in range(a // TP, (a + w) // TP):
                                ins = nc.tensor.transpose(bank[0:TP, 6, i * E0:(i + 1) * E0], logits_c[:, i * TP:(i + 1) * TP],
                                                          ident[0:E0, 0:E0])
                        ins.then_inc(s_lg, 1)
                        pe.wait_ge(s_oh, 2)
                        hot = m01[:].rearrange("p t e -> p (t e)")
                        nc.tensor.matmul(bank[0:TP, 1, 0:NT * E0], before[0:TP, 0:TP], hot, start=True, stop=True)
                        nc.tensor.matmul(bank[0:TP, 2, 0:NT * E0], ones[0:TP, 0:TP], hot, start=True, stop=True).then_inc(s_pre, 1)
                        tables["pe"] = read_table(pe)

                    @block.vector
                    def _(dve):
                        chain = Chain(dve, dve_n)
                        V = nc.vector
                        full = [TP, NT, E0]

                        def over_e(a):
                            return a.unsqueeze(2).to_broadcast(full)

                        def over_t(a):
                            return a.unsqueeze(1).to_broadcast(full)
                        iota_e = over_t(smallc[0:TP, 128:128 + E0])
                        for c, (a, w) in enumerate(CHUNKS):
                            dve.wait_ge(s_lgc, c + 1)
                            nc.vector.tensor_copy(logits_c[:, a:a + w], bank[0:E0, c, 0:w]).then_inc(s_lgs, 1)
                        dve.wait_ge(s_gate_w, 32)
                        dve.wait_ge(s_lg, 1)
                        lg = bank[0:TP, 6, 0:NT * E0].rearrange("p (t e) -> p t e", e=E0)
                        chain(V.tensor_tensor(pr[:], lg, over_t(gate_b[:]), ALU.add))
                        chain(V.tensor_reduce(mx[:], pr[:], AX.X, ALU.max))
                        V.tensor_tensor(pr[:], pr[:], over_e(mx[:]), ALU.subtract).then_inc(s_oh, 1)
                        dve.wait_ge(act_n.sem, act_n.n + 1)
                        chain(V.tensor_reduce(sm[:], pr[:], AX.X, ALU.add))
                        chain(V.reciprocal(sm[:], sm[:]))
                        chain(V.tensor_tensor(pr[:], pr[:], over_e(sm[:]), ALU.mult))

                        def pick(probs, best, hot):
                            chain(V.tensor_reduce(best, probs, AX.X, ALU.max))
                            chain(V.tensor_tensor(ex[:], probs, over_e(best), ALU.is_equal))
                            chain(V.scalar_tensor_tensor(ky[:], ex[:], -float(E0), iota_e, ALU.mult, ALU.add))
                            chain(V.tensor_reduce(mx[:], ky[:], AX.X, ALU.min))
                            chain(V.tensor_tensor(hot, ky[:], over_e(mx[:]), ALU.is_equal))
                        pick(pr[:], r1[:], oh1[:])
                        chain(V.scalar_tensor_tensor(p2[:], oh1[:], -2.0, pr[:], ALU.mult, ALU.add))
                        pick(p2[:], r2[:], oh2[:])
                        V.tensor_tensor(m01[:], oh1[:], oh2[:], ALU.add).then_inc(s_oh, 1)
                        chain(V.tensor_tensor(sm[:], r1[:], r2[:], ALU.add))
                        chain(V.reciprocal(sm[:], sm[:]))
                        chain(V.tensor_tensor(choice[:, 0], r1[:], sm[:], ALU.mult))
                        chain(V.tensor_tensor(choice[:, 1], r2[:], sm[:], ALU.mult))
                        chain(V.memset(tot[:, 0], 0.0))
                        dve.wait_ge(s_pre, 1)
                        for i in range(NT):
                            chain(V.tensor_tensor(tot[:, i + 1], tot[:, i], bank[0:TP, 2, i * E0:(i + 1) * E0], ALU.add))
                        steps = smallc[0:TP, 144:144 + NT].unsqueeze(1).to_broadcast([TP, E0, NT])
                        chain(V.tensor_tensor(gt[:], tot[:, NT].unsqueeze(2).to_broadcast([TP, E0, NT]), steps, ALU.is_gt))
                        chain(V.tensor_reduce(tbl[:, 0, 0:E0], gt[:], AX.X, ALU.add))
                        chain(V.tensor_scalar(tbl[:, 0, 0:E0], tbl[:, 0, 0:E0], 1.0, None, ALU.max))
                        chain(V.memset(tbl[:, 1, 0:1], 0.0))
                        chain(V.memset(tbl[:, 0, E0:E0 + 1], 0.0))
                        for e in range(E0):
                            chain(V.tensor_tensor(tbl[:, 1, e + 1:e + 2], tbl[:, 1, e:e + 1], tbl[:, 0, e:e + 1], ALU.add))
                        V.tensor_copy(table_i[:], tbl[0:1]).then_inc(s_table, 1)
                        pre = bank[0:TP, 1, 0:NT * E0].rearrange("p (t e) -> p t e", e=E0)
                        chain(V.tensor_tensor(rank[:], tot[:, 0:NT], pre, ALU.add))
                        chain(V.scalar_tensor_tensor(rank[:], over_t(tbl[:, 1, 0:E0]), float(SLOT), rank[:], ALU.mult, ALU.add))
                        for c, hot in enumerate((oh1, oh2)):
                            chain(V.tensor_tensor(ky[:], hot[:], rank[:], ALU.mult))
                            chain(V.tensor_reduce(slot_row[:, c], ky[:], AX.X, ALU.add))
                        V.tensor_copy(place_i[:], slot_row[:]).then_inc(s_pl, 1)
                        tables["dve"] = read_table(dve)

                    @block.scalar
                    def _(act):
                        act.wait_ge(s_oh, 1)
                        act_n.add(nc.scalar.activation(pr[:], pr[:], ACT.Exp))
                        tables["act"] = read_table(act)

                    @block.gpsimd
                    def _(pool):
                        pool.wait_ge(s_pl, 1)
                        for i in range(NT):
                            for c in range(2):
                                pool.indirect_dma_start(
                                    out=slots_x, out_offset=bass.IndirectOffsetOnAxis(ap=place_i[:, c, i:i + 1], axis=0),
                                    in_=rows1[:, i], in_offset=None).then_inc(s_sc, 16)
                        tables["pool"] = read_table(pool)
                        pool.wait_ge(s_sc, 16 * 2 * NT)

            with ExitStack() as scope:
                s_free, s_stored = sem("expert_buffers_free"), sem("results_stored")
                slot_r = place("slot_r", [P, D], 32 * K)
                slot_c = place("slot_c", [P, KB, P], 34 * K)
                hid = place("hid", [P, FB, P], 36 * K)
                hid_hi, hid_lo = (place(n, [P, FB, P], (109 + 4 * i) * K, F32R) for i, n in enumerate(("hid_hi", "hid_lo")))
                w2_hi = place("w2_hi", [P, 2, FB, D], 0, F32R)
                w2_lo = place("w2_lo", [P, 2, FB, D], 72 * K, F32R)
                s_hhi, s_hlo, s_whi, s_wlo = (sem(n) for n in ("hidden_high", "hidden_low", "w2_high", "w2_low"))
                y_sb = place("y_sb", [P, D], 117 * K)
                hid_p = bank[:, 4:8, 0:P]
                turn_p = bank[:, 2, :].rearrange("p (b n) -> p b n", b=KB)
                y_p = bank[:, 3, :]

                def slot_rows(dram, g):
                    if not isinstance(g, int):
                        g = nc.s_assert_within(g, 0, SLOTS - 1, skip_runtime_bounds_check_because=(
                            "the experts' slots number SLOTS - 1 at most, as their sizes sum to 2 N"))
                    return dram.rearrange("(s p) d -> s p d", p=SLOT)[bass.ds(g, 1)].rearrange("a p d -> (a p) d")

                with nc.Block() as block:
                    @block.gpsimd
                    def _(pool):
                        def w2_low(e):
                            for f in range(FB):
                                pool.wait_ge(s_whi, e * FB + f + 1)
                                nc.gpsimd.tensor_tensor(w2_lo[:, e % 2, f], w2_sb[:, e % 2, f], w2_hi[:, e % 2, f].bitcast(F32),
                                                        ALU.subtract).then_inc(s_wlo, 1)

                        w2_low(0)
                        table = tables["pool"]
                        for e in range(1, E0):
                            w2_low(e)
                            if e + 1 < E0:
                                count, base = table[e - 1]
                                pool.wait_ge(s_ye, base + count + 1)
                                pool.sem_inc(s_free, 1)
                                pool.wait_ge(s_free, e)
                                load_expert(pool, e + 1)

                    @block.sync
                    def _(sp):
                        sp.sem_inc(s_yst, 16)
                        sp.dma_start(slot_r[:], slot_rows(slots_x, 0)).then_inc(s_xl, 16)
                        load_expert(sp, 1)
                        table = tables["sp"]
                        for e in range(E0):
                            count, base = table[e]
                            with sp.Fori(0, count) as i:
                                g = base + i
                                sp.wait_ge(s_xt, g + 1)
                                sp.dma_start(slot_r[:], slot_rows(slots_x, g + 1)).then_inc(s_xl, 16)
                                sp.wait_ge(s_ye, g + 2)
                                sp.dma_start(slot_rows(slots_y, g), y_sb[:]).then_inc(s_yst, 16)
                        total = sp.value_load(table_i[0:1, 1, E0:E0 + 1], min_val=E0, max_val=SLOTS - 1)
                        sp.wait_ge(s_yst, 16 * total + 16)
                        sp.sem_inc(s_stored, 1)
                        sp.wait_ge(s_stored, 1)

                    @block.tensor
                    def _(pe):
                        def turn(g):
                            pe.wait_ge(s_xl, 16 * (g + 1))
                            for b in range(KB):
                                ins = nc.tensor.transpose(turn_p[:, b], slot_r[:, b * P:(b + 1) * P], ident[:])
                            ins.then_inc(s_xt, 1)

                        turn(0)
                        table = tables["pe"]
                        pe.sem_inc(s_yd, 1)
                        for e in range(E0):
                            q = e % 2
                            pe.wait_ge(s_w[e], 64)
                            count, base = table[e]
                            with pe.Fori(0, count) as i:
                                g = base + i
                                pe.wait_ge(s_xr, g + 1)
                                for f in range(FB):
                                    if f >= 4:
                                        pe.wait_ge(s_gelu, g * FB + f - 3)
                                    for b in range(KB):
                                        ins = nc.tensor.matmul(hid_p[:, f % 4], w1_sb[:, q, b, f * P:(f + 1) * P], slot_c[:, b],
                                                               start=b == 0, stop=b == KB - 1)
                                    ins.then_inc(s_hd, 1)
                                turn(g + 1)
                                pe.wait_ge(s_ye, g + 1)
                                for f in range(FB):
                                    pe.wait_ge(s_wlo, e * FB + f + 1)
                                    pe.wait_ge(s_hlo, g * FB + f + 1)
                                    for k, (left, right) in enumerate(((hid_hi, w2_hi), (hid_lo, w2_hi), (hid_hi, w2_lo))):
                                        ins = nc.tensor.matmul(y_p, left[:, f], right[:, q, f], start=f == 0 and k == 0,
                                                               stop=f == FB - 1 and k == 2)
                                ins.then_inc(s_yd, 1)

                    @block.scalar
                    def _(act):
                        def w2_high(e):
                            act.wait_ge(s_w[e], 64)
                            for f in range(FB):
                                nc.scalar.copy(w2_hi[:, e % 2, f], w2_sb[:, e % 2, f]).then_inc(s_whi, 1)

                        w2_high(0)
                        table = tables["act"]
                        for e in range(E0):
                            q = e % 2
                            count, base = table[e]
                            with act.Fori(0, count) as i:
                                g = base + i
                                act.wait_ge(s_yd, g + 1)
                                for f in range(FB):
                                    act.wait_ge(s_hd, g * FB + f + 1)
                                    nc.scalar.activation(hid[:, f], hid_p[:, f % 4], ACT.Gelu,
                                                         bias=b1_sb[:, q, f:f + 1]).then_inc(s_gelu, 1)
                            if e + 1 < E0:
                                w2_high(e + 1)

                    @block.vector
                    def _(dve):
                        dve.sem_inc(s_ye, 1)
                        dve.wait_ge(s_xt, 1)
                        nc.vector.tensor_copy(slot_c[:], turn_p).then_inc(s_xr, 1)
                        table = tables["dve"]
                        for e in range(E0):
                            q = e % 2
                            dve.wait_ge(s_w[e], 64)
                            count, base = table[e]
                            with dve.Fori(0, count) as i:
                                g = base + i
                                for f in range(FB):
                                    dve.wait_ge(s_gelu, g * FB + f + 1)
                                    nc.vector.tensor_copy(hid_hi[:, f], hid[:, f]).then_inc(s_hhi, 1)
                                    dve.wait_ge(s_hhi, g * FB + f + 1)
                                    nc.vector.tensor_tensor(hid_lo[:, f], hid[:, f], hid_hi[:, f].bitcast(F32),
                                                            ALU.subtract).then_inc(s_hlo, 1)
                                dve.wait_ge(s_xt, g + 2)
                                nc.vector.tensor_copy(slot_c[:], turn_p).then_inc(s_xr, 1)
                                dve.wait_ge(s_yd, g + 2)
                                dve.wait_ge(s_yst, 16 * g + 16)
                                nc.vector.tensor_tensor(y_sb[:], y_p, b2_sb[:, q], ALU.add).then_inc(s_ye, 1)

        layer0.close()

        with ExitStack() as layer1:
            qi = sb("qi", [P, H * N], scope=layer1)
            qi_h = qi[:].rearrange("p (h n) -> p h n", h=H)
            wqkv1 = qi[:, 0:KB * 3 * D].rearrange("p (b n) -> p b n", b=KB)
            w_out = sb("w_out", [P, KB, D], scope=layer1)
            bias_c = sb("bias_c", [P, H + KB], scope=layer1)
            s_w1l, s_wg = sem("layer1_mix_weights"), sem("layer1_gnn_weights")

            xn_c = sb("xn_c2", [P, KB, N], scope=layer1)
            place1 = arena("row_room", 4 * NT * D, layer1)
            xn_rows = place1("xn_rows2", [TP, NT, D], 0)
            xw_hi = place1("xw_hi", [P, NT, D], 0, F32R)
            r_c = place1("r_c", [P, KB, N], 0)

            with ExitStack() as scope:
                w_g = sb("w_g", [P, KB, D], scope=scope)
                w_t = sb("w_t", [P, 2, D], scope=scope)
                t_emb = sb("t_emb", [P, 2], scope=scope)
                t_rep = sb("t_rep", [P, 2, TP], scope=scope)
                bias3 = sb("bias3", [TP, 3, D], scope=scope)
                bias_r = sb("bias_r", [TP, D], scope=scope)
                dinv = sb("dinv", [TP, NT], scope=scope)
                place_lo = arena("xw_lo_room", 4 * NT * D, scope)
                xw_lo = place_lo("xw_lo", [P, NT, D], 0, F32R)
                got = place_lo("got", [TP, 4, D], 4 * (NT - 4) * D)
                s_got = [sem(f"gathered_{q}") for q in range(4)]
                s_mix = sem("gathered_used")
                utmp = bias3
                LAG = 3
                s_xws, s_xwh = sem("xw_scaled"), sem("xw_high")
                s_dinv, s_te, s_xw, s_xwc, s_hop, s_hopc, s_trep, s_b3 = (sem(n) for n in (
                    "dinv_ready", "time_ready", "xw_ready", "xw_copied", "hop_ready", "hop_used", "time_repeated", "bias_summed"))
                with nc.Block() as block:
                    @block.gpsimd
                    def _(pool):
                        for n in range(2 * NT):
                            i, c = n // 2, n % 2
                            if n >= 4:
                                pool.wait_ge(s_mix, n - 3)
                            pool.indirect_dma_start(
                                out=got[:, n % 4], out_offset=None, in_=slots_y,
                                in_offset=bass.IndirectOffsetOnAxis(ap=place_i[:, c, i:i + 1], axis=0)).then_inc(s_got[n % 4], 16)

                    @block.vector
                    def _(dve):
                        chain = Chain(dve, dve_n)
                        nc.vector.tensor_scalar(rs_var[:], deg[:], 1.0, None, ALU.add).then_inc(s_dinv, 1)
                        dve.wait_ge(s_dinv, 2)
                        refine_rsqrt(chain, dinv[:], rs_var[:], rs_root[:], rs_tmp[:])
                        for c in range(2):
                            for i in range(c * HALF, (c + 1) * HALF):
                                for n in (2 * i, 2 * i + 1):
                                    dve.wait_ge(s_got[n % 4], 16 * (n // 4 + 1))
                                    nc.vector.scalar_tensor_tensor(x_res[:, i], got[:, n % 4], choice[:, n % 2, i:i + 1], x_res[:, i],
                                                                   ALU.mult, ALU.add).then_inc(s_mix, 1)
                                    dve.wait_ge(s_mix, n + 1)
                                ins = norm_stats(dve, 2, i)
                            chain(ins)
                            norm_variance(c)
                            norm_apply(dve, chain, 2, c, xn_rows)
                            if c == 0:
                                dve.wait_ge(s_wg, 96)
                                nc.vector.tensor_scalar(t_rep[:, 0], ones[:, 0:TP], t_emb[:, 0:1], None, ALU.mult)
                                nc.vector.tensor_scalar(t_rep[:, 1], ones[:, 0:TP], t_emb[:, 1:2], None, ALU.mult).then_inc(s_trep, 1)
                                chain(nc.vector.tensor_tensor(bias_r[:], bias3[:, 0], bias3[:, 1], ALU.add))
                                nc.vector.tensor_tensor(bias_r[:], bias_r[:], bias3[:, 2], ALU.add).then_inc(s_b3, 1)
                        for i in range(NT):
                            dve.wait_ge(s_xwh, i + 1)
                            nc.vector.tensor_tensor(xw_lo[0:TP, i], utmp[:, i % 2], xw_hi[0:TP, i].bitcast(F32),
                                                    ALU.subtract).then_inc(s_xwc, 1)

                    @block.tensor
                    def _(pe):
                        def xw_product(i):
                            pe.wait_ge(s_evac, 2 * NT + i + 1)
                            if i >= 4:
                                pe.wait_ge(s_xws, i - 3)
                            for b in range(KB):
                                ins = nc.tensor.matmul(bank[0:TP, 2 + i % 4, :], xn_c[:, b, i * TP:(i + 1) * TP], w_g[:, b],
                                                       start=b == 0, stop=b == KB - 1)
                            ins.then_inc(s_xw, 1)
                        for i in range(HALF):
                            norm_turn(pe, 2, i, xn_rows)
                        pe.wait_ge(s_wg, 96)
                        for i in range(LAG):
                            xw_product(i)
                        for i in range(HALF, NT):
                            norm_turn(pe, 2, i, xn_rows)
                            xw_product(i - HALF + LAG)
                        for i in range(HALF + LAG, NT):
                            xw_product(i)

                    @block.scalar
                    def _(act):
                        def xw_scaled(i):
                            act.wait_ge(s_xw, i + 1)
                            if i >= 2:
                                act.wait_ge(s_xwc, i - 1)
                            nc.scalar.activation(utmp[:, i % 2], bank[0:TP, 2 + i % 4, :], ACT.Copy, scale=dinv[:, i:i + 1]).then_inc(s_xws, 1)
                            act.wait_ge(s_xws, i + 1)
                            nc.scalar.copy(xw_hi[0:TP, i], utmp[:, i % 2]).then_inc(s_xwh, 1)
                        act.wait_ge(s_dinv, 1)
                        nc.scalar.activation(rs_root[:], rs_var[:], ACT.Sqrt).then_inc(s_dinv, 1)
                        norm_root(act, 2, 0)
                        for i in range(HALF):
                            norm_columns(act, 2, i, xn_rows, xn_c)
                        norm_root(act, 2, 1)
                        act.wait_ge(s_b3, 1)
                        for i in range(2):
                            xw_scaled(i)
                        for i in range(HALF, NT):
                            norm_columns(act, 2, i, xn_rows, xn_c)
                            xw_scaled(i - HALF + 2)
                        for i in range(HALF + 2, NT):
                            xw_scaled(i)

                    @block.sync
                    def _(sp):
                        sp.dma_start(w_g[:], blocks(t["L1_gnn_W"])).then_inc(s_wg, 16)
                        sp.dma_start(w_t[:], blocks(t["L1_gnn_Wt"])).then_inc(s_wg, 16)
                        sp.dma_start(t_emb[:], t["L1_gnn_t_emb"]).then_inc(s_wg, 16)
                        for c, name in enumerate(("L1_gnn_b", "L1_gnn_bt", "L1_mix_b_out")):
                            sp.dma_start(bias3[:, c], t[name].partition_broadcast(TP)).then_inc(s_wg, 16)
                        sp.wait_ge(s_mix, 2 * NT - 2)
                        sp.dma_start(wqkv1, blocks(t["L1_mix_W_qkv"])).then_inc(s_w1l, 16)
                        sp.dma_start(w_out[:], blocks(t["L1_mix_W_out"])).then_inc(s_w1l, 16)
                        sp.dma_start(bias_c[:], t["L1_mix_b_qkv"]).then_inc(s_w1l, 16)

                with nc.Block() as block:
                    @block.tensor
                    def _(pe):
                        pe.wait_ge(s_trep, 1)
                        for b in range(2):
                            ins = nc.tensor.matmul(bank[0:TP, 2, :], t_rep[:, b], w_t[:, b], start=b == 0, stop=b == 1)
                        ins.then_inc(s_te, 1)
                        large = pe.value_load(large_i[0:1, 0:1], min_val=0, max_val=1)
                        pe.wait_ge(s_xwc, NT)
                        for i in range(NT):
                            if i >= 2:
                                pe.wait_ge(s_hopc, i - 1)
                            def neighbours(adjacency, cast):
                                for s in range(NT):
                                    for k, part in enumerate((xw_hi, xw_lo)):
                                        ins = nc.tensor.matmul(bank[0:TP, 3 + i % 2, :], adjacency[:, s, i * TP:(i + 1) * TP],
                                                               cast(part[0:TP, s]), start=s == 0 and k == 0, stop=s == NT - 1 and k == 1)
                                ins.then_inc(s_hop, 1)
                            exact_counts(pe, large, neighbours)

                    @block.vector
                    def _(dve):
                        chain = Chain(dve, dve_n)
                        dve.wait_ge(s_te, 1)
                        chain(nc.vector.tensor_tensor(bias_r[:], bias_r[:], bank[0:TP, 2, :], ALU.add))
                        for i in range(NT):
                            chain(nc.vector.tensor_tensor(x_res[:, i], x_res[:, i], bias_r[:], ALU.add))
                        dve.wait_ge(s_xwc, NT)
                        for i in range(NT):
                            dve.wait_ge(s_hop, i + 1)
                            y = utmp[:, i % 2]
                            chain(nc.vector.tensor_tensor(y, bank[0:TP, 3 + i % 2, :], xw_hi[0:TP, i].bitcast(F32), ALU.add))
                            chain(nc.vector.tensor_tensor(y, y, xw_lo[0:TP, i].bitcast(F32), ALU.add))
                            nc.vector.scalar_tensor_tensor(x_res[:, i], y, dinv[:, i:i + 1], x_res[:, i],
                                                           ALU.mult, ALU.add).then_inc(s_hopc, 1)
                        dve.wait_ge(s_hopc, NT)

            with ExitStack() as scope:
                NC5, CW = 5, 250
                qk = sb("qk", [P, H, N], scope=scope)
                kv = adj[:, 0:H * N].rearrange("p (g h s) -> p g h s", g=GROUPS, h=H)
                free = xn_c[:].rearrange("p b n -> p (b n)")
                pm_sb = free[:, 0:2 * BATCH * GW].rearrange("p (q n) -> p q n", q=2)
                H2, NC = 2 * H, len(CHUNKS)
                ROW = NT * D
                assert 4 * N <= ROW and ROW % 32 == 0
                row_hi, row_lo = (place1(n, [H2, N], i * ROW, F32R) for i, n in enumerate(("row_hi", "row_lo")))
                ex_hat, sig_hat = (place1(n, [H2, N], i * ROW) for i, n in ((2, "ex_hat"), (3, "sig_hat")))
                sums, sums2, sw = (sb(n, [P, H], scope=scope) for n in ("sums", "sums2", "sw"))
                sw2 = sb("sw2", [P, H * (H2 + 2)], scope=scope)
                inv = ex_hat
                mx3, sm3 = (sb(n, [H2, NC], scope=scope) for n in ("mx3", "sm3"))
                nmax, norm = (sb(n, [H2, 1], scope=scope) for n in ("nmax", "norm"))
                vg_sb = sb("vg_sb", [P, 2, BATCH * HD], scope=scope)
                swap = sb("swap", [P, P], scope=scope)
                (s_qk, s_qkc, s_v, s_vcp, s_sw, s_swr, s_lh, s_io, s_ioc, s_hat, s_sig, s_mx, s_ex, s_kt,
                 s_swap, s_rows, s_inv, s_hi, s_lo, s_fac,
                 s_pm, s_pmc, s_vgc, s_r, s_rc, s_o, s_oc) = (sem(n) for n in (
                     "qk_ready", "qk_sigmoid", "v_ready", "v_biased", "sums_swapped", "sums_ready", "heads_ready", "io_ready",
                     "io_used", "hat_ready", "sig_ready", "max_ready", "exp_hat_ready", "q_k_weighted",
                     "swap_made", "token_sums", "inverses_ready", "rows_high", "rows_low", "factors_ready",
                     "pm_ready", "pm_masked", "v_turned", "r_ready", "r_copied", "out1_ready", "out1_used"))

                def banks3(q):
                    return bank[:, 3 * q:3 * q + 3, :].rearrange("p b (r n) -> p (b r) n", n=256)

                def head_chunks(q):
                    return banks3(q)[:, 0:NC5, 0:CW]

                def by5(a):
                    return a.rearrange("p (c n) -> p c n", c=NC5)

                with nc.Block() as block:
                    @block.tensor
                    def _(pe):
                        pe.wait_ge(s_w1l, 48)
                        for h in range(H):
                            if h >= 2:
                                pe.wait_ge(s_qkc, h - 1)
                            for c in range(NC5):
                                for b in range(KB):
                                    ins = nc.tensor.matmul(banks3(h % 2)[:, c, 0:CW], wqkv1[:, b, h * P:(h + 1) * P],
                                                           xn_c[:, b, c * CW:(c + 1) * CW], start=b == 0, stop=b == KB - 1)
                            ins.then_inc(s_qk, 1)
                        def values_of(m):
                            if m < 2:
                                pe.wait_ge(s_qkc, H - 1 + m)
                            else:
                                pe.wait_ge(s_vcp, 2 * m - 2)
                            for c in range(NC5):
                                for b in range(KB):
                                    ins = nc.tensor.matmul(banks3(m % 2)[:, c, 0:CW], wqkv1[:, b, 2 * D + m * P:2 * D + (m + 1) * P],
                                                           xn_c[:, b, c * CW:(c + 1) * CW], start=b == 0, stop=b == KB - 1)
                            ins.then_inc(s_v, 1)

                        def token_sums(c, at):
                            a, w = CHUNKS[c]
                            for h in range(H):
                                ins = nc.tensor.matmul(bank[0:H2, at, 0:w], sw2[:, h * H2:(h + 1) * H2], qk[:, h, a:a + w],
                                                       start=h == 0, stop=h == H - 1)
                            ins.then_inc(s_rows, 1)

                        def spread_rows(h):
                            for c, (a, w) in enumerate(CHUNKS):
                                r = w // CW
                                for k, part in enumerate((row_hi, row_lo)):
                                    ins = nc.tensor.matmul(banks3(h % 2)[:, 2 * c:2 * c + r, 0:CW], select[:, h], part[:, a:a + w],
                                                           start=k == 0, stop=k == 1)
                            return ins
                        values_of(0)
                        pe.wait_ge(s_qkc, H)
                        pe.wait_ge(s_swap, 1)
                        nc.tensor.matmul(bank[:, 6, 0:H], swap[:], sums[:], start=True, stop=True).then_inc(s_sw, 1)
                        values_of(1)
                        values_of(2)
                        pe.wait_ge(s_lh, 1)
                        token_sums(0, 6)
                        token_sums(1, 7)
                        values_of(3)
                        pe.wait_ge(s_inv, 1)
                        token_sums(2, 6)
                        pe.wait_ge(s_lo, NC)
                        for h in range(H):
                            if h < 2:
                                pe.wait_ge(s_vcp, 2 * KB - 2 + 2 * h)
                            else:
                                pe.wait_ge(s_ioc, h - 1)
                            spread_rows(h).then_inc(s_io, 1)
                        pe.wait_ge(s_swr, 1)
                        nc.tensor.matmul(bank[:, 6, 0:H], swap[:], sums2[:], start=True, stop=True).then_inc(s_sw, 1)
                        pe.wait_ge(s_lh, 2)
                        pe.wait_ge(s_ioc, H)
                        for c in range(NC):
                            token_sums(c, c)
                        pe.wait_ge(s_lo, 2 * NC)
                        for h in range(H):
                            if h >= 2:
                                pe.wait_ge(s_kt, h - 1)
                            spread_rows(h).then_inc(s_hat, 1)

                    @block.scalar
                    def _(act):
                        for h in range(H):
                            act.wait_ge(s_qk, h + 1)
                            nc.scalar.activation(by5(qk[:, h, 0:N]), head_chunks(h % 2), ACT.Sigmoid, bias=bias_c[:, h:h + 1],
                                                 accum_out=sums[:, h:h + 1]).then_inc(s_qkc, 1)
                        for c, (a, w) in enumerate(CHUNKS):
                            act.wait_ge(s_inv, c + 1)
                            nc.scalar.copy(row_hi[:, a:a + w], inv[:, a:a + w]).then_inc(s_hi, 1)
                        for c, (a, w) in enumerate(CHUNKS):
                            act.wait_ge(s_mx, c + 1)
                            nc.scalar.activation(sig_hat[:, a:a + w], bank[0:H2, c, 0:w], ACT.Sigmoid).then_inc(s_sig, 1)
                        act.wait_ge(s_mx, NC + 1)
                        for c, (a, w) in enumerate(CHUNKS):
                            nc.scalar.activation(ex_hat[:, a:a + w], bank[0:H2, c, 0:w], ACT.Exp, bias=nmax[:],
                                                 accum_out=sm3[:, c:c + 1]).then_inc(s_ex, 1)
                        for c, (a, w) in enumerate(CHUNKS):
                            act.wait_ge(s_fac, c + 1)
                            nc.scalar.copy(row_hi[:, a:a + w], sig_hat[:, a:a + w]).then_inc(s_hi, 1)

                    @block.vector
                    def _(dve):
                        chain = Chain(dve, dve_n)
                        V = nc.vector
                        chain(V.memset(sw2[:], 0.0))
                        V.tensor_copy(swap[:, 0:HD], ident[:, HD:P])
                        V.tensor_copy(swap[:, HD:P], ident[:, 0:HD]).then_inc(s_swap, 1)

                        def v_bias(m):
                            dve.wait_ge(s_v, m + 1)
                            for c in range(2):
                                rows = slice(c * HD, (c + 1) * HD)
                                V.tensor_scalar(kv[HD:P, :, 2 * m + c].rearrange("p (c g) s -> p c g s", c=NC5),
                                                head_chunks(m % 2)[rows].rearrange("p c (g s) -> p c g s", s=GROUP),
                                                bias_c[rows, H + m:H + m + 1], None, ALU.add).then_inc(s_vcp, 1)

                        def place_sums(n):
                            dve.wait_ge(s_sw, n)
                            chain(V.tensor_copy(sw[:], bank[:, 6, 0:H]))
                            V.tensor_tensor(sw2[:].rearrange("p (h k) -> p h k", k=H2 + 2)[:, :, 0:2],
                                            sw[:].unsqueeze(2).to_broadcast([P, H, 2]),
                                            headmask[:, 0:P:HD].unsqueeze(1).to_broadcast([P, H, 2]), ALU.mult).then_inc(s_lh, 1)

                        def inverse(c, at):
                            a, w = CHUNKS[c]
                            dve.wait_ge(s_rows, c + 1)
                            V.reciprocal(inv[:, a:a + w], bank[0:H2, at, 0:w]).then_inc(s_inv, 1)

                        def low(c):
                            a, w = CHUNKS[c]
                            dve.wait_ge(s_hi, c + 1)
                            V.tensor_tensor(row_lo[:, a:a + w], inv[:, a:a + w], row_hi[:, a:a + w].bitcast(F32),
                                            ALU.subtract).then_inc(s_lo, 1)
                        v_bias(0)
                        place_sums(1)
                        v_bias(1)
                        v_bias(2)
                        inverse(0, 6)
                        inverse(1, 7)
                        low(0)
                        low(1)
                        v_bias(3)
                        inverse(2, 6)
                        low(2)
                        for h in range(H):
                            dve.wait_ge(s_io, h + 1)
                            V.tensor_tensor_reduce(by5(qi_h[:, h, 0:N]), by5(qk[:, h, 0:N]), head_chunks(h % 2), 1.0, 0.0,
                                                   ALU.mult, ALU.add, sums2[:, h:h + 1]).then_inc(s_ioc, 1)
                        dve.wait_ge(s_ioc, H)
                        dve.engine_nop().then_inc(s_swr, 1)
                        place_sums(2)
                        for c, (a, w) in enumerate(CHUNKS):
                            dve.wait_ge(s_rows, NC + c + 1)
                            V.tensor_reduce(mx3[:, c:c + 1], bank[0:H2, c, 0:w], AX.X, ALU.max).then_inc(s_mx, 1)
                        dve.wait_ge(s_mx, NC)
                        chain(V.tensor_reduce(nmax[:], mx3[:], AX.X, ALU.max))
                        V.tensor_scalar(nmax[:], nmax[:], -1.0, None, ALU.mult).then_inc(s_mx, 1)
                        even, odd = smallc[0:H2, 160:161], smallc[0:H2, 161:162]
                        for c, (a, w) in enumerate(CHUNKS):
                            dve.wait_ge(s_sig, c + 1)
                            chain(V.tensor_scalar(sig_hat[:, a:a + w], sig_hat[:, a:a + w], even, None, ALU.mult))
                        dve.wait_ge(s_ex, NC)
                        chain(V.tensor_reduce(norm[:], sm3[:], AX.X, ALU.add))
                        chain(V.reciprocal(norm[:], norm[:]))
                        chain(V.tensor_tensor(norm[:], norm[:], odd, ALU.mult))
                        for c, (a, w) in enumerate(CHUNKS):
                            V.scalar_tensor_tensor(sig_hat[:, a:a + w], ex_hat[:, a:a + w], norm[:], sig_hat[:, a:a + w],
                                                   ALU.mult, ALU.add).then_inc(s_fac, 1)
                        for c, (a, w) in enumerate(CHUNKS):
                            dve.wait_ge(s_hi, NC + c + 1)
                            V.tensor_tensor(row_lo[:, a:a + w], sig_hat[:, a:a + w], row_hi[:, a:a + w].bitcast(F32),
                                            ALU.subtract).then_inc(s_lo, 1)
                        for h in range(H):
                            dve.wait_ge(s_hat, h + 1)
                            V.tensor_tensor(by5(qi_h[0:HD, h, 0:N]), by5(qi_h[0:HD, h, 0:N]), head_chunks(h % 2)[0:HD], ALU.mult)
                            V.tensor_tensor(kv[0:HD, :, h].rearrange("p (c g) s -> p c g s", c=NC5),
                                            head_chunks(h % 2)[HD:P].rearrange("p c (g s) -> p c g s", s=GROUP),
                                            qk[HD:P, h].rearrange("p (c g s) -> p c g s", c=NC5, s=GROUP), ALU.mult).then_inc(s_kt, 1)
                        dve.wait_ge(s_kt, H)

                with nc.Block() as block:
                    NB = GROUPS // BATCH
                    norm_rows = adj[0:TP, 0:HALF * D].rearrange("p (t d) -> p t d", t=HALF)

                    def score_bank(q):
                        return bank[0:GW, q, 0:BATCH * GW].rearrange("p (j n) -> p j n", n=GW)

                    @block.tensor
                    def _(pe):
                        def scores(n):
                            if n >= 2:
                                pe.wait_ge(s_pmc, n - 1)
                                pe.wait_ge(s_vgc, n - 1)
                            for j in range(BATCH):
                                g = n * BATCH + j
                                tok = slice(g * GROUP, (g + 1) * GROUP)
                                nc.tensor.matmul(bank[0:GW, n % 2, j * GW:(j + 1) * GW],
                                                 kv[0:HD, g].rearrange("p h s -> p (h s)"), qi_h[0:HD, :, tok],
                                                 start=True, stop=True)
                                ins = nc.tensor.transpose(bank[0:GW, 2 + n % 2, j * HD:(j + 1) * HD],
                                                          kv[HD:P, g].rearrange("p h s -> p (h s)"), ident[HD:P, HD:P])
                            ins.then_inc(s_pm, 1)

                        def values(n):
                            pe.wait_ge(s_pmc, n + 1)
                            pe.wait_ge(s_vgc, n + 1)
                            if n >= 2:
                                pe.wait_ge(s_rc, n - 1)
                            for j in range(BATCH):
                                ins = nc.tensor.matmul(bank[0:HD, 4 + n % 2, j * GW:(j + 1) * GW],
                                                       vg_sb[0:GW, n % 2, j * HD:(j + 1) * HD],
                                                       pm_sb[0:GW, n % 2, j * GW:(j + 1) * GW], start=True, stop=True)
                            ins.then_inc(s_r, 1)
                        for n in range(NB):
                            scores(n)
                            if n >= 1:
                                values(n - 1)
                        values(NB - 1)
                        pe.wait_ge(s_rc, NB)

                        def out_product(i):
                            if i >= 2:
                                pe.wait_ge(s_oc, i - 1)
                            for b in range(KB):
                                ins = nc.tensor.matmul(bank[0:TP, 6 + i % 2, :], r_c[:, b, i * TP:(i + 1) * TP], w_out[:, b],
                                                       start=b == 0, stop=b == KB - 1)
                            ins.then_inc(s_o, 1)
                        for i in range(HALF + 2):
                            out_product(i)
                        turned = 0
                        for i in range(HALF + 2, NT):
                            for _ in range(2):
                                if turned < HALF:
                                    norm_turn(pe, 3, turned, norm_rows)
                                    turned += 1
                            out_product(i)
                        for i in range(turned, NT):
                            norm_turn(pe, 3, i, norm_rows)

                    def r_in(n, par):
                        return bank[0:HD, 4 + n % 2, 0:BATCH * GW].rearrange("p (j b c s) -> p c b j s", j=BATCH, b=KB, c=2)[:, par]

                    def r_out(n, par):
                        cols = r_c[par * HD:(par + 1) * HD, :, n * BATCH * GROUP:(n + 1) * BATCH * GROUP]
                        return cols.rearrange("p b (j s) -> p b j s", j=BATCH)

                    @block.vector
                    def _(dve):
                        mask4 = tokmask[0:GW, 0:GW].unsqueeze(1).to_broadcast([GW, BATCH, GW])
                        for n in range(NB):
                            dve.wait_ge(s_pm, n + 1)
                            if n >= 2:
                                dve.wait_ge(s_r, n - 1)
                            nc.vector.tensor_tensor(pm_sb[0:GW, n % 2].rearrange("p (j n) -> p j n", n=GW), score_bank(n % 2), mask4,
                                                    ALU.mult).then_inc(s_pmc, 1)
                            nc.vector.tensor_copy(vg_sb[0:GW, n % 2], bank[0:GW, 2 + n % 2, 0:BATCH * HD]).then_inc(s_vgc, 1)
                        chain = Chain(dve, dve_n)
                        for c in range(2):
                            for i in range(c * HALF, (c + 1) * HALF):
                                dve.wait_ge(s_o, i + 1)
                                nc.vector.tensor_tensor(x_res[:, i], x_res[:, i], bank[0:TP, 6 + i % 2, :], ALU.add).then_inc(s_oc, 1)
                                dve.wait_ge(s_oc, i + 1)
                                ins = norm_stats(dve, 3, i)
                            chain(ins)
                            norm_variance(c)
                            norm_apply(dve, chain, 3, c, norm_rows)

                    @block.scalar
                    def _(act):
                        for n in range(NB):
                            act.wait_ge(s_r, n + 1)
                            nc.scalar.copy(r_out(n, 0), r_in(n, 0))
                            nc.scalar.copy(r_out(n, 1), r_in(n, 1)).then_inc(s_rc, 1)
                        for c in range(2):
                            norm_root(act, 3, c)
                            for i in range(c * HALF, (c + 1) * HALF):
                                norm_columns(act, 3, i, norm_rows, xn_c)

            with ExitStack() as scope:
                wg = sb("wg", [P, KB, E1], scope=scope)
                bg = sb("bg", [TP, E1], scope=scope)
                mean_c = sb("mean_c", [P, KB], scope=scope)
                mean_rep = sb("mean_rep", [P, KB, TP], scope=scope)
                lg, eg, kg = (sb(n, [TP, E1], scope=scope) for n in ("lg", "eg", "kg"))
                sc = sb("sc", [TP, 8], scope=scope)
                pick_i = sb("pick_i", [1, 1], I32, scope=scope)
                w_e = sb("w_e", [P, KB, D], scope=scope)
                b_e = sb("b_e", [TP, D], scope=scope)
                xh_c, xl_c = (place_adj(n, [P, KB, N], i * 20 * 1024, F32R) for i, n in enumerate(("xh_c", "xl_c")))
                we_hi, we_lo = (sb(n, [P, KB, D], F32R, scope=scope) for n in ("we_hi", "we_lo"))
                token_halves = [slice(c * HALF * TP, (c + 1) * HALF * TP) for c in range(2)]
                s_xh, s_xlo, s_weh, s_wel = (sem(n) for n in ("x_high", "x_low", "picked_high", "picked_low"))
                ytmp = sb("ytmp", [TP, 2, D], scope=scope)
                s_g1, s_mean, s_l1, s_e1, s_pick, s_we, s_y, s_yc, s_st = (sem(n) for n in (
                    "gate1_weights", "mean_ready", "logits1_ready", "exp1_ready", "pick_ready", "picked_loaded", "y1_ready", "x_done", "x_stored"))
                with nc.Block() as block:
                    @block.sync
                    def _(sp):
                        sp.dma_start(wg[:], blocks(t["L1_ffn_Wg"])).then_inc(s_g1, 16)
                        sp.dma_start(bg[:], t["L1_ffn_bg"].partition_broadcast(TP)).then_inc(s_g1, 16)

                with nc.Block() as block:
                    @block.sync
                    def _(sp):
                        sp.wait_ge(s_pick, 1)
                        e = sp.value_load(pick_i[0:1, 0:1], min_val=0, max_val=E1 - 1)
                        sp.dma_start(w_e[:], t["L1_ffn_We"][bass.ds(e, 1)].rearrange("a (b p) n -> p (a b) n", p=P)).then_inc(s_we, 16)
                        sp.dma_start(b_e[:], t["L1_ffn_be"][bass.ds(e, 1)].rearrange("a n -> (a n)").partition_broadcast(TP)).then_inc(s_we, 16)
                        for i in range(NT):
                            sp.wait_ge(s_yc, i + 1)
                            sp.dma_start(t["out"][i * TP:(i + 1) * TP, :], x_res[:, i]).then_inc(s_st, 16)
                        sp.wait_ge(s_st, 16 * NT)

                    @block.tensor
                    def _(pe):
                        pe.wait_ge(s_mean, 1)
                        pe.wait_ge(s_g1, 32)
                        for b in range(KB):
                            ins = nc.tensor.matmul(bank[0:TP, 0, 0:E1], mean_rep[:, b], wg[:, b], start=b == 0, stop=b == KB - 1)
                        ins.then_inc(s_l1, 1)
                        for i in range(NT):
                            if i >= 2:
                                pe.wait_ge(s_yc, i - 1)
                            pe.wait_ge(s_xlo, i // HALF + 1)
                            for b in range(KB):
                                pe.wait_ge(s_wel, b + 1)
                                for k, (left, right) in enumerate(((xh_c, we_hi), (xl_c, we_hi), (xh_c, we_lo))):
                                    ins = nc.tensor.matmul(bank[0:TP, 1 + i % 2, :], left[:, b, i * TP:(i + 1) * TP], right[:, b],
                                                           start=b == 0 and k == 0, stop=b == KB - 1 and k == 2)
                            ins.then_inc(s_y, 1)

                    @block.scalar
                    def _(act):
                        for tok in token_halves:
                            nc.scalar.copy(xh_c[:, :, tok], xn_c[:, :, tok]).then_inc(s_xh, 1)
                        act.wait_ge(s_e1, 1)
                        nc.scalar.activation(eg[:], lg[:], ACT.Exp, bias=sc[:, 0:1], accum_out=sc[:, 1:2]).then_inc(s_e1, 1)
                        act.wait_ge(s_we, 32)
                        for b in range(KB):
                            nc.scalar.copy(we_hi[:, b], w_e[:, b]).then_inc(s_weh, 1)

                    @block.vector
                    def _(dve):
                        chain = Chain(dve, dve_n)
                        V = nc.vector
                        chain(V.tensor_reduce(mean_c[:], xn_c[:], AX.X, ALU.add))
                        chain(V.tensor_scalar(mean_c[:], mean_c[:], 1.0 / N, None, ALU.mult))
                        for b in range(KB):
                            ins = V.tensor_scalar(mean_rep[:, b], ones[:, 0:TP], mean_c[:, b:b + 1], None, ALU.mult)
                        ins.then_inc(s_mean, 1)
                        dve.wait_ge(s_l1, 1)
                        dve.wait_ge(s_g1, 32)
                        chain(V.tensor_tensor(lg[:], bank[0:TP, 0, 0:E1], bg[:], ALU.add))
                        chain(V.tensor_reduce(sc[:, 2:3], lg[:], AX.X, ALU.max))
                        V.tensor_scalar(sc[:, 0:1], sc[:, 2:3], -1.0, None, ALU.mult).then_inc(s_e1, 1)
                        dve.wait_ge(s_e1, 2)
                        chain(V.reciprocal(sc[:, 3:4], sc[:, 1:2]))
                        chain(V.tensor_reduce(sc[:, 4:5], eg[:], AX.X, ALU.max))
                        chain(V.tensor_tensor(sc[:, 5:6], sc[:, 4:5], sc[:, 3:4], ALU.mult))
                        chain(V.tensor_scalar(kg[:], eg[:], sc[:, 4:5], -float(E1), ALU.is_equal, ALU.mult))
                        chain(V.tensor_tensor(kg[:], kg[:], smallc[0:TP, 128:128 + E1], ALU.add))
                        chain(V.tensor_reduce(sc[:, 6:7], kg[:], AX.X, ALU.min))
                        chain(V.tensor_scalar(sc[:, 6:7], sc[:, 6:7], float(E1), None, ALU.add))
                        V.tensor_copy(pick_i[:], sc[0:1, 6:7]).then_inc(s_pick, 1)
                        for c, tok in enumerate(token_halves):
                            dve.wait_ge(s_xh, c + 1)
                            V.tensor_tensor(xl_c[:, :, tok], xn_c[:, :, tok], xh_c[:, :, tok].bitcast(F32), ALU.subtract).then_inc(s_xlo, 1)
                        dve.wait_ge(s_we, 32)
                        for b in range(KB):
                            dve.wait_ge(s_weh, b + 1)
                            V.tensor_tensor(we_lo[:, b], w_e[:, b], we_hi[:, b].bitcast(F32), ALU.subtract).then_inc(s_wel, 1)
                        for i in range(NT):
                            dve.wait_ge(s_y, i + 1)
                            y = ytmp[:, i % 2]
                            chain(V.tensor_tensor(y, bank[0:TP, 1 + i % 2, :], b_e[:], ALU.add))
                            V.scalar_tensor_tensor(x_res[:, i], y, sc[:, 5:6], x_res[:, i], ALU.mult, ALU.add).then_inc(s_yc, 1)


def host_constants():
    i = np.arange(P)
    small = np.zeros((P, 256), np.float32)
    small[:NT, 0] = np.arange(NT) * TP
    small[:NT, 1] = np.arange(NT) * TP + TP - 1
    small[:, 8:8 + STEPS] = np.arange(STEPS)
    small[:, 128:144] = np.arange(16)
    small[:, 160] = i % 2 == 0
    small[:, 161] = i % 2 == 1
    small[:, 144:144 + NT] = np.arange(NT) * SLOT
    return {
        "c_ident": np.eye(P, dtype=np.float32),
        "c_before": (i[:, None] < i[None, :]).astype(np.float32),
        "c_ones": np.ones((P, P), np.float32),
        "c_headmask": (i[:, None] // HD == i[None, :] // HD).astype(np.float32),
        "c_tokmask": (i[:, None] % GROUP == i[None, :] % GROUP).astype(np.float32),
        "c_iota": np.broadcast_to(np.arange(N), (P, N)).astype(np.float16),
        "c_small": small,
        "c_select": (np.arange(2 * H)[:, None] == 2 * (np.arange(H * P) // P) + np.arange(H * P) % P // HD).astype(np.float32),
    }


def kernel(**inputs):
    import concourse.bacc as bacc
    from concourse.bass_utils import run_bass_kernel_spmd

    a = {k: np.asarray(v) for k, v in inputs.items()}
    for name in ("L0_gnn_W_l", "L0_gnn_W_r", "L1_mix_W_out", "L1_mix_W_qkv"):
        a[name] = a[name].T
    order = np.arange(3 * D).reshape(H, 3, HD)
    order = np.concatenate([order[:, 0:2].reshape(-1), order[:, 2].reshape(-1)])
    a["L1_mix_W_qkv"] = a["L1_mix_W_qkv"][:, order]
    a["L1_mix_b_qkv"] = a["L1_mix_b_qkv"][order].reshape(-1, P).T
    a["L1_gnn_t_emb"] = a["L1_gnn_t_emb"].reshape(-1, P).T
    a["L0_ffn_b1"] = a["L0_ffn_b1"].reshape(E0, FB, P).transpose(0, 2, 1)
    a.update(host_constants())
    nc = bacc.Bacc("TRN2", target_bir_lowering=False, num_devices=1)
    arrays, t = {}, {}
    for name, v in a.items():
        v = np.ascontiguousarray(v)
        arrays["in_" + name] = v
        t[name] = nc.dram_tensor("in_" + name, v.shape, mybir.dt.from_np(v.dtype), kind="ExternalInput").ap()
    t["out"] = nc.dram_tensor("out_x", (N, D), F32, kind="ExternalOutput").ap()
    build(nc, t)
    r = run_bass_kernel_spmd(nc, [arrays], core_ids=[0])
    return r.results[0]["out_x"]
```
